# Optimizing a Trainium2 kernel written in Bass

```python
import numpy as np
import jax
import jax.numpy as jnp

def _softmax(x, axis=-1):
    return jax.nn.softmax(x, axis=axis)

def _gelu(x):
    return jax.nn.gelu(x, approximate=True)

def _silu(x):
    return jax.nn.silu(x)

def _sigmoid(x):
    return jax.nn.sigmoid(x)

def _layernorm(x, axis=-1, eps=1e-05):
    m = jnp.mean(x, axis=axis, keepdims=True)
    v = jnp.var(x, axis=axis, keepdims=True)
    return (x - m) / jnp.sqrt(v + eps)

def _scatter_add(tgt, idx, src, axis=0):
    return tgt.at[idx].add(src)

def _segment_sum(src, seg, n):
    return jax.ops.segment_sum(src, seg, n)
kernel_name = 'mk_perceiver_d1_seqx_r2_348fa1'

def setup_inputs(seed: int=0):
    np.random.seed(seed)
    _w = jnp.asarray

    def _rec_inputs():
        import jax
        import jax.numpy as jnp
        _rk = jax.random.key(seed)
        x = -0.0003929 + 0.9999 * jax.random.normal(jax.random.fold_in(_rk, 1), (32, 32, 512), jnp.float32)
        _lenS = 32 - jax.random.randint(jax.random.fold_in(_rk, 7), (32,), 0, max(1, 32 // 4) + 1, jnp.int32)
        _lenS2 = 257 - jax.random.randint(jax.random.fold_in(_rk, 8), (32,), 0, max(1, 257 // 4) + 1, jnp.int32)
        _ctx_768P = jax.random.normal(jax.random.fold_in(_rk, 11), (32, 16, 384), jnp.float32)
        _ctx_768c = jax.random.dirichlet(jax.random.fold_in(_rk, 511), 0.3 * jnp.ones((16,), jnp.float32), (32, 257))
        _ctx_768t = jnp.einsum('bsk,bkd->bsd', _ctx_768c, _ctx_768P)
        _ctx_768t = _ctx_768t * jax.lax.rsqrt(jnp.mean(jnp.square(_ctx_768t)) + 1e-12) * 0.953939
        ctx_768 = -7.36909e-05 + 0.999899 * (_ctx_768t + 0.3 * jax.random.normal(jax.random.fold_in(_rk, 611), (32, 257, 384), jnp.float32))
        return (x, ctx_768)
    x, ctx_768 = _rec_inputs()

    def _L0_xattn_setup():
        import jax, jax.numpy as jnp
        import numpy as np
        EPS = 1e-05

        def layernorm(x, g, b):
            mu = jnp.mean(x, axis=-1, keepdims=True)
            var = jnp.mean(jnp.square(x - mu), axis=-1, keepdims=True)
            return (x - mu) * jax.lax.rsqrt(var + EPS) * g + b
        key = jax.random.key(seed)
        ks = jax.random.split(key, 12)
        B, L1, L2 = (8, 1024, 1024)
        D1, D2, E = (512, 384, 512)
        s1, s2, se = (D1 ** (-0.5), D2 ** (-0.5), E ** (-0.5))
        return {'modality1': jax.random.normal(ks[0], (B, L1, D1), jnp.float32), 'modality2': jax.random.normal(ks[1], (B, L2, D2), jnp.float32), 'ln1_g': jnp.ones((D1,), jnp.float32), 'ln1_b': jnp.zeros((D1,), jnp.float32), 'ln2_g': jnp.ones((D2,), jnp.float32), 'ln2_b': jnp.zeros((D2,), jnp.float32), 'Wq': jax.random.normal(ks[2], (D1, E), jnp.float32) * s1, 'bq': jax.random.normal(ks[3], (E,), jnp.float32) * 0.01, 'Wk': jax.random.normal(ks[4], (D2, E), jnp.float32) * s2, 'bk': jax.random.normal(ks[5], (E,), jnp.float32) * 0.01, 'Wv': jax.random.normal(ks[6], (D2, E), jnp.float32) * s2, 'bv': jax.random.normal(ks[7], (E,), jnp.float32) * 0.01, 'Wo': jax.random.normal(ks[8], (E, D1), jnp.float32) * se, 'bo': jax.random.normal(ks[9], (D1,), jnp.float32) * 0.01}
    _L0_xattn_all = _L0_xattn_setup()
    _L0_xattn_in = {k: v for k, v in _L0_xattn_all.items() if k in ('ln1_g', 'ln1_b', 'ln2_g', 'ln2_b', 'Wq', 'bq', 'Wk', 'bk', 'Wv', 'bv', 'Wo', 'bo')}
    del _L0_xattn_all

    def _L0_attn_setup():
        import jax, jax.numpy as jnp
        import numpy as np
        EMBED_DIM = 512
        NUM_HEADS = 16
        HEAD_DIM = EMBED_DIM // NUM_HEADS

        def apply_rope(x):
            B, T, H, D = x.shape
            half = D // 2
            theta = 10000.0 ** (-jnp.arange(half, dtype=x.dtype) / half)
            freqs = jnp.arange(T, dtype=x.dtype)[:, None] * theta[None, :]
            cos = freqs.reshape(1, T, 1, half)
            sin = jnp.sin(freqs).reshape(1, T, 1, half)
            cos = jnp.cos(freqs).reshape(1, T, 1, half)
            x1, x2 = (x[..., :half], x[..., half:])
            return jnp.concatenate([x1 * cos - x2 * sin, x1 * sin + x2 * cos], axis=-1)
        key = jax.random.key(seed)
        ks = jax.random.split(key, 9)
        s = 1.0 / np.sqrt(EMBED_DIM)
        inp = {'x': jax.random.normal(ks[0], (4, 1024, EMBED_DIM), dtype=jnp.float32), 'Wq': jax.random.uniform(ks[1], (EMBED_DIM, EMBED_DIM), jnp.float32, -s, s), 'bq': jnp.zeros((EMBED_DIM,), jnp.float32), 'Wk': jax.random.uniform(ks[2], (EMBED_DIM, EMBED_DIM), jnp.float32, -s, s), 'bk': jnp.zeros((EMBED_DIM,), jnp.float32), 'Wv': jax.random.uniform(ks[3], (EMBED_DIM, EMBED_DIM), jnp.float32, -s, s), 'bv': jnp.zeros((EMBED_DIM,), jnp.float32), 'Wo': jax.random.uniform(ks[4], (EMBED_DIM, EMBED_DIM), jnp.float32, -s, s), 'bo': jnp.zeros((EMBED_DIM,), jnp.float32)}
        return inp
    _L0_attn_all = _L0_attn_setup()
    _L0_attn_in = {k: v for k, v in _L0_attn_all.items() if k in ('Wq', 'bq', 'Wk', 'bk', 'Wv', 'bv', 'Wo', 'bo')}
    del _L0_attn_all

    def _L0_ffn_setup():
        import jax, jax.numpy as jnp
        import numpy as np
        DIM = 512
        NUM_EXPERTS = 8
        ACTIVE_EXPERTS = 2
        EXPERT_DIM = 1024
        key = jax.random.key(seed)
        k1, k2, k3, k4 = jax.random.split(key, 4)
        x = jax.random.normal(k1, (1, 1024, DIM), dtype=jnp.float32)
        gate_w = jax.random.normal(k2, (NUM_EXPERTS, DIM), dtype=jnp.float32) * 0.02
        balance_bias = jnp.zeros((NUM_EXPERTS,), dtype=jnp.float32)
        w1 = jax.random.normal(k3, (NUM_EXPERTS, EXPERT_DIM, DIM), dtype=jnp.float32) * 0.02
        w2 = jax.random.normal(k4, (NUM_EXPERTS, DIM, EXPERT_DIM), dtype=jnp.float32) * 0.02
        return {'x': x, 'gate_w': gate_w, 'balance_bias': balance_bias, 'w1': w1, 'w2': w2}
    _L0_ffn_all = _L0_ffn_setup()
    _L0_ffn_in = {k: v for k, v in _L0_ffn_all.items() if k in ('gate_w', 'balance_bias', 'w1', 'w2')}
    del _L0_ffn_all
    return {'x': x, 'ctx_768': ctx_768, 'L0_xattn_ln1_g': _L0_xattn_in['ln1_g'], 'L0_xattn_ln1_b': _L0_xattn_in['ln1_b'], 'L0_xattn_ln2_g': _L0_xattn_in['ln2_g'], 'L0_xattn_ln2_b': _L0_xattn_in['ln2_b'], 'L0_xattn_Wq': _L0_xattn_in['Wq'], 'L0_xattn_bq': _L0_xattn_in['bq'], 'L0_xattn_Wk': _L0_xattn_in['Wk'], 'L0_xattn_bk': _L0_xattn_in['bk'], 'L0_xattn_Wv': _L0_xattn_in['Wv'], 'L0_xattn_bv': _L0_xattn_in['bv'], 'L0_xattn_Wo': _L0_xattn_in['Wo'], 'L0_xattn_bo': _L0_xattn_in['bo'], 'L0_attn_Wq': _L0_attn_in['Wq'], 'L0_attn_bq': _L0_attn_in['bq'], 'L0_attn_Wk': _L0_attn_in['Wk'], 'L0_attn_bk': _L0_attn_in['bk'], 'L0_attn_Wv': _L0_attn_in['Wv'], 'L0_attn_bv': _L0_attn_in['bv'], 'L0_attn_Wo': _L0_attn_in['Wo'], 'L0_attn_bo': _L0_attn_in['bo'], 'L0_ffn_gate_w': _L0_ffn_in['gate_w'], 'L0_ffn_balance_bias': _L0_ffn_in['balance_bias'], 'L0_ffn_w1': _L0_ffn_in['w1'], 'L0_ffn_w2': _L0_ffn_in['w2']}

def reference(x, ctx_768, L0_xattn_ln1_g, L0_xattn_ln1_b, L0_xattn_ln2_g, L0_xattn_ln2_b, L0_xattn_Wq, L0_xattn_bq, L0_xattn_Wk, L0_xattn_bk, L0_xattn_Wv, L0_xattn_bv, L0_xattn_Wo, L0_xattn_bo, L0_attn_Wq, L0_attn_bq, L0_attn_Wk, L0_attn_bk, L0_attn_Wv, L0_attn_bv, L0_attn_Wo, L0_attn_bo, L0_ffn_gate_w, L0_ffn_balance_bias, L0_ffn_w1, L0_ffn_w2):
    import jax
    import jax.numpy as jnp

    def _L0_xattn_ref(modality1, modality2, ln1_g, ln1_b, ln2_g, ln2_b, Wq, bq, Wk, bk, Wv, bv, Wo, bo):
        import jax, jax.numpy as jnp
        import numpy as np
        EPS = 1e-05

        def layernorm(x, g, b):
            mu = jnp.mean(x, axis=-1, keepdims=True)
            var = jnp.mean(jnp.square(x - mu), axis=-1, keepdims=True)
            return (x - mu) * jax.lax.rsqrt(var + EPS) * g + b
        E = Wq.shape[1]
        scaling = E ** (-0.5)
        x1 = layernorm(modality1, ln1_g, ln1_b)
        x2 = layernorm(modality2, ln2_g, ln2_b)
        q = x1 @ Wq + bq
        k = x2 @ Wk + bk
        v = x2 @ Wv + bv
        scores = jnp.einsum('bqe,bke->bqk', q, k) * scaling
        attn = jax.nn.softmax(scores, axis=-1)
        ctx = jnp.einsum('bqk,bke->bqe', attn, v)
        return ctx @ Wo + bo

    def _L0_attn_ref(x, Wq, bq, Wk, bk, Wv, bv, Wo, bo):
        import jax, jax.numpy as jnp
        import numpy as np
        EMBED_DIM = 512
        NUM_HEADS = 16
        HEAD_DIM = EMBED_DIM // NUM_HEADS

        def apply_rope(x):
            B, T, H, D = x.shape
            half = D // 2
            theta = 10000.0 ** (-jnp.arange(half, dtype=x.dtype) / half)
            freqs = jnp.arange(T, dtype=x.dtype)[:, None] * theta[None, :]
            cos = freqs.reshape(1, T, 1, half)
            sin = jnp.sin(freqs).reshape(1, T, 1, half)
            cos = jnp.cos(freqs).reshape(1, T, 1, half)
            x1, x2 = (x[..., :half], x[..., half:])
            return jnp.concatenate([x1 * cos - x2 * sin, x1 * sin + x2 * cos], axis=-1)
        B, T, C = x.shape
        H, D = (NUM_HEADS, HEAD_DIM)
        q = (x @ Wq.T + bq).reshape(B, T, H, D)
        k = (x @ Wk.T + bk).reshape(B, T, H, D)
        v = (x @ Wv.T + bv).reshape(B, T, H, D)
        q = apply_rope(q)
        k = apply_rope(k)
        scores = jnp.einsum('bthd,bshd->bhts', q, k) / np.sqrt(D).astype(x.dtype)
        attn = jax.nn.softmax(scores, axis=-1)
        out = jnp.einsum('bhts,bshd->bthd', attn, v).reshape(B, T, C)
        return out @ Wo.T + bo

    def _L0_ffn_ref(x, gate_w, balance_bias, w1, w2):
        import jax, jax.numpy as jnp
        import numpy as np
        DIM = 512
        NUM_EXPERTS = 8
        ACTIVE_EXPERTS = 2
        EXPERT_DIM = 1024
        B, S, D = x.shape
        T = B * S
        xf = x.reshape(T, D)
        gate_logits = jnp.einsum('td,ed->te', xf, gate_w)
        gate_scores = jax.nn.sigmoid(gate_logits + balance_bias)
        topk_scores, topk_idx = jax.lax.top_k(gate_scores, ACTIVE_EXPERTS)
        topk_scores = topk_scores / (topk_scores.sum(axis=-1, keepdims=True) + 1e-06)
        comb = jnp.zeros((T, NUM_EXPERTS), dtype=x.dtype)
        comb = comb.at[jnp.arange(T)[:, None], topk_idx].add(topk_scores)
        h = jax.nn.silu(jnp.einsum('td,ehd->teh', xf, w1))
        expert_out = jnp.einsum('teh,edh->ted', h, w2)
        out = jnp.einsum('te,ted->td', comb, expert_out)
        return out.reshape(B, S, D)
    x = x + _L0_xattn_ref(_layernorm(x, axis=-1), ctx_768, L0_xattn_ln1_g, L0_xattn_ln1_b, L0_xattn_ln2_g, L0_xattn_ln2_b, L0_xattn_Wq, L0_xattn_bq, L0_xattn_Wk, L0_xattn_bk, L0_xattn_Wv, L0_xattn_bv, L0_xattn_Wo, L0_xattn_bo)
    x = x + _L0_attn_ref(_layernorm(x, axis=-1), L0_attn_Wq, L0_attn_bq, L0_attn_Wk, L0_attn_bk, L0_attn_Wv, L0_attn_bv, L0_attn_Wo, L0_attn_bo)
    x = x + _L0_ffn_ref(_layernorm(x, axis=-1), L0_ffn_gate_w, L0_ffn_balance_bias, L0_ffn_w1, L0_ffn_w2)
    return x

_drawn_inputs = setup_inputs


def setup_inputs(seed=0):
    import zlib

    import numpy as np

    out = dict(_drawn_inputs(seed))
    spreads = {'L0_xattn_ln1_g': (1.0, 0.2),
     'L0_xattn_ln1_b': (0.0, 0.376),
     'L0_xattn_ln2_g': (1.0, 0.2),
     'L0_xattn_ln2_b': (0.0, 0.1),
     'L0_attn_bq': (0.0, 0.8),
     'L0_attn_bk': (0.0, 0.8),
     'L0_attn_bv': (0.0, 0.1),
     'L0_attn_bo': (0.0, 0.1),
     'L0_ffn_balance_bias': (0.0, 0.1)}
    factors = {'L0_xattn_bq': 27.769,
     'L0_xattn_bk': 64.0,
     'L0_xattn_bv': 5.362,
     'L0_xattn_bo': 4.322,
     'L0_attn_Wq': 3.067,
     'L0_attn_Wk': 2.801}
    for name, (base, spread) in spreads.items():
        noise = np.random.default_rng([zlib.crc32(name.encode()), seed]).standard_normal(out[name].shape)
        drawn = base * np.exp(spread * noise) if base else spread * noise
        out[name] = jnp.asarray(drawn.astype(out[name].dtype))
    for name, factor in factors.items():
        out[name] = (out[name] * factor).astype(out[name].dtype)
    return out
```

```python
from contextlib import ExitStack

import numpy as np

import concourse.bass as bass
from concourse import mybir

F32 = mybir.dt.float32
I32 = mybir.dt.int32
U32 = mybir.dt.uint32
ALU = mybir.AluOpType
ACT = mybir.ActivationFunctionType
AX = mybir.AxisListType
ds = bass.ds

P = 128
B, L, D = 32, 32, 512
KEYS, DC = 257, 384
KC, CC = D // P, DC // P
TOK = B * L
TILES = TOK // P
PAIRS = TILES // 2
BT = P // L
HEADS, HD = 16, 32
E, EH = 8, 1024
HC = EH // P
EPS = 1e-5
X_SCALE = float(D) ** -0.5
H_SCALE = float(HD) ** -0.5
SLOT_TILES = (2 * TOK + (E - 1) * (P - 1) + P) // P
ROW = D + 8
C_TOKEN, C_G1, C_E1, C_G2, C_E2 = range(D, D + 5)
W2_AT = KC * EH
EXPERT = KC * EH + HC * D

CONST = {}
_at = 0
for _name, _width in (("ident", P), ("before", P), ("ones", P), ("cos", L), ("sin", L), ("left_mask", 60),
                      ("low", E * E), ("tile_no", 32), ("steps", 8)):
    CONST[_name] = slice(_at, _at + _width)
    _at += _width
CONST_W = _at
COLS = {}
_at = 0
for _name, _width in (("ln1_g", KC), ("ln1_b", KC), ("bq", KC), ("ln2_g", CC), ("ln2_b", CC), ("bk", KC), ("bv", KC),
                      ("sbq", KC), ("sbk", KC)):
    COLS[_name] = slice(_at, _at + _width)
    _at += _width
COLS_W = _at
ROWS = {"bo": slice(0, D), "sbv": slice(D, 2 * D), "sbo": slice(2 * D, 3 * D), "balance": slice(3 * D, 3 * D + E)}
ROWS_W = 3 * D + E

SEMS = """const_in x_in left_in wq_in wkT_in wk_in wv_in wo_in swq_in swk_in swv_in swo_in gate_in
rows_in cols_in ints_in
ctx_in0 ctx_in1 ctx_in2 ctx_in3
ln1_stats ln1_mv ln1_ve ln1_rstd ln1_out ln2_stats ln2_mv ln2_ve ln2_rstd ln2_out
x1T_ps x1T x_plus_bo
left_stats left_mv left_ve left_rstd left_n left_ps left_T
kb_ps kb
cx_stats cx_mv cx_ve cx_rstd cx_n cxT_ps cxT left_cols
q_ps qT qk_ps qkT q_bias sc_ps sc_max sc_u sc_nb sc_exp sc_rinv sc_p sc_pm pT_ps pT cv_ps x2aT av_ps avT y_ps x_new
ptx_zero ln3_stats ln3_mv ln3_ve ln3_rstd ln3_out xnT_ps xnT sq_ps sk_ps sq sk q_swap k_swap q_cos k_cos q_sin k_sin
q_rot k_exp k_zero sv_ps sv ss_ps s_max s_sub s_exp s_sum s_rinv s_norm s_pT ao_ps aoT sy_ps x_post x_plus_sbo
ln4_stats ln4_mv ln4_ve ln4_rstd xf xfT_ps xfT z_ps z out_init
route rt_sel rt_cnt_ps rt_z rt_exp rt_slots rt_map zrow_fill zrow xs_zero rows_set scattered
xg_in0 xg_in1 xgT_ps xgT h_ps h hT_ps0 hT_ps1 hT0 hT1 y2_ps y2 gate_parts gate idx scat added out_spare
land0 land1 expert_ready""".split()


def program(nc, t_in, out):
    with ExitStack() as ctx:
        def sb(name, shape, dt=F32):
            return ctx.enter_context(nc.sbuf_tensor(name, shape, dt))

        s = {n: ctx.enter_context(nc.semaphore(n)) for n in SEMS}
        ctx_in = (s["ctx_in0"], s["ctx_in1"], s["ctx_in2"], s["ctx_in3"])
        bank = [ctx.enter_context(nc.psum_tensor(f"bank{i}", [P, 512], F32)) for i in range(8)]
        xs_dram = nc.dram_tensor("routed_rows", ((SLOT_TILES + 2) * P, ROW), F32).ap()

        consts = sb("consts", [P, CONST_W])
        cols = sb("cols", [P, COLS_W])
        rows = sb("rows", [P, ROWS_W])
        token_no = sb("token_no", [P, TILES + 1], I32)
        gate_w = sb("gate_w", [P, KC, E])
        x = sb("x", [P, TILES * D])
        shared = sb("shared", [P, TILES * ROW])
        wbuf = sb("wbuf", [P, 2 * EXPERT])
        ctx_region = sb("ctx_region", [P, 4 * BT * 2 * DC])
        ctxT_region = sb("ctxT_region", [P, 2 * CC * BT * KEYS])
        small = sb("small", [P, 600])
        ints = sb("ints", [P, 128], I32)
        xn = sb("xn", [P, 2, D])
        actT = sb("actT", [P, KC * 2 * P])
        misc = sb("misc", [P, 3072])

        def const(name):
            return consts[:, CONST[name]]

        def col(name, i):
            return cols[:, COLS[name].start + i:COLS[name].start + i + 1]

        def row(name):
            return rows[:, ROWS[name]]

        ident = const("ident")

        class Carve:

            def __init__(self, region, at, end):
                self.region, self.at, self.end = region, at, end

            def take(self, *shape):
                n = int(np.prod(shape))
                assert self.at + n <= self.end, (self.at, n, self.end)
                part = self.region[:, self.at:self.at + n]
                self.at += n
                if len(shape) == 1:
                    return part
                names = "abcd"[:len(shape)]
                pattern = f"p ({' '.join(names)}) -> p {' '.join(names)}"
                return part.rearrange(pattern, **dict(zip(names, shape)))

        c = Carve(wbuf, 0, EXPERT)
        wq, wkT, wv, wo = c.take(KC, D), c.take(KC, DC), c.take(CC, D), c.take(KC, D)
        c = Carve(wbuf, EXPERT, 2 * EXPERT)
        swq, swk, swv, swo = c.take(KC, D), c.take(KC, D), c.take(KC, D), c.take(KC, D)
        x1T = shared[:, 0:KC * TOK].rearrange("p (k t) -> p k t", k=KC)
        ctx_n = ctx_region[:, :].rearrange("p (s b c d) -> p s b c d", s=4, b=BT, c=2)
        ctxT = ctxT_region[:, :].rearrange("p (t c b k) -> p t c b k", t=2, c=CC, b=BT)
        qT = actT[:, :].rearrange("p (k t) -> p k t", k=KC)
        c = Carve(misc, 0, 3072)
        qkT = c.take(CC, 2 * P)
        probs = c.take(2, 264)
        pT = c.take(2, 2 * P)
        p_left = c.take(2, P)
        left_T = c.take(CC, B)
        left_n = c.take(DC)
        p_mask = c.take(2, B)
        x2aT = ctxT_region[:, 0:CC * 2 * P].rearrange("p (k t) -> p k t", k=CC)
        avT = qT
        wk = ctx_region[:, 3 * BT * 2 * DC:3 * BT * 2 * DC + CC * D].rearrange("p (k e) -> p k e", k=CC)
        c = Carve(small, 0, 600)
        stats = c.take(2, 6)
        mv = c.take(2, 2)
        ve = c.take(2)
        rstd = c.take(2)
        cx_stats = c.take(2, 8, 6)
        cx_mv = c.take(2, 8, 2)
        cx_ve = c.take(2, 8)
        cx_rstd = c.take(2, 8)
        l_stats, l_mv, l_ve, l_rstd = c.take(6), c.take(2), c.take(1), c.take(1)
        kb = c.take(KC)
        q_bias = c.take(2)
        sc_max, sc_u, sc_nb, sc_sum, sc_rinv = c.take(2), c.take(2), c.take(2), c.take(2), c.take(2)
        s_max, s_sum, s_rinv = c.take(2, HEADS), c.take(2, HEADS), c.take(2, HEADS)
        z = c.take(TILES, E)
        neg_half = c.take(8)
        gates = c.take(2, 4)
        c = Carve(ctx_region, 0, 4 * BT * 2 * DC)
        xnT = c.take(KC, 2 * P)
        qb, q_sw, kbuf, k_sw = (c.take(KC * 2 * P) for _ in range(4))
        q_T, k_T = (a.rearrange("p (k t) -> p k t", k=KC) for a in (qb, kbuf))
        k_exp = c.take(KC, 2 * BT, 4, L)
        v = c.take(2, D)
        c = Carve(ctxT_region, 0, 2 * CC * BT * KEYS)
        p_T = c.take(2, HEADS, P)
        soft = c.take(2, D)
        aoT = actT[:, :].rearrange("p (t c q) -> p t c q", t=2, c=KC)
        xf = shared[:, :].rearrange("p (t r) -> p t r", t=TILES)
        c = Carve(ctx_region, 0, 4 * BT * 2 * DC)
        _keep = c.take(KC, 2 * P)
        cmp_a, cmp_b = c.take(TILES, E, E), c.take(TILES, E, E)
        rank, sel, sel1, sel2 = c.take(TILES, E), c.take(TILES, E), c.take(TILES, E), c.take(TILES, E)
        sig, picked, base, slot = c.take(TILES, E), c.take(TILES, E), c.take(TILES + 1, E), c.take(TILES, E)
        g1, g2, gsum = c.take(TILES), c.take(TILES), c.take(TILES)
        slot_f = c.take(2, TILES)
        over, ntile, ends, ends_tmp = c.take(E, 8), c.take(E), c.take(E), c.take(E, E)
        emap, emap_cmp, parity = c.take(32), c.take(32, E), c.take(3, 32)
        xg = c.take(2, ROW)
        xgT = c.take(2, D)
        h = c.take(EH)
        hT = c.take(2, EH)
        y_out = c.take(2, D)
        idx_f = c.take(2)
        zrow = ctxT_region[:, 5600:5600 + ROW]
        slot_i = ints[:, 0:2 * TILES].rearrange("p (a t) -> p a t", a=2)
        map_i = ints[:, 16:16 + 96].rearrange("p (a t) -> p a t", a=3)
        idx = ints[:, 112:114]

        block = ctx.enter_context(nc.Block())


        @block.sync
        def _(sp):
            sp.dma_start(consts[:, :], t_in["consts"]).then_inc(s["const_in"], 16)
            sp.dma_start(x[:, :].rearrange("p (t d) -> p t d", t=TILES),
                         t_in["x"].rearrange("(t p) d -> p t d", p=P)).then_inc(s["x_in"], 16)
            sp.dma_start(cols[:, :], t_in["cols"]).then_inc(s["cols_in"], 16)
            sp.dma_start(left_n[0:B, :], t_in["ctx_768"][:, KEYS - 1, :]).then_inc(s["left_in"], 16)
            sp.dma_start(wk, t_in["wk"].rearrange("(k p) e -> p k e", p=P)).then_inc(s["wk_in"], 16)

            def load_ctx(tile):
                sp.dma_start(
                    ctx_n[:, tile % 4].rearrange("p b c d -> p b (c d)"),
                    t_in["ctx_768"][tile * BT:(tile + 1) * BT, 0:KEYS - 1, :].rearrange("b (p c) d -> p b (c d)", c=2),
                ).then_inc(ctx_in[tile % 4], 16)

            def load_w(w, name, sem):
                sp.dma_start(w, t_in[name].rearrange("(k p) e -> p k e", p=P)).then_inc(sem, 16)

            load_ctx(0)
            load_ctx(1)
            load_w(wq, "wq", s["wq_in"])
            load_w(wkT, "wkT", s["wkT_in"])
            sp.dma_start(rows[:, :], t_in["rows"]).then_inc(s["rows_in"], 16)
            load_ctx(2)
            load_w(wv, "wv", s["wv_in"])
            load_w(wo, "wo", s["wo_in"])
            sp.wait_ge(s["kb_ps"], 1)
            load_ctx(3)
            load_w(gate_w[:, :, :], "gate_wT", s["gate_in"])
            sp.dma_start(token_no[:, :], t_in["token_no"]).then_inc(s["ints_in"], 16)
            for w, name, sem in ((swq, "swqT", s["swq_in"]), (swk, "swkT", s["swk_in"]),
                                 (swv, "swvT", s["swv_in"]), (swo, "swoT", s["swo_in"])):
                load_w(w, name, sem)
            for tile in range(4, TILES):
                sp.wait_ge(s["cv_ps"], tile - 3)
                load_ctx(tile)
            sp.wait_ge(s["y_ps"], TILES)
            sp.dma_start(wbuf[:, 0:EXPERT], t_in["experts"][0]).then_inc(s["land0"], 16)
            sp.wait_ge(s["zrow"], 1)
            sp.dma_start(xs_dram.rearrange("(n p) r -> p n r", p=P),
                         zrow[:, None, :].to_broadcast([P, SLOT_TILES + 2, ROW])).then_inc(s["xs_zero"], 16)
            sp.dma_start(out[TOK:TOK + P, :], zrow[:, 0:D]).then_inc(s["out_spare"], 16)
            sp.wait_ge(s["sy_ps"], TILES)
            sp.dma_start(wbuf[:, EXPERT:2 * EXPERT], t_in["experts"][1]).then_inc(s["land1"], 16)
            land = (s["land0"], s["land1"])
            for e in range(2):
                sp.wait_ge(land[e], 16)
                sp.sem_inc(s["expert_ready"], 1)
            sp.wait_ge(s["rt_map"], 1)
            for e in range(2, E):
                last = sp.value_load(map_i[0:1, 2, e - 2:e - 1], min_val=1, max_val=SLOT_TILES)
                sp.wait_ge(s["y2_ps"], last)
                sp.dma_start(wbuf[:, e % 2 * EXPERT:(e % 2 + 1) * EXPERT], t_in["experts"][e]).then_inc(land[e % 2], 16)
                sp.wait_ge(land[e % 2], 16 * (e // 2 + 1))
                sp.sem_inc(s["expert_ready"], 1)
            sp.wait_ge(s["scat"], 16 * SLOT_TILES)
            sp.wait_ge(s["out_init"], 16 * TILES)

        @block.tensor
        def _(pe):
            pe.wait_ge(s["const_in"], 16)

            def transposes(dst, pieces, sem):
                at = 0
                for piece in pieces:
                    n = piece.shape[0]
                    last = nc.tensor.transpose(dst[0:piece.shape[1], at:at + n], piece, ident[0:n, 0:n])
                    at += n
                last.then_inc(sem, 1)

            for tile in range(TILES):
                t = tile % 2
                pe.wait_ge(s["ln2_out"], tile + 1)
                transposes(bank[2 + t], [xn[:, t, k * P:(k + 1) * P] for k in range(KC)], s["x1T_ps"])
                if tile == 1:
                    pe.wait_ge(s["left_n"], 1)
                    transposes(bank[0], [left_n[0:B, k * P:(k + 1) * P] for k in range(CC)], s["left_ps"])
                    pe.wait_ge(s["wk_in"], 16)
                    pe.wait_ge(s["cols_in"], 16)
                    for e in range(KC):
                        for k in range(CC):
                            mm = nc.tensor.matmul(bank[1][:, e:e + 1], wk[:, k, e * P:(e + 1) * P], col("ln2_b", k),
                                                  start=(k == 0), stop=(k == CC - 1))
                    mm.then_inc(s["kb_ps"], 1)

            def ctx_transposes(tile):
                pe.wait_ge(s["cx_n"], tile + 1)
                for n in range(2 * CC):
                    k, half = n // 2, n % 2
                    use = 2 * CC * tile + n
                    if use >= 2:
                        pe.wait_ge(s["cxT"], use - 1)
                    else:
                        pe.wait_ge(s["left_T"] if use == 0 else s["kb"], 1)
                    transposes(bank[use % 2], [ctx_n[:, tile % 4, 2 * half + b, c2, k * P:(k + 1) * P]
                                               for b in range(2) for c2 in range(2)], s["cxT_ps"])

            for pair in range(PAIRS):
                ctx_transposes(2 * pair)
                pe.wait_ge(s["wq_in"], 16)
                pe.wait_ge(s["x1T"], 2 * pair + 2)
                for e in range(KC):
                    for k in range(KC):
                        mm = nc.tensor.matmul(bank[4 + e // 2][:, e % 2 * 256:e % 2 * 256 + 256], wq[:, k, e * P:(e + 1) * P],
                                              x1T[:, k, pair * 256:pair * 256 + 256], start=(k == 0), stop=(k == KC - 1))
                    if e % 2:
                        mm.then_inc(s["q_ps"], 1)
                ctx_transposes(2 * pair + 1)
                pe.wait_ge(s["wkT_in"], 16)
                pe.wait_ge(s["qT"], 2 * pair + 2)
                pe.wait_ge(s["kb"], 1)
                for d in range(CC):
                    for k in range(KC):
                        mm = nc.tensor.matmul(bank[6 + d // 2][:, d % 2 * 256:d % 2 * 256 + 256], wkT[:, k, d * P:(d + 1) * P],
                                              qT[:, k, :], start=(k == 0), stop=(k == KC - 1))
                    if d == 1:
                        mm.then_inc(s["qk_ps"], 1)
                for t in range(2):
                    for k in range(KC):
                        mm = nc.tensor.matmul(bank[7][:, 256 + t:257 + t], qT[:, k, t * P:(t + 1) * P], kb[:, k:k + 1],
                                              start=(k == 0), stop=(k == KC - 1))
                mm.then_inc(s["qk_ps"], 1)
                for t in range(2):
                    tile = 2 * pair + t
                    pe.wait_ge(s["qkT"], pair + 1)
                    pe.wait_ge(s["cxT"], 2 * CC * (tile + 1))
                    pe.wait_ge(s["left_cols"], tile + 1)
                    for k in range(CC):
                        for b in range(BT):
                            mm = nc.tensor.matmul(bank[2 + t][b * L:(b + 1) * L, 0:KEYS],
                                                  qkT[:, k, t * P + b * L:t * P + (b + 1) * L], ctxT[:, t, k, b, :],
                                                  start=(k == 0), stop=(k == CC - 1), tile_position=(0, b * L),
                                                  skip_group_check=True)
                    mm.then_inc(s["sc_ps"], 1)
                for t in range(2):
                    pe.wait_ge(s["sc_pm"], 2 * pair + t + 1)
                    transposes(bank[4 + t], [probs[:, t, 0:P], probs[:, t, P:2 * P], p_mask[:, t, :]], s["pT_ps"])
                for t in range(2):
                    tile = 2 * pair + t
                    pe.wait_ge(s["pT"], 2 * tile + 2)
                    cv = bank[6 + t]
                    for k in range(CC):
                        nc.tensor.matmul(cv[:, k * P:(k + 1) * P], left_n[0:B, k * P:(k + 1) * P], p_left[0:B, t, :],
                                         start=(k == 0), stop=False, skip_group_check=True)
                    for b in range(BT):
                        for c2 in range(2):
                            for k in range(CC):
                                mm = nc.tensor.matmul(cv[:, k * P + b * L:k * P + (b + 1) * L],
                                                      ctx_n[:, tile % 4, b, c2, k * P:(k + 1) * P],
                                                      pT[:, t, c2 * P + b * L:c2 * P + (b + 1) * L],
                                                      start=False, stop=(c2 == 1), skip_group_check=True)
                    mm.then_inc(s["cv_ps"], 1)
                pe.wait_ge(s["wv_in"], 16)
                pe.wait_ge(s["x2aT"], 2 * pair + 2)
                for e in range(KC):
                    for k in range(CC):
                        mm = nc.tensor.matmul(bank[4 + e // 2][:, e % 2 * 256:e % 2 * 256 + 256], wv[:, k, e * P:(e + 1) * P],
                                              x2aT[:, k, :], start=(k == 0), stop=(k == CC - 1))
                    if e % 2:
                        mm.then_inc(s["av_ps"], 1)
                pe.wait_ge(s["wo_in"], 16)
                pe.wait_ge(s["avT"], 2 * pair + 2)
                for t in range(2):
                    for k in range(KC):
                        mm = nc.tensor.matmul(bank[2 + t][:, :], avT[:, k, t * P:(t + 1) * P], wo[:, k, :],
                                              start=(k == 0), stop=(k == KC - 1))
                    mm.then_inc(s["y_ps"], 1)

            pe.wait_ge(s["swq_in"], 16)
            pe.wait_ge(s["swk_in"], 16)
            pe.wait_ge(s["swv_in"], 16)
            pe.wait_ge(s["swo_in"], 16)
            pe.wait_ge(s["gate_in"], 16)
            pe.wait_ge(s["ptx_zero"], 2)
            for pair in range(PAIRS):
                for t in range(2):
                    pe.wait_ge(s["ln3_out"], 2 * pair + t + 1)
                    if pair == 0:
                        pe.wait_ge(s["x_new"], TILES)
                    else:
                        pe.wait_ge(s["z"], 2 * pair + t - 1)
                    transposes(bank[t], [xn[:, t, k * P:(k + 1) * P] for k in range(KC)], s["xnT_ps"])
                pe.wait_ge(s["xnT"], 2 * pair + 2)
                for w, first, sem in ((swq, 2, s["sq_ps"]), (swk, 4, s["sk_ps"])):
                    for e in range(KC):
                        for k in range(KC):
                            mm = nc.tensor.matmul(bank[first + e // 2][:, e % 2 * 256:e % 2 * 256 + 256],
                                                  w[:, k, e * P:(e + 1) * P], xnT[:, k, :], start=(k == 0), stop=(k == KC - 1))
                        if e % 2:
                            mm.then_inc(sem, 1)
                for t in range(2):
                    for k in range(KC):
                        mm = nc.tensor.matmul(bank[6 + t][:, :], xnT[:, k, t * P:(t + 1) * P], swv[:, k, :],
                                              start=(k == 0), stop=(k == KC - 1))
                    mm.then_inc(s["sv_ps"], 1)
                pe.wait_ge(s["q_rot"], pair + 1)
                pe.wait_ge(s["k_exp"], pair + 1)
                for t in range(2):
                    for c4 in range(KC):
                        for b in range(BT):
                            mm = nc.tensor.matmul(bank[t][b * L:(b + 1) * L, c4 * P:(c4 + 1) * P],
                                                  q_T[:, c4, t * P + b * L:t * P + (b + 1) * L],
                                                  k_exp[:, c4, t * BT + b, :, :].rearrange("p h l -> p (h l)"),
                                                  start=True, stop=True, tile_position=(0, b * L), skip_group_check=True)
                    mm.then_inc(s["ss_ps"], 1)
                for t in range(2):
                    pe.wait_ge(s["s_pT"], 2 * pair + t + 1)
                    pe.wait_ge(s["sv"], 2 * pair + t + 1)
                    for hd in range(HEADS):
                        at = hd % 4 * HD
                        mm = nc.tensor.matmul(bank[2 + t][at:at + HD, hd // 4 * P:(hd // 4 + 1) * P],
                                              v[:, t, hd * HD:(hd + 1) * HD], p_T[:, t, hd, :],
                                              start=True, stop=True, tile_position=(0, at), skip_group_check=True)
                    mm.then_inc(s["ao_ps"], 1)
                for t in range(2):
                    pe.wait_ge(s["aoT"], 2 * pair + t + 1)
                    for k in range(KC):
                        mm = nc.tensor.matmul(bank[4 + t][:, :], aoT[:, t, k, :], swo[:, k, :],
                                              start=(k == 0), stop=(k == KC - 1))
                    mm.then_inc(s["sy_ps"], 1)
                for t in range(2):
                    tile = 2 * pair + t
                    pe.wait_ge(s["xf"], tile + 1)
                    transposes(bank[6 + t], [xf[:, tile, k * P:(k + 1) * P] for k in range(KC)], s["xfT_ps"])
                for t in range(2):
                    pe.wait_ge(s["xfT"], 2 * pair + t + 1)
                    for k in range(KC):
                        mm = nc.tensor.matmul(bank[t][:, 0:E], xnT[:, k, t * P:(t + 1) * P], gate_w[:, k, :],
                                              start=(k == 0), stop=(k == KC - 1))
                    mm.then_inc(s["z_ps"], 1)

            pe.wait_ge(s["rt_sel"], 1)
            sel_all = sel.rearrange("p t e -> p (t e)")
            nc.tensor.matmul(bank[0][:, 0:TILES * E], const("before"), sel_all, start=True, stop=True).then_inc(s["rt_cnt_ps"], 1)
            nc.tensor.matmul(bank[1][:, 0:TILES * E], const("ones"), sel_all, start=True, stop=True).then_inc(s["rt_cnt_ps"], 1)

            pe.wait_ge(s["rt_map"], 1)

            def rows_T(slot_no, landed):
                pe.wait_ge((s["xg_in0"], s["xg_in1"])[slot_no], landed)
                transposes(bank[2], [xg[:, slot_no, k * P:(k + 1) * P] for k in range(KC)], s["xgT_ps"])

            def first_product(tile, slot_no):
                ready = pe.value_load(map_i[0:1, 0, ds(tile, 1)], min_val=1, max_val=E)
                at = pe.value_load(map_i[0:1, 1, ds(tile, 1)], min_val=0, max_val=EXPERT)
                pe.wait_ge(s["expert_ready"], ready)
                pe.wait_ge(s["xgT"], tile + 1)
                for half in range(2):
                    for k in range(KC):
                        mm = nc.tensor.matmul(bank[half][:, :], xgT[:, slot_no, k * P:(k + 1) * P],
                                              wbuf[:, ds(at + (k * EH + half * 512), 512)],
                                              start=(k == 0), stop=(k == KC - 1))
                    mm.then_inc(s["h_ps"], 1)

            def second_product(tile, slot_no):
                at = pe.value_load(map_i[0:1, 1, ds(tile, 1)], min_val=0, max_val=EXPERT)
                pe.wait_ge(s["hT0"], tile + 1)
                pe.wait_ge(s["hT1"], tile + 1)
                for k in range(HC):
                    mm = nc.tensor.matmul(bank[5 + slot_no][:, :], hT[:, slot_no, k * P:(k + 1) * P],
                                          wbuf[:, ds(at + (W2_AT + k * D), D)], start=(k == 0), stop=(k == HC - 1))
                mm.then_inc(s["y2_ps"], 1)

            def hidden_T(tile):
                pe.wait_ge(s["h"], tile * 2 + 2)
                transposes(bank[3], [h[:, k * P:(k + 1) * P] for k in range(4)], s["hT_ps0"])
                transposes(bank[4], [h[:, k * P:(k + 1) * P] for k in range(4, 8)], s["hT_ps1"])

            rows_T(0, 16)
            first_product(0, 0)
            rows_T(1, 16)
            hidden_T(0)
            with pe.Fori(0, (SLOT_TILES - 1) // 2) as i:
                for u in (1, 2):
                    first_product(i * 2 + u, u % 2)
                    rows_T((u + 1) % 2, i * 16 + 32)
                    second_product(i * 2 + (u - 1), (u - 1) % 2)
                    hidden_T(i * 2 + u)
            second_product(SLOT_TILES - 1, (SLOT_TILES - 1) % 2)

        @block.scalar
        def _(act):
            act.wait_ge(s["cols_in"], 16)

            def ctx_copies(tile):
                for n in range(2 * CC):
                    k, half = n // 2, n % 2
                    use = 2 * CC * tile + n
                    act.wait_ge(s["cxT_ps"], use + 1)
                    nc.scalar.copy(ctxT[:, tile % 2, k, 2 * half:2 * half + 2, 0:KEYS - 1],
                                   bank[use % 2][:, :].rearrange("p (b k) -> p b k", b=2)).then_inc(s["cxT"], 1)

            def biased(dst, first, ps_sem, count, bias, sem):
                for n in range(2):
                    act.wait_ge(ps_sem, count + n + 1)
                    for i in range(2):
                        e = 2 * n + i
                        op = nc.scalar.activation(dst[:, e, :], bank[first + n][:, i * 256:i * 256 + 256], ACT.Identity,
                                                  bias=col(bias, e))
                    op.then_inc(sem, 1)

            for pair in range(PAIRS):
                ctx_copies(2 * pair)
                biased(qT, 4, s["q_ps"], 2 * pair, "bq", s["qT"])
                ctx_copies(2 * pair + 1)
                for t in range(2):
                    act.wait_ge(s["sc_nb"], 2 * pair + t + 1)
                    nc.scalar.activation(probs[:, t, 0:KEYS], bank[2 + t][:, 0:KEYS], ACT.Exp, bias=sc_nb[:, t:t + 1],
                                         scale=X_SCALE, accum_out=sc_sum[:, t:t + 1]).then_inc(s["sc_exp"], 1)
                for t in range(2):
                    act.wait_ge(s["pT_ps"], 2 * pair + t + 1)
                    nc.scalar.copy(pT[:, t, :], bank[4 + t][:, 0:2 * P]).then_inc(s["pT"], 1)
                    nc.scalar.copy(p_left[0:B, t, :], bank[4 + t][0:B, 2 * P:3 * P]).then_inc(s["pT"], 1)
                biased(avT, 4, s["av_ps"], 2 * pair, "bv", s["avT"])

            for pair in range(PAIRS):
                for t in range(2):
                    act.wait_ge(s["xnT_ps"], 2 * pair + t + 1)
                    nc.scalar.copy(xnT[:, :, t * P:(t + 1) * P],
                                   bank[t][:, :].rearrange("p (k t) -> p k t", k=KC)).then_inc(s["xnT"], 1)
                biased(q_T, 2, s["sq_ps"], 2 * pair, "sbq", s["sq"])
                biased(k_T, 4, s["sk_ps"], 2 * pair, "sbk", s["sk"])
                for t in range(2):
                    act.wait_ge(s["s_sub"], 2 * pair + t + 1)
                    nc.scalar.activation(soft[:, t, :], soft[:, t, :], ACT.Exp, scale=H_SCALE).then_inc(s["s_exp"], 1)
                for t in range(2):
                    act.wait_ge(s["ao_ps"], 2 * pair + t + 1)
                    nc.scalar.copy(aoT[:, t, :, :].rearrange("p c q -> p (c q)"), bank[2 + t][:, :]).then_inc(s["aoT"], 1)
                for t in range(2):
                    tile = 2 * pair + t
                    act.wait_ge(s["x_post"], tile + 1)
                    act.dma_start(out[tile * P:(tile + 1) * P, :], x[:, tile * D:(tile + 1) * D]).then_inc(s["out_init"], 16)
                for t in range(2):
                    act.wait_ge(s["xfT_ps"], 2 * pair + t + 1)
                    nc.scalar.copy(xnT[:, :, t * P:(t + 1) * P],
                                   bank[6 + t][:, :].rearrange("p (k t) -> p k t", k=KC)).then_inc(s["xfT"], 1)
            act.wait_ge(s["z"], TILES)
            nc.scalar.activation(sig, z, ACT.Exp, scale=-1.0).then_inc(s["rt_exp"], 1)

            xg_in = (s["xg_in0"], s["xg_in1"])

            def load_rows(tile, slot_no):
                act.dma_start(xg[:, slot_no, :], xs_dram[ds(tile * P, P), :]).then_inc(xg_in[slot_no], 16)

            def silu(tile):
                for half in range(2):
                    act.wait_ge(s["h_ps"], tile * 2 + (half + 1))
                    nc.scalar.activation(h[:, half * 512:half * 512 + 512], bank[half][:, :], ACT.Silu).then_inc(s["h"], 1)

            def hidden_copy(tile, slot_no):
                act.wait_ge(s["hT_ps0"], tile + 1)
                nc.scalar.copy(hT[:, slot_no, 0:512], bank[3][:, :]).then_inc(s["hT0"], 1)

            def gated(tile, slot_no):
                act.wait_ge(s["gate"], tile + 1)
                act.wait_ge(s["added"], tile + 1)
                act.wait_ge(s["y2_ps"], tile + 1)
                nc.scalar.activation(y_out[:, slot_no, :], bank[5 + slot_no][:, :], ACT.Copy,
                                     scale=gates[:, slot_no, 2:3]).then_inc(s["y2"], 1)

            act.wait_ge(s["scattered"], 16 * 2 * TILES)
            load_rows(0, 0)
            load_rows(1, 1)
            silu(0)
            hidden_copy(0, 0)
            act.wait_ge(s["idx"], 1)
            load_rows(2, 0)
            with act.Fori(0, (SLOT_TILES - 1) // 2) as i:
                for u in (1, 2):
                    silu(i * 2 + u)
                    gated(i * 2 + (u - 1), (u - 1) % 2)
                    hidden_copy(i * 2 + u, u % 2)
                    act.wait_ge(s["idx"], i * 2 + (u + 1))
                    load_rows(i * 2 + (u + 2), u % 2)
            gated(SLOT_TILES - 1, (SLOT_TILES - 1) % 2)
            act.wait_ge(xg_in[(SLOT_TILES + 1) % 2], 16 * ((SLOT_TILES + 1) // 2 + 1))

        @block.vector
        def _(dve):
            def norm_stats(srcs, stats_, mv_, ve_, sems, n, done, pair):
                stats_sem, mv_sem, ve_sem = sems
                for i, src in enumerate(srcs):
                    nc.vector.bn_stats(stats_[:, i, :], src).then_inc(stats_sem, 1)
                dve.wait_ge(stats_sem, done + n)
                for i in range(n):
                    nc.vector.bn_aggr(mv_[:, i, :], stats_[:, i, :]).then_inc(mv_sem, 1)
                dve.wait_ge(mv_sem, done + n)
                nc.vector.tensor_scalar(ve_, mv_[:, :, 1], EPS, None, ALU.add).then_inc(ve_sem, 1)

            def normalise(dst, src, mean, inverse):
                return nc.vector.tensor_scalar(dst, src, mean, inverse, ALU.subtract, ALU.mult)

            def x_at(tile):
                return x[:, tile * D:(tile + 1) * D]

            def norm_pair(srcs, dsts, name, pair):
                sems = {k: s[f"{name}_{k}"] for k in ("stats", "mv", "ve", "rstd")}
                norm_stats(srcs, stats, mv, ve, (sems["stats"], sems["mv"], sems["ve"]), 2, 2 * pair, pair)
                dve.wait_ge(sems["rstd"], pair + 1)
                out_sem = s[f"{name}_out"]
                for t in range(2):
                    normalise(dsts[t], srcs[t], mv[:, t, 0:1], rstd[:, t:t + 1]).then_inc(out_sem, 1)
                dve.wait_ge(out_sem, 2 * pair + 2)

            nc.vector.memset(neg_half, -0.5).then_inc(s["route"], 1)
            dve.wait_ge(s["x_in"], 16)
            dve.wait_ge(s["cols_in"], 16)

            def left_norm():
                dve.wait_ge(s["left_in"], 16)
                norm_stats([left_n[0:B, :]], l_stats[0:B, None, :], l_mv[0:B, None, :], l_ve[0:B, :],
                           (s["left_stats"], s["left_mv"], s["left_ve"]), 1, 0, 0)
                dve.wait_ge(s["left_rstd"], 1)
                normalise(left_n[0:B, :], left_n[0:B, :], l_mv[0:B, 0:1], l_rstd[0:B, :]).then_inc(s["left_n"], 1)

            def ctx_norm(tile):
                u, part = tile % 2, ctx_n[:, tile % 4]
                dve.wait_ge(ctx_in[tile % 4], 16 * (tile // 4 + 1))
                pieces = [part[:, b, c2, :] for b in range(BT) for c2 in range(2)]
                norm_stats(pieces, cx_stats[:, u], cx_mv[:, u], cx_ve[:, u], (s["cx_stats"], s["cx_mv"], s["cx_ve"]), 8, 8 * tile, 0)
                dve.wait_ge(s["cx_rstd"], tile + 1)
                for i, piece in enumerate(pieces):
                    op = normalise(piece, piece, cx_mv[:, u, i, 0:1], cx_rstd[:, u, i:i + 1])
                op.then_inc(s["cx_n"], 1)

            for pair in range(PAIRS):
                tiles = [x_at(2 * pair), x_at(2 * pair + 1)]
                norm_pair(tiles, [xn[:, 0, :], xn[:, 1, :]], "ln1", pair)
                norm_pair([xn[:, 0, :], xn[:, 1, :]], [xn[:, 0, :], xn[:, 1, :]], "ln2", pair)
                if pair == 0:
                    left_norm()
                for t in range(2):
                    tile = 2 * pair + t
                    dve.wait_ge(s["x1T_ps"], tile + 1)
                    for k in range(KC):
                        op = nc.vector.tensor_scalar(x1T[:, k, tile * P:(tile + 1) * P], bank[2 + t][:, k * P:(k + 1) * P],
                                                     col("ln1_g", k), col("ln1_b", k), ALU.mult, ALU.add)
                    op.then_inc(s["x1T"], 1)
                if pair == 0:
                    dve.wait_ge(s["left_ps"], 1)
                    nc.vector.tensor_copy(left_T, bank[0][:, 0:CC * B].rearrange("p (c b) -> p c b", c=CC)).then_inc(s["left_T"], 1)
                    dve.wait_ge(s["kb_ps"], 1)
                    nc.vector.tensor_tensor(kb, bank[1][:, 0:KC], cols[:, COLS["bk"]], ALU.add).then_inc(s["kb"], 1)
                    dve.wait_ge(s["left_T"], 1)
                    ctx_norm(0)
                    ctx_norm(1)

            for pair in range(PAIRS):
                for t in range(2):
                    tile = 2 * pair + t
                    nc.vector.tensor_copy(ctxT[:, t, :, :, KEYS - 1], left_T[:, :, tile * BT:(tile + 1) * BT]).then_inc(s["left_cols"], 1)
                if pair + 1 < PAIRS:
                    ctx_norm(2 * pair + 2)
                    ctx_norm(2 * pair + 3)
                for k in range(CC):
                    if k != 1:
                        dve.wait_ge(s["qk_ps"], 2 * pair + k // 2 + 1)
                    op = nc.vector.tensor_scalar(qkT[:, k, :], bank[6 + k // 2][:, k % 2 * 256:k % 2 * 256 + 256],
                                                 col("ln2_g", k), None, ALU.mult)
                op.then_inc(s["qkT"], 1)
                nc.vector.tensor_copy(q_bias, bank[7][:, 256:258]).then_inc(s["q_bias"], 1)
                dve.wait_ge(s["q_bias"], pair + 1)
                for t in range(2):
                    tile = 2 * pair + t
                    one = slice(t, t + 1)
                    dve.wait_ge(s["sc_ps"], tile + 1)
                    nc.vector.tensor_reduce(sc_max[:, one], bank[2 + t][:, 0:KEYS], AX.X, ALU.max).then_inc(s["sc_max"], 1)
                    dve.wait_ge(s["sc_max"], tile + 1)
                    nc.vector.tensor_tensor(sc_u[:, one], sc_max[:, one], q_bias[:, one], ALU.add).then_inc(s["sc_u"], 1)
                    dve.wait_ge(s["sc_u"], tile + 1)
                    nc.vector.tensor_scalar(sc_nb[:, one], q_bias[:, one], sc_u[:, one], X_SCALE, ALU.subtract, ALU.mult)\
                        .then_inc(s["sc_nb"], 1)
                for t in range(2):
                    tile = 2 * pair + t
                    dve.wait_ge(s["sc_exp"], tile + 1)
                    nc.vector.reciprocal(sc_rinv[:, t:t + 1], sc_sum[:, t:t + 1]).then_inc(s["sc_rinv"], 1)
                    dve.wait_ge(s["sc_rinv"], tile + 1)
                    nc.vector.tensor_scalar(probs[:, t, 0:KEYS], probs[:, t, 0:KEYS], sc_rinv[:, t:t + 1], None, ALU.mult)\
                        .then_inc(s["sc_p"], 1)
                    dve.wait_ge(s["sc_p"], tile + 1)
                    at = CONST["left_mask"].start + 28 - BT * tile
                    nc.vector.tensor_scalar(p_mask[:, t, :], consts[:, at:at + B], probs[:, t, KEYS - 1:KEYS], None, ALU.mult)\
                        .then_inc(s["sc_pm"], 1)
                for t in range(2):
                    tile = 2 * pair + t
                    dve.wait_ge(s["cv_ps"], tile + 1)
                    for k in range(CC):
                        op = nc.vector.tensor_scalar(x2aT[:, k, t * P:(t + 1) * P], bank[6 + t][:, k * P:(k + 1) * P],
                                                     col("ln2_g", k), col("ln2_b", k), ALU.mult, ALU.add)
                    op.then_inc(s["x2aT"], 1)
                for t in range(2):
                    tile = 2 * pair + t
                    dve.wait_ge(s["y_ps"], tile + 1)
                    dve.wait_ge(s["x_plus_bo"], tile + 1)
                    nc.vector.tensor_tensor(x_at(tile), bank[2 + t][:, :], x_at(tile), ALU.add).then_inc(s["x_new"], 1)

            swap = [(i + HD // 2) % HD for i in range(HD)]

            def by_place(a):
                return a.rearrange("p (n l) -> p n l", l=L)

            table = [P, KC * 2 * BT, L]
            sin_t = const("sin")[:, None, :].to_broadcast(table)

            def first_norm(pair):
                dve.wait_ge(s["x_new"], 2 * pair + 2)
                norm_pair([x_at(2 * pair), x_at(2 * pair + 1)], [xn[:, 0, :], xn[:, 1, :]], "ln3", pair)

            first_norm(0)
            dve.wait_ge(s["ptx_zero"], 2)
            for pair in range(PAIRS):
                for src, sw, name in ((qb, q_sw, "q"), (kbuf, k_sw, "k")):
                    dve.wait_ge(s[f"s{name}"], 2 * pair + 2)
                    nc.vector.stream_shuffle(sw, src, swap).then_inc(s[f"{name}_swap"], 1)
                    dve.wait_ge(s[f"{name}_swap"], pair + 1)
                    nc.vector.tensor_tensor(by_place(sw), by_place(sw), sin_t, ALU.mult).then_inc(s[f"{name}_sin"], 1)
                    dve.wait_ge(s[f"{name}_sin"], pair + 1)
                    dve.wait_ge(s[f"{name}_cos"], pair + 1)
                    if name == "q":
                        nc.vector.tensor_tensor(src, src, sw, ALU.add).then_inc(s["q_rot"], 1)
                        continue
                    for r in range(4):
                        part = slice(r * HD, (r + 1) * HD)
                        op = nc.vector.tensor_tensor(k_exp[part, :, :, r, :],
                                                     src[part].rearrange("p (c b l) -> p c b l", c=KC, l=L),
                                                     sw[part].rearrange("p (c b l) -> p c b l", c=KC, l=L), ALU.add)
                    op.then_inc(s["k_exp"], 1)
                for t in range(2):
                    dve.wait_ge(s["sv_ps"], 2 * pair + t + 1)
                    nc.vector.tensor_tensor(v[:, t, :], bank[6 + t][:, :], row("sbv"), ALU.add).then_inc(s["sv"], 1)
                if pair + 1 < PAIRS:
                    first_norm(pair + 1)
                by_head = [P, HEADS, L]
                for t in range(2):
                    tile = 2 * pair + t
                    dve.wait_ge(s["ss_ps"], tile + 1)
                    scores = bank[t][:, :].rearrange("p (h l) -> p h l", l=L)
                    nc.vector.tensor_reduce(s_max[:, t, :], scores, AX.X, ALU.max).then_inc(s["s_max"], 1)
                    dve.wait_ge(s["s_max"], tile + 1)
                    nc.vector.tensor_tensor(by_place(soft[:, t, :]), scores, s_max[:, t, :, None].to_broadcast(by_head),
                                            ALU.subtract).then_inc(s["s_sub"], 1)
                for t in range(2):
                    tile = 2 * pair + t
                    dve.wait_ge(s["s_exp"], tile + 1)
                    nc.vector.tensor_reduce(s_sum[:, t, :], by_place(soft[:, t, :]), AX.X, ALU.add).then_inc(s["s_sum"], 1)
                    dve.wait_ge(s["s_sum"], tile + 1)
                    nc.vector.reciprocal(s_rinv[:, t, :], s_sum[:, t, :]).then_inc(s["s_rinv"], 1)
                    dve.wait_ge(s["s_rinv"], tile + 1)
                    nc.vector.tensor_tensor(by_place(soft[:, t, :]), by_place(soft[:, t, :]),
                                            s_rinv[:, t, :, None].to_broadcast(by_head), ALU.mult).then_inc(s["s_norm"], 1)
                    dve.wait_ge(s["s_norm"], tile + 1)
                    for b in range(BT):
                        part = slice(b * L, (b + 1) * L)
                        op = nc.vector.transpose(p_T[part, t, :, b * L:(b + 1) * L], by_place(soft[part, t, :]))
                    op.then_inc(s["s_pT"], 1)
                for t in range(2):
                    tile = 2 * pair + t
                    dve.wait_ge(s["sy_ps"], tile + 1)
                    dve.wait_ge(s["x_plus_sbo"], tile + 1)
                    nc.vector.tensor_tensor(x_at(tile), bank[4 + t][:, :], x_at(tile), ALU.add).then_inc(s["x_post"], 1)
                dve.wait_ge(s["x_post"], 2 * pair + 2)
                norm_stats([x_at(2 * pair), x_at(2 * pair + 1)], stats, mv, ve, (s["ln4_stats"], s["ln4_mv"], s["ln4_ve"]), 2, 2 * pair, pair)
                dve.wait_ge(s["ln4_rstd"], pair + 1)
                for t in range(2):
                    tile = 2 * pair + t
                    normalise(xf[:, tile, 0:D], x_at(tile), mv[:, t, 0:1], rstd[:, t:t + 1]).then_inc(s["xf"], 1)
                for t in range(2):
                    tile = 2 * pair + t
                    dve.wait_ge(s["z_ps"], tile + 1)
                    nc.vector.tensor_tensor(z[:, tile, :], bank[t][:, 0:E], row("balance"), ALU.add).then_inc(s["z"], 1)

            steps = [1]

            def then(op):
                op.then_inc(s["route"], 1)
                steps[0] += 1
                dve.wait_ge(s["route"], steps[0])

            tt, ts = nc.vector.tensor_tensor, nc.vector.tensor_scalar
            dve.wait_ge(s["z"], TILES)
            full = [P, TILES, E, E]
            then(tt(cmp_a, z[:, :, None, :].to_broadcast(full), z[:, :, :, None].to_broadcast(full), ALU.is_gt))
            then(tt(cmp_b, z[:, :, None, :].to_broadcast(full), z[:, :, :, None].to_broadcast(full), ALU.is_equal))
            low = const("low")
            then(tt(cmp_b.rearrange("p t a b -> p t (a b)"), cmp_b.rearrange("p t a b -> p t (a b)"),
                    low[:, None, :].to_broadcast([P, TILES, E * E]), ALU.mult))
            then(tt(cmp_a, cmp_a, cmp_b, ALU.add))
            then(nc.vector.tensor_reduce(rank, cmp_a, AX.X, ALU.add))
            ts(sel, rank, 2.0, None, ALU.is_lt).then_inc(s["rt_sel"], 1)
            then(ts(sel1, rank, 0.0, None, ALU.is_equal))
            then(ts(sel2, rank, 1.0, None, ALU.is_equal))
            dve.wait_ge(s["rt_exp"], 1)
            then(ts(sig, sig, 1.0, None, ALU.add))
            then(nc.vector.reciprocal(sig, sig))
            for g, chosen in ((g1, sel1), (g2, sel2)):
                then(tt(picked, sig, chosen, ALU.mult))
                then(nc.vector.tensor_reduce(g, picked, AX.X, ALU.add))
            then(tt(gsum, g1, g2, ALU.add))
            then(ts(gsum, gsum, 1e-6, None, ALU.add))
            then(nc.vector.reciprocal(gsum, gsum))
            for g, chosen, g_col, e_col in ((g1, sel1, C_G1, C_E1), (g2, sel2, C_G2, C_E2)):
                then(tt(xf[:, :, g_col], g, gsum, ALU.mult))
                then(tt(picked, chosen, const("tile_no")[:, None, 0:E].to_broadcast([P, TILES, E]), ALU.mult))
                then(nc.vector.tensor_reduce(xf[:, :, e_col], picked, AX.X, ALU.add))
            dve.wait_ge(s["ints_in"], 16)
            then(nc.vector.tensor_copy(xf[:, :, C_TOKEN].bitcast(I32), token_no[:, 0:TILES]))
            then(nc.vector.memset(base[:, 0, :], 0.0))
            dve.wait_ge(s["rt_cnt_ps"], 2)
            for tile in range(TILES):
                then(tt(base[:, tile + 1, :], bank[1][:, tile * E:(tile + 1) * E], base[:, tile, :], ALU.add))
            then(tt(over, base[:, TILES, :, None].to_broadcast([P, E, 8]), const("steps")[:, None, :].to_broadcast([P, E, 8]),
                    ALU.is_gt))
            then(nc.vector.tensor_reduce(ntile, over, AX.X, ALU.add))
            then(ts(ntile, ntile, 1.0, None, ALU.add))
            then(tt(ends_tmp, ntile[:, None, :].to_broadcast([P, E, E]), low.rearrange("p (a b) -> p a b", a=E), ALU.mult))
            then(nc.vector.tensor_reduce(ends, ends_tmp, AX.X, ALU.add))
            then(tt(slot, bank[0][:, 0:TILES * E].rearrange("p (t e) -> p t e", t=TILES), base[:, 0:TILES, :], ALU.add))
            then(ts(ends_tmp[:, 0, :], ends, float(P), None, ALU.mult))
            then(tt(slot, slot, ends_tmp[:, 0, None, :].to_broadcast([P, TILES, E]), ALU.add))
            for n, chosen in enumerate((sel1, sel2)):
                then(tt(picked, slot, chosen, ALU.mult))
                then(nc.vector.tensor_reduce(slot_f[:, n, :], picked, AX.X, ALU.add))
            nc.vector.tensor_copy(slot_i, slot_f).then_inc(s["rt_slots"], 1)
            then(tt(ends, ends, ntile, ALU.add))
            by_tile = [P, 32, E]
            then(tt(emap_cmp, ends[:, None, :].to_broadcast(by_tile), const("tile_no")[:, :, None].to_broadcast(by_tile), ALU.is_le))
            then(nc.vector.tensor_reduce(emap, emap_cmp, AX.X, ALU.add))
            then(ts(emap, emap, float(E - 1), None, ALU.min))
            then(ts(map_i[:, 0, :], emap, 1.0, None, ALU.add))
            then(nc.vector.tensor_copy(map_i[:, 1, :], emap))
            then(ts(map_i[:, 1, :], map_i[:, 1, :], 1, int(np.log2(EXPERT)), ALU.bitwise_and, ALU.logical_shift_left))
            nc.vector.tensor_copy(map_i[:, 2, 0:E], ends).then_inc(s["rt_map"], 1)

            def rows_copy(tile, slot_no):
                dve.wait_ge(s["xgT_ps"], tile + 1)
                nc.vector.tensor_copy(xgT[:, slot_no, :], bank[2][:, :]).then_inc(s["xgT"], 1)

            def hidden_copy(tile, slot_no):
                dve.wait_ge(s["hT_ps1"], tile + 1)
                nc.vector.tensor_copy(hT[:, slot_no, 512:1024], bank[4][:, :]).then_inc(s["hT1"], 1)

            def gate_of(tile, slot_no):
                expert = emap[:, ds(tile, 1)]
                for n, (g_col, e_col) in enumerate(((C_G1, C_E1), (C_G2, C_E2))):
                    op = ts(gates[:, slot_no, n:n + 1], xg[:, slot_no, e_col:e_col + 1], expert,
                            xg[:, slot_no, g_col:g_col + 1], ALU.is_equal, ALU.mult)
                op.then_inc(s["gate_parts"], 1)
                dve.wait_ge(s["gate_parts"], tile + 1)
                tt(gates[:, slot_no, 2:3], gates[:, slot_no, 0:1], gates[:, slot_no, 1:2], ALU.add).then_inc(s["gate"], 1)
                dve.wait_ge(s["added"], tile + 1)
                nc.vector.tensor_copy(idx[:, slot_no:slot_no + 1], xg[:, slot_no, C_TOKEN:C_TOKEN + 1].bitcast(I32)).then_inc(s["idx"], 1)

            rows_copy(0, 0)
            rows_copy(1, 1)
            hidden_copy(0, 0)
            gate_of(0, 0)
            with dve.Fori(0, (SLOT_TILES - 1) // 2) as i:
                for u in (1, 2):
                    rows_copy(i * 2 + (u + 1), (u + 1) % 2)
                    hidden_copy(i * 2 + u, u % 2)
                    gate_of(i * 2 + u, u % 2)

        @block.gpsimd
        def _(pool):
            def inverse_root(name, count, out_, in_, n, parts=P):
                pool.wait_ge(s[f"{name}_ve"], count)
                nc.gpsimd.tensor_tensor(out_, in_, neg_half[0:parts, 0:n], ALU.pow).then_inc(s[f"{name}_rstd"], 1)

            def x_at(tile):
                return x[:, tile * D:(tile + 1) * D]

            def ctx_root(tile):
                inverse_root("cx", tile + 1, cx_rstd[:, tile % 2], cx_ve[:, tile % 2], 8)

            pool.wait_ge(s["route"], 1)
            for pair in range(PAIRS):
                inverse_root("ln1", pair + 1, rstd, ve, 2)
                inverse_root("ln2", pair + 1, rstd, ve, 2)
                if pair == 0:
                    inverse_root("left", 1, l_rstd[0:B, :], l_ve[0:B, :], 1, B)
                    ctx_root(0)
                    ctx_root(1)
            pool.wait_ge(s["rows_in"], 16)
            for tile in range(TILES):
                nc.gpsimd.tensor_tensor(x_at(tile), x_at(tile), row("bo"), ALU.add).then_inc(s["x_plus_bo"], 1)
            for tile in range(2, TILES):
                ctx_root(tile)
            inverse_root("ln3", 1, rstd, ve, 2)
            pool.wait_ge(s["y_ps"], TILES)
            nc.gpsimd.memset(k_exp, 0.0).then_inc(s["ptx_zero"], 1)
            nc.gpsimd.memset(p_T, 0.0).then_inc(s["ptx_zero"], 1)
            table = [P, KC * 2 * BT, L]
            cos_t = const("cos")[:, None, :].to_broadcast(table)
            for pair in range(PAIRS):
                for buf, name in ((qb, "q"), (kbuf, "k")):
                    pool.wait_ge(s[f"{name}_swap"], pair + 1)
                    by_place = buf.rearrange("p (n l) -> p n l", l=L)
                    nc.gpsimd.tensor_tensor(by_place, by_place, cos_t, ALU.mult).then_inc(s[f"{name}_cos"], 1)
                for t in range(2):
                    tile = 2 * pair + t
                    pool.wait_ge(s["ln3_out"], tile + 1)
                    nc.gpsimd.tensor_tensor(x_at(tile), x_at(tile), row("sbo"), ALU.add).then_inc(s["x_plus_sbo"], 1)
                if pair + 1 < PAIRS:
                    inverse_root("ln3", pair + 2, rstd, ve, 2)
                inverse_root("ln4", pair + 1, rstd, ve, 2)
                if pair == 0:
                    pool.wait_ge(s["ints_in"], 16)
                    nc.gpsimd.memset(zrow, 0.0).then_inc(s["zrow_fill"], 1)
                    pool.wait_ge(s["zrow_fill"], 1)
                    nc.gpsimd.tensor_copy(zrow[:, C_TOKEN:C_TOKEN + 1].bitcast(I32), token_no[:, TILES:TILES + 1]).then_inc(s["zrow"], 1)
                    nc.gpsimd.memset(xf[:, :, C_E2 + 1:ROW], 0.0).then_inc(s["rows_set"], 1)
            pool.wait_ge(s["xs_zero"], 16)
            pool.wait_ge(s["rt_slots"], 1)
            pool.wait_ge(s["rows_set"], 1)
            for tile in range(TILES):
                for n in range(2):
                    nc.gpsimd.indirect_dma_start(
                        xs_dram, bass.IndirectOffsetOnAxis(slot_i[:, n, tile:tile + 1].bitcast(U32), axis=0), xf[:, tile, :], None,
                    ).then_inc(s["scattered"], 16)

            def add_rows(tile, slot_no, first=False):
                pool.wait_ge(s["y2"], tile + 1)
                pool.wait_ge(s["idx"], tile + 1)
                if not first:
                    pool.wait_ge(s["scat"], tile * 16)
                pool.sem_inc(s["added"], 1)
                nc.gpsimd.indirect_dma_start(
                    out, bass.IndirectOffsetOnAxis(idx[:, slot_no:slot_no + 1].bitcast(U32), axis=0), y_out[:, slot_no, :], None,
                    compute_op=ALU.add).then_inc(s["scat"], 16)

            pool.wait_ge(s["out_init"], 16 * TILES)
            pool.wait_ge(s["out_spare"], 16)
            pool.sem_inc(s["added"], 1)
            add_rows(0, 0, first=True)
            with pool.Fori(0, (SLOT_TILES - 1) // 2) as i:
                for u in (1, 2):
                    add_rows(i * 2 + u, u % 2)


def constants():
    c = np.zeros((P, CONST_W), np.float32)
    p = np.arange(P)
    c[:, CONST["ident"]] = np.eye(P)
    c[:, CONST["before"]] = p[:, None] < p[None, :]
    c[:, CONST["ones"]] = 1.0
    half = HD // 2
    theta = np.float32(10000.0) ** (-np.arange(half, dtype=np.float32) / half)
    angle = theta[p % half][:, None] * np.arange(L, dtype=np.float32)[None, :]
    c[:, CONST["cos"]] = np.cos(angle)
    c[:, CONST["sin"]] = np.sin(angle) * np.where(p % HD < half, -1.0, 1.0)[:, None]
    c[:, CONST["left_mask"]] = np.arange(60)[None, :] - (B - BT) == p[:, None] // L
    e = np.arange(E)
    c[:, CONST["low"]] = (e[None, :] < e[:, None]).reshape(1, -1)
    c[:, CONST["tile_no"]] = np.arange(32)
    c[:, CONST["steps"]] = P * np.arange(1, 9)
    token_no = (p[:, None] + P * np.arange(TILES + 1)[None, :]).astype(np.int32)
    return c, token_no


def kernel(x, ctx_768, L0_xattn_ln1_g, L0_xattn_ln1_b, L0_xattn_ln2_g, L0_xattn_ln2_b, L0_xattn_Wq, L0_xattn_bq,
           L0_xattn_Wk, L0_xattn_bk, L0_xattn_Wv, L0_xattn_bv, L0_xattn_Wo, L0_xattn_bo, L0_attn_Wq, L0_attn_bq,
           L0_attn_Wk, L0_attn_bk, L0_attn_Wv, L0_attn_bv, L0_attn_Wo, L0_attn_bo, L0_ffn_gate_w,
           L0_ffn_balance_bias, L0_ffn_w1, L0_ffn_w2):
    import concourse.bacc as bacc
    from concourse.bass_utils import run_bass_kernel_spmd

    def blocks(a):
        return np.asarray(a).reshape(-1, P).T

    cols = np.concatenate([blocks(a) for a in (L0_xattn_ln1_g, L0_xattn_ln1_b, L0_xattn_bq, L0_xattn_ln2_g, L0_xattn_ln2_b,
                                               L0_xattn_bk, L0_xattn_bv, L0_attn_bq, L0_attn_bk)], 1)
    rows = np.concatenate([np.asarray(a) for a in (L0_xattn_bo, L0_attn_bv, L0_attn_bo, L0_ffn_balance_bias)])
    w1T = np.asarray(L0_ffn_w1).transpose(0, 2, 1).reshape(E, KC, P, EH).transpose(0, 2, 1, 3).reshape(E, P, KC * EH)
    w2T = np.asarray(L0_ffn_w2).transpose(0, 2, 1).reshape(E, HC, P, D).transpose(0, 2, 1, 3).reshape(E, P, HC * D)
    consts, token_no = constants()
    arrays = {
        "x": np.asarray(x).reshape(TOK, D), "ctx_768": ctx_768, "cols": cols, "rows": np.broadcast_to(rows, (P, ROWS_W)),
        "consts": consts, "token_no": token_no,
        "wq": L0_xattn_Wq, "wk": L0_xattn_Wk, "wkT": np.asarray(L0_xattn_Wk).T, "wv": L0_xattn_Wv, "wo": L0_xattn_Wo,
        "swqT": np.asarray(L0_attn_Wq).T, "swkT": np.asarray(L0_attn_Wk).T, "swvT": np.asarray(L0_attn_Wv).T,
        "swoT": np.asarray(L0_attn_Wo).T, "gate_wT": np.asarray(L0_ffn_gate_w).T,
        "experts": np.concatenate([w1T, w2T], 2),
    }
    arrays = {name: np.ascontiguousarray(a) for name, a in arrays.items()}
    nc = bacc.Bacc("TRN2", target_bir_lowering=False, num_devices=1)
    t_in = {name: nc.dram_tensor(f"in_{name}", a.shape, mybir.dt.from_np(a.dtype), kind="ExternalInput").ap()
            for name, a in arrays.items()}
    out = nc.dram_tensor("out", (TOK + P, D), F32, kind="ExternalOutput").ap()
    program(nc, t_in, out)
    result = run_bass_kernel_spmd(nc, [{f"in_{name}": a for name, a in arrays.items()}], core_ids=[0])
    return result.results[0]["out"][0:TOK].reshape(B, L, D)
```

```python
from contextlib import ExitStack

import numpy as np

import concourse.bass as bass
from concourse import mybir

F32 = mybir.dt.float32
F16 = mybir.dt.float16
I32 = mybir.dt.int32
U32 = mybir.dt.uint32
ALU = mybir.AluOpType
ACT = mybir.ActivationFunctionType
AX = mybir.AxisListType
ds = bass.ds

P = 128
B, L, D = 32, 32, 512
KEYS, DC = 257, 384
KC, CC = D // P, DC // P
TOK = B * L
TILES = TOK // P
PAIRS = TILES // 2
BT = P // L
HEADS, HD = 16, 32
E, EH = 8, 1024
HC = EH // P
EPS = 1e-5
X_SCALE = float(D) ** -0.5
H_SCALE = float(HD) ** -0.5
SLOT_TILES = (2 * TOK + (E - 1) * (P - 1) + P) // P
ROW = D + 8
C_TOKEN, C_G1, C_E1, C_G2, C_E2 = range(D, D + 5)
W2_AT = KC * EH
EXPERT = KC * EH + HC * D
W_SCALE = 256.0
W_PIECES = 4
PIECE = EXPERT // W_PIECES
ROW_SLOTS = 2

CONST = {}
_at = 0
for _name, _width in (("ident", P), ("before", P), ("ones", P), ("cos", L), ("sin", L), ("left_mask", 60),
                      ("low", E * E), ("tile_no", 32), ("steps", 8)):
    CONST[_name] = slice(_at, _at + _width)
    _at += _width
CONST_W = _at
COLS = {}
_at = 0
for _name, _width in (("ln1_g", KC), ("ln1_b", KC), ("bq", KC), ("ln2_g", CC), ("ln2_b", CC), ("bk", KC), ("bv", KC),
                      ("sbq", KC), ("sbk", KC)):
    COLS[_name] = slice(_at, _at + _width)
    _at += _width
COLS_W = _at
ROWS = {"bo": slice(0, D), "sbv": slice(D, 2 * D), "sbo": slice(2 * D, 3 * D), "balance": slice(3 * D, 3 * D + E)}
ROWS_W = 3 * D + E

SEMS = """const_in x_in left_in wq_in wkT_in wk_in wv_in wo_in swq_in swk_in swv_in swo_in gate_in
rows_in cols_in ints_in
ctx_in0 ctx_in1 ctx_in2 ctx_in3
norm_stats norm_mv ln1_ve ln1_rstd ln1_out ln2_ve ln2_rstd ln2_out
x1T_ps x1T x_plus_bo
left_ve left_rstd left_n left_ps left_T
kb_ps kb
cx_ve cx_rstd cx_n cxT_ps cxT left_cols
q_ps qT qk_ps qkT q_bias sc_ps sc_max sc_u sc_nb sc_exp sc_rinv sc_pm pT_ps pT cv_ps cv cvT_ps x2aT av_ps avT y_ps x_new
ptx_zero ln3_ve ln3_rstd ln3_out xnT_ps xnT sq_ps sk_ps sq sk q_swap k_swap q_cos k_cos q_sin k_sin
q_rot k_exp k_zero sv_ps sv ss_ps s_max s_sub s_exp s_sum s_rinv s_norm s_pT ao_ps aoT sy_ps x_post x_plus_sbo
ln4_ve ln4_rstd xf xf_hi xf_lo xfT_ps xfT z_ps z out_init
route rt_sel rt_cnt_ps rt_z rt_exp rt_slots rt_map zrow_fill zrow xs_zero rows_set scattered
xg_in0 xg_in1 fields xgT_ps xgT h_ps h h_hi h_lo hT_ps0 hT_ps1 hT0 hT1 y2_ps y2 gate_parts gate idx scat added out_spare
ident16 staged w_hi w1_lo w2_lo""".split()


def program(nc, t_in, out):
    with ExitStack() as ctx:
        def sb(name, shape, dt=F32):
            return ctx.enter_context(nc.sbuf_tensor(name, shape, dt))

        s = {n: ctx.enter_context(nc.semaphore(n)) for n in SEMS}
        ctx_in = (s["ctx_in0"], s["ctx_in1"], s["ctx_in2"], s["ctx_in3"])
        bank = [ctx.enter_context(nc.psum_tensor(f"bank{i}", [P, 512], F32)) for i in range(8)]
        xs_dram = nc.dram_tensor("routed_rows", ((SLOT_TILES + ROW_SLOTS) * P, ROW), F32).ap()

        consts = sb("consts", [P, CONST_W])
        cols = sb("cols", [P, COLS_W])
        rows = sb("rows", [P, ROWS_W])
        token_no = sb("token_no", [P, TILES + 1], I32)
        gate_w = sb("gate_w", [P, KC, E])
        x = sb("x", [P, TILES * D])
        shared = sb("shared", [P, TILES * ROW])
        wbuf = sb("wbuf", [P, 2 * EXPERT])
        ctx_region = sb("ctx_region", [P, 4 * BT * 2 * DC])
        ctxT_region = sb("ctxT_region", [P, 2 * CC * BT * KEYS])
        small = sb("small", [P, 600])
        ints = sb("ints", [P, 128], I32)
        xn = sb("xn", [P, 2, D])
        actT = sb("actT", [P, KC * 2 * P])
        misc = sb("misc", [P, 3072])
        ident16 = sb("ident16", [P, P], F16)

        def const(name):
            return consts[:, CONST[name]]

        def col(name, i):
            return cols[:, COLS[name].start + i:COLS[name].start + i + 1]

        def row(name):
            return rows[:, ROWS[name]]

        ident = const("ident")

        class Carve:

            def __init__(self, region, at, end):
                self.region, self.at, self.end = region, at, end

            def take(self, *shape):
                n = int(np.prod(shape))
                assert self.at + n <= self.end, (self.at, n, self.end)
                part = self.region[:, self.at:self.at + n]
                self.at += n
                if len(shape) == 1:
                    return part
                names = "abcd"[:len(shape)]
                pattern = f"p ({' '.join(names)}) -> p {' '.join(names)}"
                return part.rearrange(pattern, **dict(zip(names, shape)))

        c = Carve(wbuf, 0, EXPERT)
        wq, wkT, wv, wo = c.take(KC, D), c.take(KC, DC), c.take(CC, D), c.take(KC, D)
        c = Carve(wbuf, EXPERT, 2 * EXPERT)
        swq, swk, swv, swo = c.take(KC, D), c.take(KC, D), c.take(KC, D), c.take(KC, D)
        x1T = shared[:, 0:KC * TOK].rearrange("p (k t) -> p k t", k=KC)
        ctx_n = ctx_region[:, :].rearrange("p (s b c d) -> p s b c d", s=4, b=BT, c=2)
        ctxT = ctxT_region[:, :].rearrange("p (t c b k) -> p t c b k", t=2, c=CC, b=BT)
        qT = actT[:, :].rearrange("p (k t) -> p k t", k=KC)
        c = Carve(misc, 0, 3072)
        qkT = c.take(CC, 2 * P)
        cv = misc[:, 0:2 * DC].rearrange("p (t d) -> p t d", t=2)
        probs = c.take(2, 264)
        pT = c.take(2, 2 * P)
        p_left = c.take(2, P)
        left_T = c.take(CC, B)
        left_n = c.take(DC)
        p_mask = c.take(2, B)
        x2aT = ctxT_region[:, 0:CC * 2 * P].rearrange("p (k t) -> p k t", k=CC)
        avT = qT
        wk = ctx_region[:, 3 * BT * 2 * DC:3 * BT * 2 * DC + CC * D].rearrange("p (k e) -> p k e", k=CC)
        c = Carve(small, 0, 600)
        stats = c.take(2, 6)
        mv = c.take(2, 2)
        ve = c.take(2)
        rstd = c.take(2)
        cx_stats = c.take(2, 8, 6)
        cx_mv = c.take(2, 8, 2)
        cx_ve = c.take(2, 8)
        cx_rstd = c.take(2, 8)
        l_stats, l_mv, l_ve, l_rstd = c.take(6), c.take(2), c.take(1), c.take(1)
        kb = c.take(KC)
        q_bias = c.take(2)
        sc_max, sc_u, sc_nb, sc_sum, sc_rinv = c.take(2), c.take(2), c.take(2), c.take(2), c.take(2)
        s_max, s_sum, s_rinv = c.take(2, HEADS), c.take(2, HEADS), c.take(2, HEADS)
        z = c.take(TILES, E)
        neg_half = c.take(8)
        gates = c.take(2, 4)
        fields = c.take(2, 4)
        c = Carve(ctx_region, 0, 4 * BT * 2 * DC)
        xnT = c.take(KC, 2 * P)
        qb, q_sw, kbuf, k_sw = (c.take(KC * 2 * P) for _ in range(4))
        q_T, k_T = (a.rearrange("p (k t) -> p k t", k=KC) for a in (qb, kbuf))
        k_exp = c.take(KC, 2 * BT, 4, L)
        v = c.take(2, 2, D)
        xfT = c.take(KC, 2 * P)
        c = Carve(ctxT_region, 0, 2 * CC * BT * KEYS)
        p_T = c.take(2, HEADS, P)
        soft = c.take(2, D)
        aoT = actT[:, :].rearrange("p (t c q) -> p t c q", t=2, c=KC)
        c = Carve(misc, 0, 3072)
        ln4_n = c.take(2, D)
        y_out = c.take(2, D)
        xf = shared[:, :].rearrange("p (t r) -> p t r", t=TILES)
        xf16 = shared[:, :].bitcast(F16).rearrange("p (t r) -> p t r", t=TILES)
        c = Carve(ctxT_region, 0, 5600)
        cmp_a, cmp_b = c.take(TILES, E, E), c.take(TILES, E, E)
        rank, sel, sel1, sel2 = c.take(TILES, E), c.take(TILES, E), c.take(TILES, E), c.take(TILES, E)
        sig, picked, base, slot = c.take(TILES, E), c.take(TILES, E), c.take(TILES + 1, E), c.take(TILES, E)
        g1, g2, gsum = c.take(TILES), c.take(TILES), c.take(TILES)
        slot_f = c.take(2, TILES)
        over, ntile, ends, ends_tmp = c.take(E, 8), c.take(E), c.take(E), c.take(E, E)
        emap, emap_cmp, first_of, not_last = c.take(32), c.take(32, E), c.take(32), c.take(32)
        h = c.take(EH)
        h16 = c.take(EH).bitcast(F16).rearrange("p (a h) -> p a h", a=2)
        zrow = ctxT_region[:, 5600:5600 + ROW]
        expert0 = wbuf[:, 0:EXPERT]
        c = Carve(ctx_region, 0, 4 * BT * 2 * DC)
        stage = c.take(EXPERT)
        xg = c.take(ROW_SLOTS, ROW)
        xg16 = xg.rearrange("p s r -> p (s r)").bitcast(F16).rearrange("p (s r) -> p s r", s=ROW_SLOTS)
        xgT = c.take(2, D).rearrange("p s d -> p (s d)").bitcast(F16).rearrange("p (s a d) -> p s a d", s=2, a=2)
        hT = [a[:, :].bitcast(F16).rearrange("p (a d) -> p a d", a=2) for a in (actT, xn[:, :, :].rearrange("p t d -> p (t d)"))]
        w16 = wbuf[:, :].bitcast(F16)
        HIGH, LOW = 0, EXPERT
        slot_i = ints[:, 0:2 * TILES].rearrange("p (a t) -> p a t", a=2)
        map_i = ints[:, 16:16 + 96].rearrange("p (a t) -> p a t", a=3)
        idx = ints[:, 112:114]
        tokens = ints[:, 114:116]

        xg_in = (s["xg_in0"], s["xg_in1"])
        block = ctx.enter_context(nc.Block())


        @block.sync
        def _(sp):
            sp.dma_start(consts[:, :], t_in["consts"]).then_inc(s["const_in"], 16)
            sp.dma_start(x[:, :].rearrange("p (t d) -> p t d", t=TILES),
                         t_in["x"].rearrange("(t p) d -> p t d", p=P)).then_inc(s["x_in"], 16)
            sp.dma_start(cols[:, :], t_in["cols"]).then_inc(s["cols_in"], 16)
            sp.dma_start(left_n[0:B, :], t_in["ctx_768"][:, KEYS - 1, :]).then_inc(s["left_in"], 16)
            sp.dma_start(wk, t_in["wk"].rearrange("(k p) e -> p k e", p=P)).then_inc(s["wk_in"], 16)

            def load_ctx(tile):
                sp.dma_start(
                    ctx_n[:, tile % 4].rearrange("p b c d -> p b (c d)"),
                    t_in["ctx_768"][tile * BT:(tile + 1) * BT, 0:KEYS - 1, :].rearrange("b (p c) d -> p b (c d)", c=2),
                ).then_inc(ctx_in[tile % 4], 16)

            def load_expert(e, dst):
                for n in range(W_PIECES):
                    if e > 1:
                        sp.wait_ge((s["w1_lo"], s["w2_lo"])[n // 2], 2 * (e - 1) + n % 2 + 1)
                    piece = slice(n * PIECE, (n + 1) * PIECE)
                    sp.dma_start(dst[:, piece], t_in["experts"][e][:, piece]).then_inc(s["staged"], 16)
                    sp.wait_ge(s["staged"], 16 * (e * W_PIECES + n + 1))

            def load_w(w, name, sem):
                sp.dma_start(w, t_in[name].rearrange("(k p) e -> p k e", p=P)).then_inc(sem, 16)

            load_ctx(0)
            load_ctx(1)
            load_w(wq, "wq", s["wq_in"])
            load_w(wkT, "wkT", s["wkT_in"])
            sp.dma_start(rows[:, :], t_in["rows"]).then_inc(s["rows_in"], 16)
            load_ctx(2)
            load_w(wv, "wv", s["wv_in"])
            load_w(wo, "wo", s["wo_in"])
            sp.wait_ge(s["kb_ps"], 1)
            load_ctx(3)
            load_w(gate_w[:, :, :], "gate_wT", s["gate_in"])
            sp.dma_start(token_no[:, :], t_in["token_no"]).then_inc(s["ints_in"], 16)
            for w, name, sem in ((swq, "swqT", s["swq_in"]), (swk, "swkT", s["swk_in"]),
                                 (swv, "swvT", s["swv_in"]), (swo, "swoT", s["swo_in"])):
                load_w(w, name, sem)
            for tile in range(4, TILES):
                sp.wait_ge(s["cv_ps"], tile - 3)
                load_ctx(tile)
            sp.wait_ge(s["y_ps"], TILES)
            load_expert(0, expert0)
            sp.wait_ge(s["zrow"], 1)
            sp.dma_start(xs_dram.rearrange("(n p) r -> p n r", p=P),
                         zrow[:, None, :].to_broadcast([P, SLOT_TILES + ROW_SLOTS, ROW])).then_inc(s["xs_zero"], 16)
            sp.dma_start(out[TOK:TOK + P, :], zrow[:, 0:D]).then_inc(s["out_spare"], 16)
            sp.wait_ge(s["z_ps"], TILES)
            for e in range(1, E):
                load_expert(e, stage)
            sp.wait_ge(s["scat"], 16 * SLOT_TILES)
            sp.wait_ge(s["out_init"], 16 * TILES)

        @block.tensor
        def _(pe):
            pe.wait_ge(s["const_in"], 16)

            def transposes(dst, pieces, sem, identity=ident):
                at = 0
                for piece in pieces:
                    n = piece.shape[0]
                    last = nc.tensor.transpose(dst[0:piece.shape[1], at:at + n], piece, identity[0:n, 0:n])
                    at += n
                last.then_inc(sem, 1)

            for tile in range(TILES):
                t = tile % 2
                pe.wait_ge(s["ln2_out"], tile + 1)
                transposes(bank[2 + t], [xn[:, t, k * P:(k + 1) * P] for k in range(KC)], s["x1T_ps"])
                if tile == 1:
                    pe.wait_ge(s["left_n"], 1)
                    transposes(bank[0], [left_n[0:B, k * P:(k + 1) * P] for k in range(CC)], s["left_ps"])
                    pe.wait_ge(s["wk_in"], 16)
                    pe.wait_ge(s["cols_in"], 16)
                    for e in range(KC):
                        for k in range(CC):
                            mm = nc.tensor.matmul(bank[1][:, e:e + 1], wk[:, k, e * P:(e + 1) * P], col("ln2_b", k),
                                                  start=(k == 0), stop=(k == CC - 1))
                    mm.then_inc(s["kb_ps"], 1)

            def ctx_transposes(tile):
                pe.wait_ge(s["cx_n"], tile + 1)
                for n in range(2 * CC):
                    k, half = n // 2, n % 2
                    use = 2 * CC * tile + n
                    if use >= 2:
                        pe.wait_ge(s["cxT"], use - 1)
                    else:
                        pe.wait_ge(s["left_T"] if use == 0 else s["kb"], 1)
                    transposes(bank[use % 2], [ctx_n[:, tile % 4, 2 * half + b, c2, k * P:(k + 1) * P]
                                               for b in range(2) for c2 in range(2)], s["cxT_ps"])

            for pair in range(PAIRS):
                ctx_transposes(2 * pair)
                pe.wait_ge(s["wq_in"], 16)
                pe.wait_ge(s["x1T"], 2 * pair + 2)
                for e in range(KC):
                    for k in range(KC):
                        mm = nc.tensor.matmul(bank[4 + e // 2][:, e % 2 * 256:e % 2 * 256 + 256], wq[:, k, e * P:(e + 1) * P],
                                              x1T[:, k, pair * 256:pair * 256 + 256], start=(k == 0), stop=(k == KC - 1))
                    if e % 2:
                        mm.then_inc(s["q_ps"], 1)
                ctx_transposes(2 * pair + 1)
                pe.wait_ge(s["wkT_in"], 16)
                pe.wait_ge(s["qT"], 2 * pair + 2)
                pe.wait_ge(s["kb"], 1)
                for d in range(CC):
                    for k in range(KC):
                        mm = nc.tensor.matmul(bank[6 + d // 2][:, d % 2 * 256:d % 2 * 256 + 256], wkT[:, k, d * P:(d + 1) * P],
                                              qT[:, k, :], start=(k == 0), stop=(k == KC - 1))
                    if d == 1:
                        mm.then_inc(s["qk_ps"], 1)
                for t in range(2):
                    for k in range(KC):
                        mm = nc.tensor.matmul(bank[7][:, 256 + t:257 + t], qT[:, k, t * P:(t + 1) * P], kb[:, k:k + 1],
                                              start=(k == 0), stop=(k == KC - 1))
                mm.then_inc(s["qk_ps"], 1)
                for t in range(2):
                    tile = 2 * pair + t
                    pe.wait_ge(s["qkT"], pair + 1)
                    pe.wait_ge(s["cxT"], 2 * CC * (tile + 1))
                    pe.wait_ge(s["left_cols"], tile + 1)
                    for k in range(CC):
                        for b in range(BT):
                            mm = nc.tensor.matmul(bank[2 + t][b * L:(b + 1) * L, 0:KEYS],
                                                  qkT[:, k, t * P + b * L:t * P + (b + 1) * L], ctxT[:, t, k, b, :],
                                                  start=(k == 0), stop=(k == CC - 1), tile_position=(0, b * L),
                                                  skip_group_check=True)
                    mm.then_inc(s["sc_ps"], 1)
                for t in range(2):
                    pe.wait_ge(s["sc_pm"], 2 * pair + t + 1)
                    transposes(bank[4 + t], [probs[:, t, 0:P], probs[:, t, P:2 * P], p_mask[:, t, :]], s["pT_ps"])
                for t in range(2):
                    tile = 2 * pair + t
                    pe.wait_ge(s["pT"], 2 * tile + 2)
                    nc.tensor.matmul(bank[6 + t][:, 0:DC], p_left[0:B, t, :], left_n[0:B, :], start=True, stop=False,
                                     skip_group_check=True)
                    for c2 in range(2):
                        for b in range(BT):
                            at = c2 * P + b * L
                            mm = nc.tensor.matmul(bank[6 + t][b * L:(b + 1) * L, 0:DC], pT[:, t, at:at + L],
                                                  ctx_n[:, tile % 4, b, c2, :], start=False, stop=(c2 == 1),
                                                  tile_position=(0, b * L), skip_group_check=True)
                    mm.then_inc(s["cv_ps"], 1)
                for t in range(2):
                    pe.wait_ge(s["cv"], 2 * pair + t + 1)
                    transposes(bank[4 + t], [cv[:, t, k * P:(k + 1) * P] for k in range(CC)], s["cvT_ps"])
                pe.wait_ge(s["wv_in"], 16)
                pe.wait_ge(s["x2aT"], 2 * pair + 2)
                for e in range(KC):
                    for k in range(CC):
                        mm = nc.tensor.matmul(bank[4 + e // 2][:, e % 2 * 256:e % 2 * 256 + 256], wv[:, k, e * P:(e + 1) * P],
                                              x2aT[:, k, :], start=(k == 0), stop=(k == CC - 1))
                    if e % 2:
                        mm.then_inc(s["av_ps"], 1)
                pe.wait_ge(s["wo_in"], 16)
                pe.wait_ge(s["avT"], 2 * pair + 2)
                for t in range(2):
                    for k in range(KC):
                        mm = nc.tensor.matmul(bank[2 + t][:, :], avT[:, k, t * P:(t + 1) * P], wo[:, k, :],
                                              start=(k == 0), stop=(k == KC - 1))
                    mm.then_inc(s["y_ps"], 1)

            pe.wait_ge(s["swq_in"], 16)
            pe.wait_ge(s["swk_in"], 16)
            pe.wait_ge(s["swv_in"], 16)
            pe.wait_ge(s["swo_in"], 16)
            pe.wait_ge(s["gate_in"], 16)
            pe.wait_ge(s["ptx_zero"], 2)
            def normalised_T(pair):
                if pair == 0:
                    pe.wait_ge(s["x_new"], TILES)
                for t in range(2):
                    pe.wait_ge(s["ln3_out"], 2 * pair + t + 1)
                    transposes(bank[t], [xn[:, t, k * P:(k + 1) * P] for k in range(KC)], s["xnT_ps"])

            def by_channel(w, first, sem):
                for e in range(KC):
                    for k in range(KC):
                        mm = nc.tensor.matmul(bank[first + e // 2][:, e % 2 * 256:e % 2 * 256 + 256],
                                              w[:, k, e * P:(e + 1) * P], xnT[:, k, :], start=(k == 0), stop=(k == KC - 1))
                    if e % 2:
                        mm.then_inc(sem, 1)

            def queries(pair):
                pe.wait_ge(s["xnT"], 2 * pair + 2)
                by_channel(swq, 2, s["sq_ps"])

            def keys(pair):
                by_channel(swk, 4, s["sk_ps"])

            def values(pair):
                if pair:
                    pe.wait_ge(s["sv"], 2 * pair)
                for t in range(2):
                    for k in range(KC):
                        mm = nc.tensor.matmul(bank[6 + t][:, :], xnT[:, k, t * P:(t + 1) * P], swv[:, k, :],
                                              start=(k == 0), stop=(k == KC - 1))
                    mm.then_inc(s["sv_ps"], 1)

            def scores(pair):
                pe.wait_ge(s["q_rot"], pair + 1)
                pe.wait_ge(s["k_exp"], pair + 1)
                for t in range(2):
                    for c4 in range(KC):
                        for b in range(BT):
                            mm = nc.tensor.matmul(bank[t][b * L:(b + 1) * L, c4 * P:(c4 + 1) * P],
                                                  q_T[:, c4, t * P + b * L:t * P + (b + 1) * L],
                                                  k_exp[:, c4, t * BT + b, :, :].rearrange("p h l -> p (h l)"),
                                                  start=True, stop=True, tile_position=(0, b * L), skip_group_check=True)
                    mm.then_inc(s["ss_ps"], 1)

            def attend(pair):
                if pair:
                    pe.wait_ge(s["z"], 2 * pair)
                for t in range(2):
                    pe.wait_ge(s["s_pT"], 2 * pair + t + 1)
                    pe.wait_ge(s["sv"], 2 * pair + t + 1)
                    for hd in range(HEADS):
                        at = hd % 4 * HD
                        mm = nc.tensor.matmul(bank[2 + t][at:at + HD, hd // 4 * P:(hd // 4 + 1) * P],
                                              v[:, pair % 2, t, hd * HD:(hd + 1) * HD], p_T[:, t, hd, :],
                                              start=True, stop=True, tile_position=(0, at), skip_group_check=True)
                    mm.then_inc(s["ao_ps"], 1)
                if pair + 1 < PAIRS:
                    pe.wait_ge(s["sk"], 2 * pair + 4)
                for t in range(2):
                    pe.wait_ge(s["aoT"], 2 * pair + t + 1)
                    for k in range(KC):
                        mm = nc.tensor.matmul(bank[4 + t][:, :], aoT[:, t, k, :], swo[:, k, :],
                                              start=(k == 0), stop=(k == KC - 1))
                    mm.then_inc(s["sy_ps"], 1)

            def features_T(pair):
                for t in range(2):
                    pe.wait_ge(s["xf"], 2 * pair + t + 1)
                    transposes(bank[6 + t], [ln4_n[:, t, k * P:(k + 1) * P] for k in range(KC)], s["xfT_ps"])

            def logits(pair):
                if pair + 2 < PAIRS:
                    pe.wait_ge(s["sq"], 2 * pair + 6)
                for t in range(2):
                    pe.wait_ge(s["xfT"], 2 * pair + t + 1)
                    for k in range(KC):
                        mm = nc.tensor.matmul(bank[2 + t][:, 0:E], xfT[:, k, t * P:(t + 1) * P], gate_w[:, k, :],
                                              start=(k == 0), stop=(k == KC - 1))
                    mm.then_inc(s["z_ps"], 1)

            normalised_T(0)
            queries(0)
            keys(0)
            values(0)
            for pair in range(PAIRS):
                if pair + 1 < PAIRS:
                    normalised_T(pair + 1)
                    queries(pair + 1)
                if pair:
                    features_T(pair - 1)
                scores(pair)
                if pair + 1 < PAIRS:
                    keys(pair + 1)
                if pair:
                    logits(pair - 1)
                if pair + 1 < PAIRS:
                    values(pair + 1)
                attend(pair)
            features_T(PAIRS - 1)
            logits(PAIRS - 1)

            pe.wait_ge(s["rt_sel"], 1)
            sel_all = sel.rearrange("p t e -> p (t e)")
            nc.tensor.matmul(bank[0][:, 0:TILES * E], const("before"), sel_all, start=True, stop=True).then_inc(s["rt_cnt_ps"], 1)
            nc.tensor.matmul(bank[1][:, 0:TILES * E], const("ones"), sel_all, start=True, stop=True).then_inc(s["rt_cnt_ps"], 1)

            pe.wait_ge(s["rt_map"], 1)
            pe.wait_ge(s["ident16"], 1)

            def rows_T(b, landed):
                pe.wait_ge(xg_in[b], landed)
                transposes(bank[(4, 7)[b]][:, :].bitcast(F16), [xg16[:, b, k * P:(k + 1) * P] for k in range(2 * KC)],
                           s["xgT_ps"], ident16)

            def expert_of(tile):
                ready = pe.value_load(map_i[0:1, 0, ds(tile, 1)], min_val=1, max_val=E)
                return ready, ready % 2 * (2 * EXPERT)

            def first_product(tile, b, expert):
                ready, at = expert
                pe.wait_ge(s["w1_lo"], ready * 2)
                pe.wait_ge(s["xgT"], tile + 1)
                for half in range(2):
                    for k in range(KC):
                        for x_part, w_part in ((0, HIGH), (1, HIGH), (0, LOW)):
                            mm = nc.tensor.matmul(bank[half][:, :], xgT[:, b, x_part, k * P:(k + 1) * P],
                                                  w16[:, ds(at + (w_part + k * EH + half * 512), 512)],
                                                  start=(k == 0 and x_part + w_part == 0), stop=(k == KC - 1 and w_part == LOW))
                    mm.then_inc(s["h_ps"], 1)

            def hidden_T(tile):
                for part, cut, done in ((0, s["h_hi"], s["hT_ps0"]), (1, s["h_lo"], s["hT_ps1"])):
                    pe.wait_ge(cut, tile + 1)
                    transposes(bank[2 + part][:, :].bitcast(F16), [h16[:, part, k * P:(k + 1) * P] for k in range(HC)], done, ident16)

            def second_product(tile, b, expert):
                ready, at = expert
                pe.wait_ge(s["w2_lo"], ready * 2)
                pe.wait_ge(s["hT0"], tile + 1)
                pe.wait_ge(s["hT1"], tile + 1)
                for k in range(HC):
                    for h_part, w_part in ((0, HIGH), (0, LOW), (1, HIGH)):
                        mm = nc.tensor.matmul(bank[5 + b][:, :], hT[b][:, h_part, k * P:(k + 1) * P],
                                              w16[:, ds(at + (w_part + W2_AT + k * D), D)],
                                              start=(k == 0 and h_part + w_part == 0), stop=(k == HC - 1 and h_part == 1))
                mm.then_inc(s["y2_ps"], 1)

            rows_T(0, 16)
            first_product(0, 0, expert_of(0))
            rows_T(1, 16)
            hidden_T(0)
            with pe.Fori(0, (SLOT_TILES - 1) // 2) as i:
                expert = expert_of(i * 2)
                for u in (1, 2):
                    before, expert = expert, expert_of(i * 2 + u)
                    first_product(i * 2 + u, u % 2, expert)
                    rows_T((u + 1) % 2, i * 16 + 32)
                    second_product(i * 2 + (u - 1), (u - 1) % 2, before)
                    hidden_T(i * 2 + u)
            second_product(SLOT_TILES - 1, (SLOT_TILES - 1) % 2, expert_of(SLOT_TILES - 1))

        @block.scalar
        def _(act):
            act.wait_ge(s["cols_in"], 16)

            def ctx_copies(tile):
                for n in range(2 * CC):
                    k, half = n // 2, n % 2
                    use = 2 * CC * tile + n
                    act.wait_ge(s["cxT_ps"], use + 1)
                    nc.scalar.copy(ctxT[:, tile % 2, k, 2 * half:2 * half + 2, 0:KEYS - 1],
                                   bank[use % 2][:, :].rearrange("p (b k) -> p b k", b=2)).then_inc(s["cxT"], 1)

            def biased(dst, first, ps_sem, count, bias, sem):
                for n in range(2):
                    act.wait_ge(ps_sem, count + n + 1)
                    for i in range(2):
                        e = 2 * n + i
                        op = nc.scalar.activation(dst[:, e, :], bank[first + n][:, i * 256:i * 256 + 256], ACT.Identity,
                                                  bias=col(bias, e))
                    op.then_inc(sem, 1)

            for pair in range(PAIRS):
                ctx_copies(2 * pair)
                biased(qT, 4, s["q_ps"], 2 * pair, "bq", s["qT"])
                ctx_copies(2 * pair + 1)
                for t in range(2):
                    act.wait_ge(s["sc_nb"], 2 * pair + t + 1)
                    nc.scalar.activation(probs[:, t, 0:KEYS], bank[2 + t][:, 0:KEYS], ACT.Exp, bias=sc_nb[:, t:t + 1],
                                         scale=X_SCALE, accum_out=sc_sum[:, t:t + 1]).then_inc(s["sc_exp"], 1)
                for t in range(2):
                    act.wait_ge(s["pT_ps"], 2 * pair + t + 1)
                    nc.scalar.copy(pT[:, t, :], bank[4 + t][:, 0:2 * P]).then_inc(s["pT"], 1)
                    nc.scalar.copy(p_left[0:B, t, :], bank[4 + t][0:B, 2 * P:3 * P]).then_inc(s["pT"], 1)
                for t in range(2):
                    act.wait_ge(s["cv_ps"], 2 * pair + t + 1)
                    act.wait_ge(s["sc_rinv"], 2 * pair + t + 1)
                    nc.scalar.activation(cv[:, t, :], bank[6 + t][:, 0:DC], ACT.Copy, scale=sc_rinv[:, t:t + 1]).then_inc(s["cv"], 1)
                biased(avT, 4, s["av_ps"], 2 * pair, "bv", s["avT"])

            def normalised_out(pair):
                for t in range(2):
                    act.wait_ge(s["xnT_ps"], 2 * pair + t + 1)
                    nc.scalar.copy(xnT[:, :, t * P:(t + 1) * P],
                                   bank[t][:, :].rearrange("p (k t) -> p k t", k=KC)).then_inc(s["xnT"], 1)

            def queries_out(pair):
                if pair:
                    act.wait_ge(s["ss_ps"], 2 * pair)
                biased(q_T, 2, s["sq_ps"], 2 * pair, "sbq", s["sq"])

            def features_out(pair):
                for t in range(2):
                    act.wait_ge(s["xfT_ps"], 2 * pair + t + 1)
                    nc.scalar.copy(xfT[:, :, t * P:(t + 1) * P],
                                   bank[6 + t][:, :].rearrange("p (k t) -> p k t", k=KC)).then_inc(s["xfT"], 1)
                for t in range(2):
                    tile = 2 * pair + t
                    nc.scalar.copy(xf16[:, tile, 0:D], ln4_n[:, t, :]).then_inc(s["xf_hi"], 1)
                    act.wait_ge(s["x_post"], tile + 1)
                    act.dma_start(out[tile * P:(tile + 1) * P, :], x[:, tile * D:(tile + 1) * D]).then_inc(s["out_init"], 16)

            normalised_out(0)
            queries_out(0)
            biased(k_T, 4, s["sk_ps"], 0, "sbk", s["sk"])
            for pair in range(PAIRS):
                if pair + 1 < PAIRS:
                    normalised_out(pair + 1)
                if pair:
                    features_out(pair - 1)
                if pair + 1 < PAIRS:
                    queries_out(pair + 1)
                for t in range(2):
                    act.wait_ge(s["s_sub"], 2 * pair + t + 1)
                    nc.scalar.activation(soft[:, t, :], soft[:, t, :], ACT.Exp, scale=H_SCALE).then_inc(s["s_exp"], 1)
                if pair + 1 < PAIRS:
                    biased(k_T, 4, s["sk_ps"], 2 * pair + 2, "sbk", s["sk"])
                for t in range(2):
                    act.wait_ge(s["ao_ps"], 2 * pair + t + 1)
                    nc.scalar.copy(aoT[:, t, :, :].rearrange("p c q -> p (c q)"), bank[2 + t][:, :]).then_inc(s["aoT"], 1)
            features_out(PAIRS - 1)
            act.wait_ge(s["z"], TILES)
            nc.scalar.activation(sig, z, ACT.Exp, scale=-1.0).then_inc(s["rt_exp"], 1)

            def cut_high(src_, at, pieces, before):
                for n in pieces:
                    act.wait_ge(s["staged"], before + 16 * (n + 1))
                    nc.scalar.activation(w16[:, ds(at + (HIGH + n * PIECE), PIECE)], src_[:, n * PIECE:(n + 1) * PIECE],
                                         ACT.Copy, scale=W_SCALE).then_inc(s["w_hi"], 1)

            def load_rows(tile, b):
                act.dma_start(xg[:, b, :], xs_dram[ds(tile * P, P), :]).then_inc(xg_in[b], 16)

            def cut_next_high(tile, pieces):
                new = act.value_load(map_i[0:1, 2, ds(tile, 1)], min_val=0, max_val=1)
                with act.If(new == 1):
                    ready = act.value_load(map_i[0:1, 0, ds(tile, 1)], min_val=1, max_val=E)
                    at = act.value_load(map_i[0:1, 1, ds(tile, 1)], min_val=0, max_val=2 * EXPERT)
                    act.wait_ge(s["y2_ps"], tile)
                    cut_high(stage, at * -1 + 2 * EXPERT, pieces, ready * (16 * W_PIECES))

            def gated(tile, b):
                act.wait_ge(s["gate"], tile + 1)
                act.wait_ge(s["added"], tile + 1)
                act.wait_ge(s["y2_ps"], tile + 1)
                nc.scalar.activation(y_out[:, b, :], bank[5 + b][:, :], ACT.Copy, scale=gates[:, b, 2:3]).then_inc(s["y2"], 1)

            def hidden(tile, b):
                act.wait_ge(s["fields"], tile * 2 + 2)
                load_rows(tile + 2, b)
                for half in range(2):
                    act.wait_ge(s["h_ps"], tile * 2 + (half + 1))
                    nc.scalar.activation(h[:, half * 512:half * 512 + 512], bank[half][:, :], ACT.Silu,
                                         scale=1.0 / W_SCALE).then_inc(s["h"], 1)

            def hidden_copy(tile, b):
                act.wait_ge(s["hT_ps0"], tile + 1)
                nc.scalar.copy(hT[b][:, 0, :], bank[2][:, :].bitcast(F16)).then_inc(s["hT0"], 1)

            act.wait_ge(s["sy_ps"], TILES)
            cut_high(expert0, 2 * EXPERT, range(4), 0)
            act.wait_ge(s["rt_map"], 1)
            act.wait_ge(s["scattered"], 16 * 2 * TILES)
            load_rows(0, 0)
            load_rows(1, 1)
            hidden(0, 0)
            hidden_copy(0, 0)
            act.wait_ge(s["w2_lo"], 2)
            cut_high(stage, 0, (0, 1), 16 * W_PIECES)
            with act.Fori(0, (SLOT_TILES - 1) // 2) as i:
                for u in (1, 2):
                    hidden(i * 2 + u, u % 2)
                    cut_next_high(i * 2 + (u - 1), (2, 3))
                    hidden_copy(i * 2 + u, u % 2)
                    gated(i * 2 + (u - 1), (u - 1) % 2)
                    cut_next_high(i * 2 + u, (0, 1))
            gated(SLOT_TILES - 1, (SLOT_TILES - 1) % 2)
            for tile in (SLOT_TILES, SLOT_TILES + 1):
                act.wait_ge(xg_in[tile % 2], 16 * (tile // 2 + 1))

        @block.vector
        def _(dve):
            norms = [0]

            def norm_stats(srcs, stats_, mv_, ve_, ve_sem):
                for i, src in enumerate(srcs):
                    nc.vector.bn_stats(stats_[:, i, :], src).then_inc(s["norm_stats"], 1)
                norms[0] += len(srcs)
                dve.wait_ge(s["norm_stats"], norms[0])
                for i in range(len(srcs)):
                    nc.vector.bn_aggr(mv_[:, i, :], stats_[:, i, :]).then_inc(s["norm_mv"], 1)
                dve.wait_ge(s["norm_mv"], norms[0])
                nc.vector.tensor_scalar(ve_, mv_[:, :, 1], EPS, None, ALU.add).then_inc(ve_sem, 1)

            def normalise(dst, src, mean, inverse):
                return nc.vector.tensor_scalar(dst, src, mean, inverse, ALU.subtract, ALU.mult)

            def x_at(tile):
                return x[:, tile * D:(tile + 1) * D]

            def norm_pair(srcs, dsts, name, pair):
                norm_stats(srcs, stats, mv, ve, s[f"{name}_ve"])
                dve.wait_ge(s[f"{name}_rstd"], pair + 1)
                out_sem = s[f"{name}_out"]
                for t in range(2):
                    normalise(dsts[t], srcs[t], mv[:, t, 0:1], rstd[:, t:t + 1]).then_inc(out_sem, 1)
                dve.wait_ge(out_sem, 2 * pair + 2)

            nc.vector.memset(neg_half, -0.5).then_inc(s["route"], 1)
            dve.wait_ge(s["const_in"], 16)
            nc.vector.tensor_copy(ident16[:, :], ident).then_inc(s["ident16"], 1)
            dve.wait_ge(s["x_in"], 16)
            dve.wait_ge(s["cols_in"], 16)

            def left_norm():
                dve.wait_ge(s["left_in"], 16)
                norm_stats([left_n[0:B, :]], l_stats[0:B, None, :], l_mv[0:B, None, :], l_ve[0:B, :],
                           s["left_ve"])
                dve.wait_ge(s["left_rstd"], 1)
                normalise(left_n[0:B, :], left_n[0:B, :], l_mv[0:B, 0:1], l_rstd[0:B, :]).then_inc(s["left_n"], 1)

            def ctx_norm(tile):
                u, part = tile % 2, ctx_n[:, tile % 4]
                dve.wait_ge(ctx_in[tile % 4], 16 * (tile // 4 + 1))
                pieces = [part[:, b, c2, :] for b in range(BT) for c2 in range(2)]
                norm_stats(pieces, cx_stats[:, u], cx_mv[:, u], cx_ve[:, u], s["cx_ve"])
                dve.wait_ge(s["cx_rstd"], tile + 1)
                for i, piece in enumerate(pieces):
                    op = normalise(piece, piece, cx_mv[:, u, i, 0:1], cx_rstd[:, u, i:i + 1])
                op.then_inc(s["cx_n"], 1)

            for pair in range(PAIRS):
                tiles = [x_at(2 * pair), x_at(2 * pair + 1)]
                norm_pair(tiles, [xn[:, 0, :], xn[:, 1, :]], "ln1", pair)
                norm_pair([xn[:, 0, :], xn[:, 1, :]], [xn[:, 0, :], xn[:, 1, :]], "ln2", pair)
                if pair == 0:
                    left_norm()
                for t in range(2):
                    tile = 2 * pair + t
                    dve.wait_ge(s["x1T_ps"], tile + 1)
                    for k in range(KC):
                        op = nc.vector.tensor_scalar(x1T[:, k, tile * P:(tile + 1) * P], bank[2 + t][:, k * P:(k + 1) * P],
                                                     col("ln1_g", k), col("ln1_b", k), ALU.mult, ALU.add)
                    op.then_inc(s["x1T"], 1)
                if pair == 0:
                    dve.wait_ge(s["left_ps"], 1)
                    nc.vector.tensor_copy(left_T, bank[0][:, 0:CC * B].rearrange("p (c b) -> p c b", c=CC)).then_inc(s["left_T"], 1)
                    dve.wait_ge(s["kb_ps"], 1)
                    nc.vector.tensor_tensor(kb, bank[1][:, 0:KC], cols[:, COLS["bk"]], ALU.add).then_inc(s["kb"], 1)
                    dve.wait_ge(s["left_T"], 1)
                    ctx_norm(0)
                    ctx_norm(1)

            for pair in range(PAIRS):
                for t in range(2):
                    tile = 2 * pair + t
                    nc.vector.tensor_copy(ctxT[:, t, :, :, KEYS - 1], left_T[:, :, tile * BT:(tile + 1) * BT]).then_inc(s["left_cols"], 1)
                if pair + 1 < PAIRS:
                    ctx_norm(2 * pair + 2)
                    ctx_norm(2 * pair + 3)
                for k in range(CC):
                    if k != 1:
                        dve.wait_ge(s["qk_ps"], 2 * pair + k // 2 + 1)
                    op = nc.vector.tensor_scalar(qkT[:, k, :], bank[6 + k // 2][:, k % 2 * 256:k % 2 * 256 + 256],
                                                 col("ln2_g", k), None, ALU.mult)
                op.then_inc(s["qkT"], 1)
                nc.vector.tensor_copy(q_bias, bank[7][:, 256:258]).then_inc(s["q_bias"], 1)
                dve.wait_ge(s["q_bias"], pair + 1)
                for t in range(2):
                    tile = 2 * pair + t
                    one = slice(t, t + 1)
                    dve.wait_ge(s["sc_ps"], tile + 1)
                    nc.vector.tensor_reduce(sc_max[:, one], bank[2 + t][:, 0:KEYS], AX.X, ALU.max).then_inc(s["sc_max"], 1)
                    dve.wait_ge(s["sc_max"], tile + 1)
                    nc.vector.tensor_tensor(sc_u[:, one], sc_max[:, one], q_bias[:, one], ALU.add).then_inc(s["sc_u"], 1)
                    dve.wait_ge(s["sc_u"], tile + 1)
                    nc.vector.tensor_scalar(sc_nb[:, one], q_bias[:, one], sc_u[:, one], X_SCALE, ALU.subtract, ALU.mult)\
                        .then_inc(s["sc_nb"], 1)
                for t in range(2):
                    tile = 2 * pair + t
                    dve.wait_ge(s["sc_exp"], tile + 1)
                    at = CONST["left_mask"].start + 28 - BT * tile
                    nc.vector.tensor_scalar(p_mask[:, t, :], consts[:, at:at + B], probs[:, t, KEYS - 1:KEYS], None, ALU.mult)\
                        .then_inc(s["sc_pm"], 1)
                    nc.vector.reciprocal(sc_rinv[:, t:t + 1], sc_sum[:, t:t + 1]).then_inc(s["sc_rinv"], 1)
                for t in range(2):
                    tile = 2 * pair + t
                    dve.wait_ge(s["cvT_ps"], tile + 1)
                    for k in range(CC):
                        op = nc.vector.tensor_scalar(x2aT[:, k, t * P:(t + 1) * P], bank[4 + t][:, k * P:(k + 1) * P],
                                                     col("ln2_g", k), col("ln2_b", k), ALU.mult, ALU.add)
                    op.then_inc(s["x2aT"], 1)
                for t in range(2):
                    tile = 2 * pair + t
                    dve.wait_ge(s["y_ps"], tile + 1)
                    dve.wait_ge(s["x_plus_bo"], tile + 1)
                    nc.vector.tensor_tensor(x_at(tile), bank[2 + t][:, :], x_at(tile), ALU.add).then_inc(s["x_new"], 1)

            swap = [(i + HD // 2) % HD for i in range(HD)]

            def by_place(a):
                return a.rearrange("p (n l) -> p n l", l=L)

            table = [P, KC * 2 * BT, L]
            sin_t = const("sin")[:, None, :].to_broadcast(table)

            def first_norm(pair):
                dve.wait_ge(s["x_new"], 2 * pair + 2)
                norm_pair([x_at(2 * pair), x_at(2 * pair + 1)], [xn[:, 0, :], xn[:, 1, :]], "ln3", pair)

            def rotate(pair):
                for src, sw, name in ((qb, q_sw, "q"), (kbuf, k_sw, "k")):
                    dve.wait_ge(s[f"s{name}"], 2 * pair + 2)
                    nc.vector.stream_shuffle(sw, src, swap).then_inc(s[f"{name}_swap"], 1)
                    dve.wait_ge(s[f"{name}_swap"], pair + 1)
                    nc.vector.tensor_tensor(by_place(sw), by_place(sw), sin_t, ALU.mult).then_inc(s[f"{name}_sin"], 1)
                    dve.wait_ge(s[f"{name}_sin"], pair + 1)
                    dve.wait_ge(s[f"{name}_cos"], pair + 1)
                    if name == "q":
                        nc.vector.tensor_tensor(src, src, sw, ALU.add).then_inc(s["q_rot"], 1)
                        continue
                    for r in range(4):
                        part = slice(r * HD, (r + 1) * HD)
                        op = nc.vector.tensor_tensor(k_exp[part, :, :, r, :],
                                                     src[part].rearrange("p (c b l) -> p c b l", c=KC, l=L),
                                                     sw[part].rearrange("p (c b l) -> p c b l", c=KC, l=L), ALU.add)
                    op.then_inc(s["k_exp"], 1)

            def values_out(pair):
                for t in range(2):
                    dve.wait_ge(s["sv_ps"], 2 * pair + t + 1)
                    nc.vector.tensor_tensor(v[:, pair % 2, t, :], bank[6 + t][:, :], row("sbv"), ALU.add).then_inc(s["sv"], 1)

            by_head = [P, HEADS, L]

            def softmax(pair):
                for t in range(2):
                    tile = 2 * pair + t
                    dve.wait_ge(s["ss_ps"], tile + 1)
                    scores = bank[t][:, :].rearrange("p (h l) -> p h l", l=L)
                    nc.vector.tensor_reduce(s_max[:, t, :], scores, AX.X, ALU.max).then_inc(s["s_max"], 1)
                    dve.wait_ge(s["s_max"], tile + 1)
                    nc.vector.tensor_tensor(by_place(soft[:, t, :]), scores, s_max[:, t, :, None].to_broadcast(by_head),
                                            ALU.subtract).then_inc(s["s_sub"], 1)
                for t in range(2):
                    tile = 2 * pair + t
                    dve.wait_ge(s["s_exp"], tile + 1)
                    nc.vector.tensor_reduce(s_sum[:, t, :], by_place(soft[:, t, :]), AX.X, ALU.add).then_inc(s["s_sum"], 1)
                    dve.wait_ge(s["s_sum"], tile + 1)
                    nc.vector.reciprocal(s_rinv[:, t, :], s_sum[:, t, :]).then_inc(s["s_rinv"], 1)
                    dve.wait_ge(s["s_rinv"], tile + 1)
                    nc.vector.tensor_tensor(by_place(soft[:, t, :]), by_place(soft[:, t, :]),
                                            s_rinv[:, t, :, None].to_broadcast(by_head), ALU.mult).then_inc(s["s_norm"], 1)
                    dve.wait_ge(s["s_norm"], tile + 1)
                    for b in range(BT):
                        part = slice(b * L, (b + 1) * L)
                        op = nc.vector.transpose(p_T[part, t, :, b * L:(b + 1) * L], by_place(soft[part, t, :]))
                    op.then_inc(s["s_pT"], 1)

            def last_norm(pair):
                for t in range(2):
                    tile = 2 * pair + t
                    dve.wait_ge(s["sy_ps"], tile + 1)
                    dve.wait_ge(s["x_plus_sbo"], tile + 1)
                    nc.vector.tensor_tensor(x_at(tile), bank[4 + t][:, :], x_at(tile), ALU.add).then_inc(s["x_post"], 1)
                dve.wait_ge(s["x_post"], 2 * pair + 2)
                norm_stats([x_at(2 * pair), x_at(2 * pair + 1)], stats, mv, ve, s["ln4_ve"])
                dve.wait_ge(s["ln4_rstd"], pair + 1)
                if pair:
                    dve.wait_ge(s["xf_lo"], 2 * pair)
                for t in range(2):
                    normalise(ln4_n[:, t, :], x_at(2 * pair + t), mv[:, t, 0:1], rstd[:, t:t + 1]).then_inc(s["xf"], 1)

            def logits_out(pair):
                for t in range(2):
                    tile = 2 * pair + t
                    dve.wait_ge(s["z_ps"], tile + 1)
                    nc.vector.tensor_tensor(z[:, tile, :], bank[2 + t][:, 0:E], row("balance"), ALU.add).then_inc(s["z"], 1)

            first_norm(0)
            dve.wait_ge(s["ptx_zero"], 2)
            rotate(0)
            first_norm(1)
            values_out(0)
            for pair in range(PAIRS):
                softmax(pair)
                if pair:
                    logits_out(pair - 1)
                if pair + 1 < PAIRS:
                    rotate(pair + 1)
                if pair + 2 < PAIRS:
                    first_norm(pair + 2)
                if pair + 1 < PAIRS:
                    values_out(pair + 1)
                last_norm(pair)
            logits_out(PAIRS - 1)

            steps = [1]

            def then(op):
                op.then_inc(s["route"], 1)
                steps[0] += 1
                dve.wait_ge(s["route"], steps[0])

            tt, ts = nc.vector.tensor_tensor, nc.vector.tensor_scalar
            dve.wait_ge(s["z"], TILES)
            full = [P, TILES, E, E]
            then(tt(cmp_a, z[:, :, None, :].to_broadcast(full), z[:, :, :, None].to_broadcast(full), ALU.is_gt))
            then(tt(cmp_b, z[:, :, None, :].to_broadcast(full), z[:, :, :, None].to_broadcast(full), ALU.is_equal))
            low = const("low")
            then(tt(cmp_b.rearrange("p t a b -> p t (a b)"), cmp_b.rearrange("p t a b -> p t (a b)"),
                    low[:, None, :].to_broadcast([P, TILES, E * E]), ALU.mult))
            then(tt(cmp_a, cmp_a, cmp_b, ALU.add))
            then(nc.vector.tensor_reduce(rank, cmp_a, AX.X, ALU.add))
            ts(sel, rank, 2.0, None, ALU.is_lt).then_inc(s["rt_sel"], 1)
            then(ts(sel1, rank, 0.0, None, ALU.is_equal))
            then(ts(sel2, rank, 1.0, None, ALU.is_equal))
            dve.wait_ge(s["rt_exp"], 1)
            then(ts(sig, sig, 1.0, None, ALU.add))
            then(nc.vector.reciprocal(sig, sig))
            for g, chosen in ((g1, sel1), (g2, sel2)):
                then(tt(picked, sig, chosen, ALU.mult))
                then(nc.vector.tensor_reduce(g, picked, AX.X, ALU.add))
            then(tt(gsum, g1, g2, ALU.add))
            then(ts(gsum, gsum, 1e-6, W_SCALE, ALU.add, ALU.mult))
            then(nc.vector.reciprocal(gsum, gsum))
            for g, chosen, g_col, e_col in ((g1, sel1, C_G1, C_E1), (g2, sel2, C_G2, C_E2)):
                then(tt(xf[:, :, g_col], g, gsum, ALU.mult))
                then(tt(picked, chosen, const("tile_no")[:, None, 0:E].to_broadcast([P, TILES, E]), ALU.mult))
                then(nc.vector.tensor_reduce(xf[:, :, e_col], picked, AX.X, ALU.add))
            dve.wait_ge(s["ints_in"], 16)
            then(nc.vector.tensor_copy(xf[:, :, C_TOKEN].bitcast(I32), token_no[:, 0:TILES]))
            then(nc.vector.memset(base[:, 0, :], 0.0))
            dve.wait_ge(s["rt_cnt_ps"], 2)
            for tile in range(TILES):
                then(tt(base[:, tile + 1, :], bank[1][:, tile * E:(tile + 1) * E], base[:, tile, :], ALU.add))
            then(tt(over, base[:, TILES, :, None].to_broadcast([P, E, 8]), const("steps")[:, None, :].to_broadcast([P, E, 8]),
                    ALU.is_gt))
            then(nc.vector.tensor_reduce(ntile, over, AX.X, ALU.add))
            then(ts(ntile, ntile, 1.0, None, ALU.add))
            then(tt(ends_tmp, ntile[:, None, :].to_broadcast([P, E, E]), low.rearrange("p (a b) -> p a b", a=E), ALU.mult))
            then(nc.vector.tensor_reduce(ends, ends_tmp, AX.X, ALU.add))
            then(tt(slot, bank[0][:, 0:TILES * E].rearrange("p (t e) -> p t e", t=TILES), base[:, 0:TILES, :], ALU.add))
            then(ts(ends_tmp[:, 0, :], ends, float(P), None, ALU.mult))
            then(tt(slot, slot, ends_tmp[:, 0, None, :].to_broadcast([P, TILES, E]), ALU.add))
            for n, chosen in enumerate((sel1, sel2)):
                then(tt(picked, slot, chosen, ALU.mult))
                then(nc.vector.tensor_reduce(slot_f[:, n, :], picked, AX.X, ALU.add))
            nc.vector.tensor_copy(slot_i, slot_f).then_inc(s["rt_slots"], 1)
            then(tt(ends, ends, ntile, ALU.add))
            by_tile = [P, 32, E]
            then(tt(emap_cmp, ends[:, None, :].to_broadcast(by_tile), const("tile_no")[:, :, None].to_broadcast(by_tile), ALU.is_le))
            then(nc.vector.tensor_reduce(emap, emap_cmp, AX.X, ALU.add))
            then(ts(emap, emap, float(E - 1), None, ALU.min))
            then(ts(map_i[:, 0, :], emap, 1.0, None, ALU.add))
            then(ts(map_i[:, 1, :], map_i[:, 0, :], 1, int(np.log2(2 * EXPERT)), ALU.bitwise_and, ALU.logical_shift_left))
            then(tt(first_of[:, 1:32], emap[:, 1:32], emap[:, 0:31], ALU.is_gt))
            then(nc.vector.memset(first_of[:, 0:1], 1.0))
            then(ts(not_last, emap, E - 1.5, None, ALU.is_lt))
            tt(map_i[:, 2, :], first_of, not_last, ALU.mult).then_inc(s["rt_map"], 1)

            def cut_low(src_, at, pieces, before):
                for n in pieces:
                    dve.wait_ge(s["w_hi"], before + (n + 1))
                    piece = slice(n * PIECE, (n + 1) * PIECE)
                    nc.vector.scalar_tensor_tensor(w16[:, ds(at + (LOW + n * PIECE), PIECE)], src_[:, piece], W_SCALE,
                                                   w16[:, ds(at + (HIGH + n * PIECE), PIECE)], ALU.mult, ALU.subtract)\
                        .then_inc((s["w1_lo"], s["w2_lo"])[n // 2], 1)

            def cut_next_low(tile, pieces):
                new = dve.value_load(map_i[0:1, 2, ds(tile, 1)], min_val=0, max_val=1)
                with dve.If(new == 1):
                    ready = dve.value_load(map_i[0:1, 0, ds(tile, 1)], min_val=1, max_val=E)
                    at = dve.value_load(map_i[0:1, 1, ds(tile, 1)], min_val=0, max_val=2 * EXPERT)
                    cut_low(stage, at * -1 + 2 * EXPERT, pieces, ready * W_PIECES)

            def rows_copy(tile, b, again=True):
                if again:
                    dve.wait_ge(s["idx"], tile - 1)
                dve.wait_ge(s["xgT_ps"], tile + 1)
                nc.vector.tensor_copy(tokens[:, b:b + 1], xg[:, b, C_TOKEN:C_TOKEN + 1].bitcast(I32)).then_inc(s["fields"], 1)
                nc.vector.tensor_copy(fields[:, b, :], xg[:, b, C_G1:C_E2 + 1]).then_inc(s["fields"], 1)
                nc.vector.tensor_copy(xgT[:, b].rearrange("p a d -> p (a d)"), bank[(4, 7)[b]][:, :].bitcast(F16)).then_inc(s["xgT"], 1)

            def cut_hidden(tile):
                dve.wait_ge(s["h"], tile * 2 + 2)
                nc.vector.tensor_copy(h16[:, 0, :], h).then_inc(s["h_hi"], 1)
                dve.wait_ge(s["h_hi"], tile + 1)
                tt(h16[:, 1, :], h, h16[:, 0, :], ALU.subtract).then_inc(s["h_lo"], 1)

            def hidden_copy(tile, b):
                dve.wait_ge(s["hT_ps1"], tile + 1)
                nc.vector.tensor_copy(hT[b][:, 1, :], bank[3][:, :].bitcast(F16)).then_inc(s["hT1"], 1)

            def gate_of(tile, b):
                expert = emap[:, ds(tile, 1)]
                field = {at: fields[:, b, at - C_G1:at - C_G1 + 1] for at in (C_G1, C_E1, C_G2, C_E2)}
                dve.wait_ge(s["fields"], tile * 2 + 2)
                for n, (g_col, e_col) in enumerate(((C_G1, C_E1), (C_G2, C_E2))):
                    op = ts(gates[:, b, n:n + 1], field[e_col], expert, field[g_col], ALU.is_equal, ALU.mult)
                op.then_inc(s["gate_parts"], 1)
                dve.wait_ge(s["gate_parts"], tile + 1)
                tt(gates[:, b, 2:3], gates[:, b, 0:1], gates[:, b, 1:2], ALU.add).then_inc(s["gate"], 1)
                dve.wait_ge(s["added"], tile + 1)
                nc.vector.tensor_copy(idx[:, b:b + 1], tokens[:, b:b + 1]).then_inc(s["idx"], 1)

            cut_low(expert0, 2 * EXPERT, range(4), 0)
            rows_copy(0, 0, again=False)
            rows_copy(1, 1, again=False)
            cut_hidden(0)
            hidden_copy(0, 0)
            cut_low(stage, 0, (0, 1), W_PIECES)
            gate_of(0, 0)
            with dve.Fori(0, (SLOT_TILES - 1) // 2) as i:
                for u in (1, 2):
                    rows_copy(i * 2 + (u + 1), (u + 1) % 2)
                    cut_hidden(i * 2 + u)
                    cut_next_low(i * 2 + (u - 1), (2, 3))
                    hidden_copy(i * 2 + u, u % 2)
                    cut_next_low(i * 2 + u, (0, 1))
                    gate_of(i * 2 + u, u % 2)

        @block.gpsimd
        def _(pool):
            def inverse_root(name, count, out_, in_, n, parts=P):
                pool.wait_ge(s[f"{name}_ve"], count)
                nc.gpsimd.tensor_tensor(out_, in_, neg_half[0:parts, 0:n], ALU.pow).then_inc(s[f"{name}_rstd"], 1)

            def x_at(tile):
                return x[:, tile * D:(tile + 1) * D]

            def ctx_root(tile):
                inverse_root("cx", tile + 1, cx_rstd[:, tile % 2], cx_ve[:, tile % 2], 8)

            pool.wait_ge(s["route"], 1)
            for pair in range(PAIRS):
                inverse_root("ln1", pair + 1, rstd, ve, 2)
                inverse_root("ln2", pair + 1, rstd, ve, 2)
                if pair == 0:
                    inverse_root("left", 1, l_rstd[0:B, :], l_ve[0:B, :], 1, B)
                    ctx_root(0)
                    ctx_root(1)
            pool.wait_ge(s["rows_in"], 16)
            for tile in range(TILES):
                nc.gpsimd.tensor_tensor(x_at(tile), x_at(tile), row("bo"), ALU.add).then_inc(s["x_plus_bo"], 1)
            for tile in range(2, TILES):
                ctx_root(tile)
            inverse_root("ln3", 1, rstd, ve, 2)
            pool.wait_ge(s["y_ps"], TILES)
            nc.gpsimd.memset(k_exp, 0.0).then_inc(s["ptx_zero"], 1)
            nc.gpsimd.memset(p_T, 0.0).then_inc(s["ptx_zero"], 1)
            pool.wait_ge(s["ints_in"], 16)
            nc.gpsimd.memset(zrow, 0.0).then_inc(s["zrow_fill"], 1)
            pool.wait_ge(s["zrow_fill"], 1)
            nc.gpsimd.tensor_copy(zrow[:, C_TOKEN:C_TOKEN + 1].bitcast(I32), token_no[:, TILES:TILES + 1]).then_inc(s["zrow"], 1)
            nc.gpsimd.memset(xf[:, :, C_E2 + 1:ROW], 0.0).then_inc(s["rows_set"], 1)
            table = [P, KC * 2 * BT, L]
            cos_t = const("cos")[:, None, :].to_broadcast(table)

            def cosines(pair):
                for buf, name in ((qb, "q"), (kbuf, "k")):
                    pool.wait_ge(s[f"{name}_swap"], pair + 1)
                    by_place = buf.rearrange("p (n l) -> p n l", l=L)
                    nc.gpsimd.tensor_tensor(by_place, by_place, cos_t, ALU.mult).then_inc(s[f"{name}_cos"], 1)

            def plus_sbo(pair):
                for t in range(2):
                    tile = 2 * pair + t
                    pool.wait_ge(s["ln3_out"], tile + 1)
                    nc.gpsimd.tensor_tensor(x_at(tile), x_at(tile), row("sbo"), ALU.add).then_inc(s["x_plus_sbo"], 1)

            def features_low(pair):
                for t in range(2):
                    tile = 2 * pair + t
                    pool.wait_ge(s["xf_hi"], tile + 1)
                    nc.gpsimd.tensor_tensor(xf16[:, tile, D:2 * D], ln4_n[:, t, :], xf16[:, tile, 0:D], ALU.subtract)\
                        .then_inc(s["xf_lo"], 1)

            cosines(0)
            inverse_root("ln3", 2, rstd, ve, 2)
            plus_sbo(0)
            plus_sbo(1)
            for pair in range(PAIRS):
                if pair:
                    features_low(pair - 1)
                if pair + 1 < PAIRS:
                    cosines(pair + 1)
                if pair + 2 < PAIRS:
                    inverse_root("ln3", pair + 3, rstd, ve, 2)
                inverse_root("ln4", pair + 1, rstd, ve, 2)
                if pair + 2 < PAIRS:
                    plus_sbo(pair + 2)
            features_low(PAIRS - 1)
            pool.wait_ge(s["xs_zero"], 16)
            pool.wait_ge(s["xf_lo"], TILES)
            pool.wait_ge(s["rt_slots"], 1)
            pool.wait_ge(s["rows_set"], 1)
            for tile in range(TILES):
                for n in range(2):
                    nc.gpsimd.indirect_dma_start(
                        xs_dram, bass.IndirectOffsetOnAxis(slot_i[:, n, tile:tile + 1].bitcast(U32), axis=0), xf[:, tile, :], None,
                    ).then_inc(s["scattered"], 16)

            def add_rows(tile, slot_no, first=False):
                pool.wait_ge(s["y2"], tile + 1)
                pool.wait_ge(s["idx"], tile + 1)
                if not first:
                    pool.wait_ge(s["scat"], tile * 16)
                pool.sem_inc(s["added"], 1)
                nc.gpsimd.indirect_dma_start(
                    out, bass.IndirectOffsetOnAxis(idx[:, slot_no:slot_no + 1].bitcast(U32), axis=0), y_out[:, slot_no, :], None,
                    compute_op=ALU.add).then_inc(s["scat"], 16)

            pool.wait_ge(s["out_init"], 16 * TILES)
            pool.wait_ge(s["out_spare"], 16)
            pool.sem_inc(s["added"], 1)
            add_rows(0, 0, first=True)
            with pool.Fori(0, (SLOT_TILES - 1) // 2) as i:
                for u in (1, 2):
                    add_rows(i * 2 + u, u % 2)


def constants():
    c = np.zeros((P, CONST_W), np.float32)
    p = np.arange(P)
    c[:, CONST["ident"]] = np.eye(P)
    c[:, CONST["before"]] = p[:, None] < p[None, :]
    c[:, CONST["ones"]] = 1.0
    half = HD // 2
    theta = np.float32(10000.0) ** (-np.arange(half, dtype=np.float32) / half)
    angle = theta[p % half][:, None] * np.arange(L, dtype=np.float32)[None, :]
    c[:, CONST["cos"]] = np.cos(angle)
    c[:, CONST["sin"]] = np.sin(angle) * np.where(p % HD < half, -1.0, 1.0)[:, None]
    c[:, CONST["left_mask"]] = np.arange(60)[None, :] - (B - BT) == p[:, None] // L
    e = np.arange(E)
    c[:, CONST["low"]] = (e[None, :] < e[:, None]).reshape(1, -1)
    c[:, CONST["tile_no"]] = np.arange(32)
    c[:, CONST["steps"]] = P * np.arange(1, 9)
    token_no = (p[:, None] + P * np.arange(TILES + 1)[None, :]).astype(np.int32)
    return c, token_no


def kernel(x, ctx_768, L0_xattn_ln1_g, L0_xattn_ln1_b, L0_xattn_ln2_g, L0_xattn_ln2_b, L0_xattn_Wq, L0_xattn_bq,
           L0_xattn_Wk, L0_xattn_bk, L0_xattn_Wv, L0_xattn_bv, L0_xattn_Wo, L0_xattn_bo, L0_attn_Wq, L0_attn_bq,
           L0_attn_Wk, L0_attn_bk, L0_attn_Wv, L0_attn_bv, L0_attn_Wo, L0_attn_bo, L0_ffn_gate_w,
           L0_ffn_balance_bias, L0_ffn_w1, L0_ffn_w2):
    import concourse.bacc as bacc
    from concourse.bass_utils import run_bass_kernel_spmd

    def blocks(a):
        return np.asarray(a).reshape(-1, P).T

    cols = np.concatenate([blocks(a) for a in (L0_xattn_ln1_g, L0_xattn_ln1_b, L0_xattn_bq, L0_xattn_ln2_g, L0_xattn_ln2_b,
                                               L0_xattn_bk, L0_xattn_bv, L0_attn_bq, L0_attn_bk)], 1)
    rows = np.concatenate([np.asarray(a) for a in (L0_xattn_bo, L0_attn_bv, L0_attn_bo, L0_ffn_balance_bias)])
    w1T = np.asarray(L0_ffn_w1).transpose(0, 2, 1).reshape(E, KC, P, EH).transpose(0, 2, 1, 3).reshape(E, P, KC * EH)
    w2T = np.asarray(L0_ffn_w2).transpose(0, 2, 1).reshape(E, HC, P, D).transpose(0, 2, 1, 3).reshape(E, P, HC * D)
    consts, token_no = constants()
    arrays = {
        "x": np.asarray(x).reshape(TOK, D), "ctx_768": ctx_768, "cols": cols, "rows": np.broadcast_to(rows, (P, ROWS_W)),
        "consts": consts, "token_no": token_no,
        "wq": L0_xattn_Wq, "wk": L0_xattn_Wk, "wkT": np.asarray(L0_xattn_Wk).T, "wv": L0_xattn_Wv, "wo": L0_xattn_Wo,
        "swqT": np.asarray(L0_attn_Wq).T, "swkT": np.asarray(L0_attn_Wk).T, "swvT": np.asarray(L0_attn_Wv).T,
        "swoT": np.asarray(L0_attn_Wo).T, "gate_wT": np.asarray(L0_ffn_gate_w).T,
        "experts": np.concatenate([w1T, w2T], 2),
    }
    arrays = {name: np.ascontiguousarray(a) for name, a in arrays.items()}
    nc = bacc.Bacc("TRN2", target_bir_lowering=False, num_devices=1)
    t_in = {name: nc.dram_tensor(f"in_{name}", a.shape, mybir.dt.from_np(a.dtype), kind="ExternalInput").ap()
            for name, a in arrays.items()}
    out = nc.dram_tensor("out", (TOK + P, D), F32, kind="ExternalOutput").ap()
    program(nc, t_in, out)
    result = run_bass_kernel_spmd(nc, [{f"in_{name}": a for name, a in arrays.items()}], core_ids=[0])
    return result.results[0]["out"][0:TOK].reshape(B, L, D)
```

```python
from contextlib import ExitStack

import numpy as np

import concourse.bass as bass
from concourse import mybir

F32 = mybir.dt.float32
F16 = mybir.dt.float16
I32 = mybir.dt.int32
U32 = mybir.dt.uint32
ALU = mybir.AluOpType
ACT = mybir.ActivationFunctionType
AX = mybir.AxisListType
ds = bass.ds

P = 128
B, L, D = 32, 32, 512
KEYS, DC = 257, 384
KC, CC = D // P, DC // P
TOK = B * L
TILES = TOK // P
PAIRS = TILES // 2
BT = P // L
HEADS, HD = 16, 32
E, EH = 8, 1024
HC = EH // P
EPS = 1e-5
X_SCALE = float(D) ** -0.5
H_SCALE = float(HD) ** -0.5
SLOT_TILES = (2 * TOK + (E - 1) * (P - 1) + P) // P
ROW = D + 8
C_TOKEN, C_G1, C_E1, C_G2, C_E2 = range(D, D + 5)
W2_AT = KC * EH
EXPERT = KC * EH + HC * D
W_SCALE = 256.0
PASSES = ((0, 0), (0, 1), (1, 0))
W_PIECES = 4
PIECE = EXPERT // W_PIECES
ROW_SLOTS = 2
ROUTED = ((0, TILES - 4), (TILES - 4, TILES - 2), (TILES - 2, TILES))
COUNT_BANKS = ((6, 7), (0, 1), (0, 1))

CONST = {}
_at = 0
for _name, _width in (("ident", P), ("before", P), ("ones", P), ("cos", L), ("sin", L), ("left_mask", 60),
                      ("low", E * E), ("tile_no", 32), ("steps", 8)):
    CONST[_name] = slice(_at, _at + _width)
    _at += _width
CONST_W = _at
COLS = {}
_at = 0
for _name, _width in (("ln1_g", KC), ("ln1_b", KC), ("bq", KC), ("ln2_g", CC), ("ln2_b", CC), ("bk", KC), ("bv", KC),
                      ("sbq", KC), ("sbk", KC), ("sbv", KC)):
    COLS[_name] = slice(_at, _at + _width)
    _at += _width
COLS_W = _at
ROWS = {"bo": slice(0, D), "sbo": slice(D, 2 * D), "balance": slice(2 * D, 2 * D + E)}
ROWS_W = 2 * D + E

SEMS = """const_in x_in0 x_in left_in qk_weights_in wk_in vo_weights_in self_weights_in
rows_in cols_in ints_in
ctx_in0 ctx_in1 ctx_in2 ctx_in3
norm_step ln1_ve ln1_rstd ln2_ve ln2_rstd ln2_out
x1T_ps x1T x_plus_bo
left_ve left_rstd left_n left_ps left_T
kb_ps kb bqk left_bias_ps left_bias m1_ps m1_hi m1_lo m2_ps m2_hi m2_lo bvo_ps bvo x1_hi x1_lo x2a_hi x2a_lo scale2
cx_ve cx_rstd cx_shift cx_n0 cx_n1 cxT_ps cxT left_cols
qk_ps qkT qb_ps q_bias sc_ps max_step sc_nb sc_exp sc_rinv sc_pm pT_ps pT cv_ps cv cvT_ps x2aT0 x2aT1 y_ps x_new
ptx_zero ln3_ve ln3_rstd ln3_out xnT_ps xnT xnT_lo sw_hi sw_lo sq_ps sk_ps sq sk swapped cosined sined
rotated k_exp sv_ps sv ss_ps softmax_step s_sub s_exp s_pT ao_ps aoT sy_ps x_post x_plus_sbo
ln4_ve ln4_rstd xf xf_hi xf_lo xfT_ps xfT z_ps z out_init
route rt_sel rt_cnt_ps rt_exp rt_slots rt_map zrow_fill zrow xs_zero rows_set scattered
xg_in0 xg_in1 fields xgT_ps xgT h_ps h h_hi h_lo hT_ps0 hT_ps1 hT0 hT1 y2_ps y2 gate_parts gate idx scat added out_spare
ident16 finished staged w_hi w1_lo w2_lo""".split()


def program(nc, t_in, out):
    with ExitStack() as ctx:
        def sb(name, shape, dt=F32):
            return ctx.enter_context(nc.sbuf_tensor(name, shape, dt))

        s = {n: ctx.enter_context(nc.semaphore(n)) for n in SEMS}
        ctx_in = (s["ctx_in0"], s["ctx_in1"], s["ctx_in2"], s["ctx_in3"])
        bank = [ctx.enter_context(nc.psum_tensor(f"bank{i}", [P, 512], F32)) for i in range(8)]
        xs_dram = nc.dram_tensor("routed_rows", (E * TOK + P, ROW), F32).ap()

        consts = sb("consts", [P, CONST_W])
        cols = sb("cols", [P, COLS_W])
        rows = sb("rows", [P, ROWS_W])
        token_no = sb("token_no", [P, TILES + 1], I32)
        gate_w = sb("gate_w", [P, KC, E])
        x = sb("x", [P, TILES * D])
        shared = sb("shared", [P, TILES * ROW])
        wbuf = sb("wbuf", [P, 2 * EXPERT])
        ctx_region = sb("ctx_region", [P, 4 * BT * 2 * DC])
        ctxT_region = sb("ctxT_region", [P, 2 * CC * BT * KEYS])
        small = sb("small", [P, 600])
        ints = sb("ints", [P, 182], I32)
        xn = sb("xn", [P, 2, D])
        actT = sb("actT", [P, KC * 2 * P])
        misc = sb("misc", [P, 3072])
        ident16 = sb("ident16", [P, P], F16)

        def const(name):
            return consts[:, CONST[name]]

        def col(name, i):
            return cols[:, COLS[name].start + i:COLS[name].start + i + 1]

        def row(name):
            return rows[:, ROWS[name]]

        ident = const("ident")

        class Carve:

            def __init__(self, region, at, end):
                self.region, self.at, self.end = region, at, end

            def take(self, *shape):
                n = int(np.prod(shape))
                assert self.at + n <= self.end, (self.at, n, self.end)
                part = self.region[:, self.at:self.at + n]
                self.at += n
                if len(shape) == 1:
                    return part
                names = "abcd"[:len(shape)]
                pattern = f"p ({' '.join(names)}) -> p {' '.join(names)}"
                return part.rearrange(pattern, **dict(zip(names, shape)))

        c = Carve(wbuf, 0, EXPERT)
        m1, m2 = c.take(KC * DC), c.take(CC * D)
        m1 = m1.bitcast(F16).rearrange("p (a k d) -> p a k d", a=2, k=KC)
        m2 = m2.bitcast(F16).rearrange("p (a k d) -> p a k d", a=2, k=CC)
        wkT, wvT, wo = c.take(KC, DC), c.take(KC, DC), c.take(KC, D)
        c = Carve(wbuf, EXPERT, 2 * EXPERT)
        wqT, wk = c.take(KC, D), c.take(CC, D)
        c = Carve(wbuf, EXPERT, 2 * EXPERT)
        swq, swk, swv, swo = c.take(KC, D), c.take(KC, D), c.take(KC, D), c.take(KC, D)
        c = Carve(wbuf, KC * DC + CC * D, EXPERT)
        swq16, swk16 = (c.take(KC * D).bitcast(F16).rearrange("p (a k d) -> p a k d", a=2, k=KC) for _ in range(2))
        swv16 = (c.take(KC * D // 2).bitcast(F16).rearrange("p (k d) -> p k d", k=KC),
                 wbuf[:, EXPERT:EXPERT + KC * D // 2].bitcast(F16).rearrange("p (k d) -> p k d", k=KC))
        self_weights = ((swq, (swq16[:, 0], swq16[:, 1])), (swk, (swk16[:, 0], swk16[:, 1])), (swv, swv16))
        c = Carve(shared, 0, TILES * ROW)
        x1T = c.take(KC, 2 * P)
        x1 = c.take(KC * 2 * P).bitcast(F16).rearrange("p (a k t) -> p a k t", a=2, k=KC)
        cv = c.take(2, DC)
        x2a = c.take(CC * 2 * P).bitcast(F16).rearrange("p (a k t) -> p a k t", a=2, k=CC)
        ctx_n = ctx_region[:, :].rearrange("p (s b c d) -> p s b c d", s=4, b=BT, c=2)
        ctxT = ctxT_region[:, :].rearrange("p (t c b k) -> p t c b k", t=2, c=CC, b=BT)
        c = Carve(misc, 0, 3072)
        qkT = c.take(CC, 2 * P)
        probs = c.take(2, 264)
        pT = c.take(2, 2 * P)
        p_left = c.take(2, P)
        left_T = c.take(CC, B)
        left_n = c.take(DC)
        p_mask = c.take(2, B)
        x2aT = actT[:, 0:CC * 2 * P].rearrange("p (k t) -> p k t", k=CC)
        c = Carve(small, 0, 600)
        stats = c.take(2, 6)
        mv = c.take(2, 2)
        ve = c.take(2)
        rstd = c.take(2)
        ve2, rstd2 = c.take(2), c.take(2)
        cx_stats = c.take(2, 8, 6)
        cx_mv = c.take(2, 8, 2)
        cx_ve = c.take(2, 8)
        cx_rstd = c.take(2, 8)
        cx_shift = c.take(8)
        l_stats, l_mv, l_ve, l_rstd = c.take(6), c.take(2), c.take(1), c.take(1)
        kb = c.take(KC)
        qk_bias = c.take(CC)
        ln2_g_scaled = c.take(CC)
        bias_of = c.take(KC + 1)
        bias16 = c.take(KC).bitcast(F16).rearrange("p (a k) -> p a k", a=2)
        q_bias = c.take(2)
        sc_max, sc_u, sc_nb, sc_sum, sc_rinv = c.take(2), c.take(2), c.take(2), c.take(2), c.take(2)
        s_max, s_sum, s_rinv = c.take(2, HEADS), c.take(2, HEADS), c.take(2, HEADS)
        z = c.take(TILES, E)
        neg_half = c.take(8)
        gates = c.take(2, 4)
        fields = c.take(2, 4)
        c = Carve(ctx_region, 0, 4 * BT * 2 * DC)
        xnT = c.take(KC * 2 * P).bitcast(F16).rearrange("p (a k t) -> p a k t", a=2, k=KC)
        qb, q_sw, kbuf, k_sw = (c.take(KC * 2 * P) for _ in range(4))
        q_T, k_T = (a.rearrange("p (k t) -> p k t", k=KC) for a in (qb, kbuf))
        k_exp = c.take(KC, 2 * BT, 4, L)
        v = c.take(2, 2, D)
        xfT = c.take(KC, 2 * P)
        c = Carve(ctxT_region, 0, 2 * CC * BT * KEYS)
        p_T = c.take(2, HEADS, P)
        soft = c.take(2, D)
        aoT = actT[:, :].rearrange("p (t c q) -> p t c q", t=2, c=KC)
        c = Carve(misc, 0, 3072)
        ln4_n = c.take(2, D)
        y_out = c.take(2, D)
        xf = shared[:, :].rearrange("p (t r) -> p t r", t=TILES)
        xf16 = shared[:, :].bitcast(F16).rearrange("p (t r) -> p t r", t=TILES)
        c = Carve(ctxT_region, 5 * 1024, 5600)
        rank, sel, sig = c.take(TILES, E), c.take(TILES, E), c.take(TILES, E)
        chosen, picked = c.take(2, TILES, E), c.take(2, TILES, E)
        gate_of_token, gate_sum = c.take(2, TILES), c.take(TILES)
        c = Carve(misc, 2048, 3072)
        cmp_a, cmp_b = c.take(TILES - 4, E, E), c.take(TILES - 4, E, E)
        base, slot, slot_f = c.take(TILES + 1, E), c.take(TILES, E), c.take(2, TILES)
        total, ntile, ends, skipped = c.take(E), c.take(E), c.take(E), c.take(E)
        c = Carve(ctxT_region, 0, 5 * 1024)
        over, ends_tmp = c.take(E, 8), c.take(E, E)
        emap, emap_cmp, first_of, not_last, packed, row_at = (c.take(32), c.take(32, E), c.take(32), c.take(32), c.take(32),
                                                              c.take(32))
        h = c.take(EH)
        h16 = c.take(EH).bitcast(F16).rearrange("p (a h) -> p a h", a=2)
        zrow = ctxT_region[:, 5600:5600 + ROW]
        expert0 = wbuf[:, 0:EXPERT]
        c = Carve(ctx_region, 0, 4 * BT * 2 * DC)
        stage = c.take(EXPERT)
        xg = c.take(ROW_SLOTS, ROW)
        xg16 = xg.rearrange("p s r -> p (s r)").bitcast(F16).rearrange("p (s r) -> p s r", s=ROW_SLOTS)
        xgT = c.take(2, D).rearrange("p s d -> p (s d)").bitcast(F16).rearrange("p (s a d) -> p s a d", s=2, a=2)
        hT = [a[:, :].bitcast(F16).rearrange("p (a d) -> p a d", a=2) for a in (actT, xn[:, :, :].rearrange("p t d -> p (t d)"))]
        w16 = wbuf[:, :].bitcast(F16)
        HIGH, LOW = 0, EXPERT
        slot_i = ints[:, 0:2 * TILES].rearrange("p (a t) -> p a t", a=2)
        map_i = ints[:, 16:16 + 160].rearrange("p (a t) -> p a t", a=5)
        idx = ints[:, 176:178]
        tokens = ints[:, 178:180]
        used, last_tile = ints[:, 180:181], ints[:, 181:182]

        xg_in = (s["xg_in0"], s["xg_in1"])
        block = ctx.enter_context(nc.Block())


        def last_of(engine):
            return engine.value_load(last_tile[0:1, :], min_val=E, max_val=SLOT_TILES - 1)

        @block.sync
        def _(sp):
            sp.dma_start(consts[:, :], t_in["consts"]).then_inc(s["const_in"], 16)
            x_tiles = x[:, :].rearrange("p (t d) -> p t d", t=TILES)
            x_dram = t_in["x"].rearrange("(t p) d -> p t d", p=P)

            def load_w(w, name, sem):
                sp.dma_start(w, t_in[name].rearrange("(k p) e -> p k e", p=P)).then_inc(sem, 16)

            def load_ctx(tile):
                sp.dma_start(
                    ctx_n[:, tile % 4].rearrange("p b c d -> p b (c d)"),
                    t_in["ctx_768"][tile * BT:(tile + 1) * BT, 0:KEYS - 1, :].rearrange("b (p c) d -> p b (c d)", c=2),
                ).then_inc(ctx_in[tile % 4], 16)

            def load_expert(e, dst):
                for n in range(W_PIECES):
                    if e > 1:
                        sp.wait_ge((s["w1_lo"], s["w2_lo"])[n // 2], 2 * (e - 1) + n % 2 + 1)
                    piece = slice(n * PIECE, (n + 1) * PIECE)
                    sp.dma_start(dst[:, piece], t_in["experts"][e][:, piece]).then_inc(s["staged"], 16)
                    sp.wait_ge(s["staged"], 16 * (e * W_PIECES + n + 1))

            sp.dma_start(x_tiles[:, 0:2], x_dram[:, 0:2]).then_inc(s["x_in0"], 16)
            load_w(wqT, "wqT", s["qk_weights_in"])
            load_w(wkT, "wkT", s["qk_weights_in"])
            sp.dma_start(cols[:, :], t_in["cols"]).then_inc(s["cols_in"], 16)
            load_ctx(0)
            sp.dma_start(left_n[0:B, :], t_in["ctx_768"][:, KEYS - 1, :]).then_inc(s["left_in"], 16)
            load_w(wk, "wk", s["wk_in"])
            load_ctx(1)
            load_w(wvT, "wvT", s["vo_weights_in"])
            load_w(wo, "wo", s["vo_weights_in"])
            sp.dma_start(rows[:, :], t_in["rows"]).then_inc(s["rows_in"], 16)
            sp.dma_start(x_tiles[:, 2:TILES], x_dram[:, 2:TILES]).then_inc(s["x_in"], 16)
            load_ctx(2)
            load_ctx(3)
            load_w(gate_w[:, :, :], "gate_wT", s["self_weights_in"])
            sp.dma_start(token_no[:, :], t_in["token_no"]).then_inc(s["ints_in"], 16)
            sp.wait_ge(s["left_bias_ps"], 1)
            for w, name in ((swq, "swqT"), (swk, "swkT"), (swv, "swvT"), (swo, "swoT")):
                load_w(w, name, s["self_weights_in"])
            for tile in range(4, TILES):
                sp.wait_ge(s["cv_ps"], tile - 3)
                load_ctx(tile)
            sp.wait_ge(s["zrow"], 1)
            sp.dma_start(xs_dram.rearrange("(n p) r -> p n r", p=P),
                         zrow[:, None, :].to_broadcast([P, E * TILES + 1, ROW])).then_inc(s["xs_zero"], 16)
            sp.dma_start(out[TOK:TOK + P, :], zrow[:, 0:D]).then_inc(s["out_spare"], 16)
            sp.wait_ge(s["sv_ps"], TILES)
            load_expert(0, expert0)
            sp.wait_ge(s["z_ps"], TILES)
            for e in range(1, E):
                load_expert(e, stage)
            sp.wait_ge(s["out_init"], 16 * TILES)
            sp.wait_ge(s["finished"], 1)

        @block.tensor
        def _(pe):
            pe.wait_ge(s["const_in"], 16)

            def transposes(dst, pieces, sem, identity=ident):
                at = 0
                for piece in pieces:
                    n = piece.shape[0]
                    last = nc.tensor.transpose(dst[0:piece.shape[1], at:at + n], piece, identity[0:n, 0:n])
                    at += n
                last.then_inc(sem, 1)

            def queries_T(pair):
                for t in range(2):
                    pe.wait_ge(s["ln2_out"], 2 * pair + t + 1)
                    transposes(bank[t], [xn[:, t, k * P:(k + 1) * P] for k in range(KC)], s["x1T_ps"])

            small_sums = bank[6]
            pe.wait_ge(s["qk_weights_in"], 32)
            for d in range(KC):
                for e in range(KC):
                    mm = nc.tensor.matmul(bank[2 + d][:, 0:DC], wqT[:, e, d * P:(d + 1) * P], wkT[:, e, :],
                                          start=(e == 0), stop=(e == KC - 1))
                mm.then_inc(s["m1_ps"], 1)
            pe.wait_ge(s["wk_in"], 16)
            pe.wait_ge(s["cols_in"], 16)
            for e in range(KC):
                for k in range(CC):
                    nc.tensor.matmul(small_sums[:, e:e + 1], wk[:, k, e * P:(e + 1) * P], col("ln2_b", k),
                                     start=(k == 0), stop=(k == CC - 1))
            for k in range(CC):
                for e in range(KC):
                    mm = nc.tensor.matmul(small_sums[:, 8 + k:9 + k], wkT[:, e, k * P:(k + 1) * P], col("bq", e),
                                          start=(e == 0), stop=(e == KC - 1))
            mm.then_inc(s["kb_ps"], 1)
            pe.wait_ge(s["left_n"], 1)
            transposes(bank[0], [left_n[0:B, k * P:(k + 1) * P] for k in range(CC)], s["left_ps"])
            pe.wait_ge(s["left_T"], 1)
            queries_T(0)
            pe.wait_ge(s["kb"], 1)
            pe.wait_ge(s["bqk"], 1)
            for d in range(KC):
                for e in range(KC):
                    nc.tensor.matmul(small_sums[:, 16 + d:17 + d], wqT[:, e, d * P:(d + 1) * P], kb[:, e:e + 1],
                                     start=(e == 0), stop=(e == KC - 1))
            for e in range(KC):
                mm = nc.tensor.matmul(small_sums[:, 16 + KC:17 + KC], col("bq", e).to_broadcast([P, P]), kb[:, e:e + 1],
                                      start=(e == 0), stop=(e == KC - 1))
            mm.then_inc(s["left_bias_ps"], 1)

            def context_T(tile):
                pe.wait_ge(s["cx_n0"], tile + 1)
                if tile % 2:
                    pe.wait_ge(s["cx_n1"], tile // 2 + 1)
                for n in range(2 * CC):
                    k, half = n // 2, n % 2
                    use = 2 * CC * tile + n
                    if tile % 2 == 0 and n < 2:
                        pe.wait_ge(s["x1T"], tile + 2)
                    else:
                        pe.wait_ge(s["cxT"], use - 1)
                    transposes(bank[use % 2], [ctx_n[:, tile % 4, 2 * half + b, c2, k * P:(k + 1) * P]
                                               for b in range(2) for c2 in range(2)], s["cxT_ps"])

            def join_values():
                pe.wait_ge(s["vo_weights_in"], 32)
                for k in range(CC):
                    for e in range(KC):
                        mm = nc.tensor.matmul(bank[(6, 7, 0)[k]][:, :], wvT[:, e, k * P:(k + 1) * P], wo[:, e, :],
                                              start=(e == 0), stop=(e == KC - 1))
                    mm.then_inc(s["m2_ps"], 1)
                for e in range(KC):
                    mm = nc.tensor.matmul(bank[1][:, :], col("bv", e).to_broadcast([P, P]), wo[:, e, :],
                                          start=(e == 0), stop=(e == KC - 1))
                mm.then_inc(s["bvo_ps"], 1)

            def asked(pair):
                pe.wait_ge(s["x1_lo"], pair + 1)
                if pair == 0:
                    pe.wait_ge(s["left_bias"], 3)
                    pe.wait_ge(s["m1_lo"], KC)
                elif pair > 1:
                    pe.wait_ge(s["x_new"], 2 * pair - 2)
                for d in range(CC):
                    for k in range(KC):
                        for w_part, x_part in PASSES:
                            mm = nc.tensor.matmul(bank[6 + d // 2][:, d % 2 * 256:d % 2 * 256 + 256],
                                                  m1[:, w_part, k, d * P:(d + 1) * P], x1[:, x_part, k, :],
                                                  start=(k == 0 and w_part + x_part == 0), stop=(k == KC - 1 and w_part == 1))
                    if d == 1:
                        mm.then_inc(s["qk_ps"], 1)
                for t in range(2):
                    for k in range(KC):
                        for x_part, b_part in PASSES:
                            mm = nc.tensor.matmul(bank[7][:, 256 + t:257 + t], x1[:, x_part, k, t * P:(t + 1) * P],
                                                  bias16[:, b_part, k:k + 1], start=(k == 0 and x_part + b_part == 0),
                                                  stop=(k == KC - 1 and x_part == 1))
                mm.then_inc(s["qb_ps"], 1)

            def context_scores(pair):
                pe.wait_ge(s["qkT"], pair + 1)
                for t in range(2):
                    tile = 2 * pair + t
                    pe.wait_ge(s["cxT"], 2 * CC * (tile + 1))
                    pe.wait_ge(s["left_cols"], tile + 1)
                    for k in range(CC):
                        for b in range(BT):
                            mm = nc.tensor.matmul(bank[2 + t][b * L:(b + 1) * L, 0:KEYS],
                                                  qkT[:, k, t * P + b * L:t * P + (b + 1) * L], ctxT[:, t, k, b, :],
                                                  start=(k == 0), stop=(k == CC - 1), tile_position=(0, b * L),
                                                  skip_group_check=True)
                    mm.then_inc(s["sc_ps"], 1)

            def probs_T(pair):
                for t in range(2):
                    pe.wait_ge(s["sc_pm"], 2 * pair + t + 1)
                    transposes(bank[4 + t], [probs[:, t, 0:P], probs[:, t, P:2 * P], p_mask[:, t, :]], s["pT_ps"])

            def context_sums(pair):
                for t in range(2):
                    tile = 2 * pair + t
                    pe.wait_ge(s["pT"], 2 * tile + 2)
                    nc.tensor.matmul(bank[2 + t][:, 0:DC], p_left[0:B, t, :], left_n[0:B, :], start=True, stop=False,
                                     skip_group_check=True)
                    for c2 in range(2):
                        for b in range(BT):
                            at = c2 * P + b * L
                            mm = nc.tensor.matmul(bank[2 + t][b * L:(b + 1) * L, 0:DC], pT[:, t, at:at + L],
                                                  ctx_n[:, tile % 4, b, c2, :], start=False, stop=(c2 == 1),
                                                  tile_position=(0, b * L), skip_group_check=True)
                    mm.then_inc(s["cv_ps"], 1)

            def sums_T(pair):
                for t in range(2):
                    pe.wait_ge(s["cv"], 2 * pair + t + 1)
                    transposes(bank[4 + t], [cv[:, t, k * P:(k + 1) * P] for k in range(CC)], s["cvT_ps"])

            def context_result(pair):
                pe.wait_ge(s["x2a_lo"], 2 * pair + 2)
                pe.wait_ge(s["q_bias"], min(pair + 2, PAIRS))
                for t in range(2):
                    for k in range(CC):
                        for x_part, w_part in PASSES:
                            mm = nc.tensor.matmul(bank[6 + t][:, :], x2a[:, x_part, k, t * P:(t + 1) * P], m2[:, w_part, k, :],
                                                  start=(k == 0 and x_part + w_part == 0), stop=(k == CC - 1 and x_part == 1))
                    mm.then_inc(s["y_ps"], 1)

            def normalised_T(pair):
                for t in range(2):
                    pe.wait_ge(s["ln3_out"], 2 * pair + t + 1)
                    transposes(bank[t], [xn[:, t, k * P:(k + 1) * P] for k in range(KC)], s["xnT_ps"])

            def by_channel(n, first, sem):
                pe.wait_ge(s["sw_lo"], n + 1)
                w = self_weights[n][1]
                for e in range(KC):
                    for k in range(KC):
                        for w_part, x_part in PASSES:
                            mm = nc.tensor.matmul(bank[first + e // 2][:, e % 2 * 256:e % 2 * 256 + 256],
                                                  w[w_part][:, k, e * P:(e + 1) * P], xnT[:, x_part, k, :],
                                                  start=(k == 0 and w_part + x_part == 0), stop=(k == KC - 1 and w_part == 1))
                    if e % 2:
                        mm.then_inc(sem, 1)

            def queries(pair):
                pe.wait_ge(s["xnT_lo"], 2 * pair + 2)
                if pair == 0:
                    pe.wait_ge(s["cv"], TILES)
                by_channel(0, 2, s["sq_ps"])

            def keys(pair):
                by_channel(1, 4, s["sk_ps"])

            def values(pair):
                pe.wait_ge(s["sw_lo"], 3)
                if pair:
                    pe.wait_ge(s["sv"], 2 * pair)
                else:
                    pe.wait_ge(s["x_new"], TILES)
                for t in range(2):
                    for k in range(KC):
                        for x_part, w_part in PASSES:
                            mm = nc.tensor.matmul(bank[6 + t][:, :], xnT[:, x_part, k, t * P:(t + 1) * P], swv16[w_part][:, k, :],
                                                  start=(k == 0 and x_part + w_part == 0), stop=(k == KC - 1 and x_part == 1))
                    mm.then_inc(s["sv_ps"], 1)

            def scores(pair):
                pe.wait_ge(s["rotated"], 2 * pair + 1)
                pe.wait_ge(s["k_exp"], pair + 1)
                for t in range(2):
                    for c4 in range(KC):
                        for b in range(BT):
                            mm = nc.tensor.matmul(bank[t][b * L:(b + 1) * L, c4 * P:(c4 + 1) * P],
                                                  q_T[:, c4, t * P + b * L:t * P + (b + 1) * L],
                                                  k_exp[:, c4, t * BT + b, :, :].rearrange("p h l -> p (h l)"),
                                                  start=True, stop=True, tile_position=(0, b * L), skip_group_check=True)
                    mm.then_inc(s["ss_ps"], 1)

            def choices_before(n):
                lo, hi = ROUTED[n]
                pe.wait_ge(s["rt_sel"], n + 1)
                some = sel[:, lo:hi, :].rearrange("p t e -> p (t e)")
                for b, name in zip(COUNT_BANKS[n], ("before", "ones")):
                    nc.tensor.matmul(bank[b][:, lo * E:hi * E], const(name), some, start=True, stop=True).then_inc(s["rt_cnt_ps"], 1)

            def attend(pair):
                if pair:
                    pe.wait_ge(s["z"], 2 * pair)
                for t in range(2):
                    pe.wait_ge(s["s_pT"], 2 * pair + t + 1)
                    pe.wait_ge(s["sv"], 2 * pair + t + 1)
                    for hd in range(HEADS):
                        at = hd % 4 * HD
                        mm = nc.tensor.matmul(bank[2 + t][at:at + HD, hd // 4 * P:(hd // 4 + 1) * P],
                                              v[:, pair % 2, t, hd * HD:(hd + 1) * HD], p_T[:, t, hd, :],
                                              start=True, stop=True, tile_position=(0, at), skip_group_check=True)
                    mm.then_inc(s["ao_ps"], 1)
                if pair + 1 == PAIRS:
                    choices_before(0)
                else:
                    pe.wait_ge(s["sk"], 2 * pair + 4)
                if pair + 2 < PAIRS:
                    normalised_T(pair + 2)
                for t in range(2):
                    pe.wait_ge(s["aoT"], 2 * pair + t + 1)
                    for k in range(KC):
                        mm = nc.tensor.matmul(bank[4 + t][:, :], aoT[:, t, k, :], swo[:, k, :],
                                              start=(k == 0), stop=(k == KC - 1))
                    mm.then_inc(s["sy_ps"], 1)

            def features_T(pair):
                pe.wait_ge(s["sv"], min(2 * pair + 4, TILES))
                for t in range(2):
                    pe.wait_ge(s["xf"], 2 * pair + t + 1)
                    transposes(bank[6 + t], [ln4_n[:, t, k * P:(k + 1) * P] for k in range(KC)], s["xfT_ps"])

            def logits(pair):
                if pair + 2 < PAIRS:
                    pe.wait_ge(s["sq"], 2 * pair + 6)
                for t in range(2):
                    pe.wait_ge(s["xfT"], 2 * pair + t + 1)
                    for k in range(KC):
                        mm = nc.tensor.matmul(bank[2 + t][:, 0:E], xfT[:, k, t * P:(t + 1) * P], gate_w[:, k, :],
                                              start=(k == 0), stop=(k == KC - 1))
                    mm.then_inc(s["z_ps"], 1)

            asked(0)
            context_T(0)
            context_T(1)
            for pair in range(PAIRS):
                last = pair + 1 == PAIRS
                context_scores(pair)
                if pair:
                    context_result(pair - 1)
                else:
                    join_values()
                probs_T(pair)
                if pair == 0:
                    pe.wait_ge(s["m2_lo"], CC)
                    pe.wait_ge(s["bvo"], 1)
                if not last:
                    queries_T(pair + 1)
                context_sums(pair)
                if last:
                    normalised_T(0)
                    sums_T(pair)
                    queries(0)
                else:
                    context_T(2 * pair + 2)
                    asked(pair + 1)
                    context_T(2 * pair + 3)
                    sums_T(pair)
            context_result(PAIRS - 1)
            keys(0)
            values(0)
            normalised_T(1)
            pe.wait_ge(s["ptx_zero"], 2)
            for pair in range(PAIRS):
                last = pair + 1 == PAIRS
                if last:
                    scores(pair)
                    features_T(pair - 1)
                    logits(pair - 1)
                else:
                    queries(pair + 1)
                    if pair:
                        features_T(pair - 1)
                    scores(pair)
                    keys(pair + 1)
                    if pair:
                        logits(pair - 1)
                    values(pair + 1)
                attend(pair)
            choices_before(1)
            pe.wait_ge(s["rt_slots"], 1)
            features_T(PAIRS - 1)
            logits(PAIRS - 1)
            choices_before(2)

            pe.wait_ge(s["rt_map"], 1)
            pe.wait_ge(s["ident16"], 1)

            def rows_T(b, landed):
                pe.wait_ge(xg_in[b], landed)
                transposes(bank[(4, 7)[b]][:, :].bitcast(F16), [xg16[:, b, k * P:(k + 1) * P] for k in range(2 * KC)],
                           s["xgT_ps"], ident16)

            def experts_of(tile):
                packed = pe.value_load(map_i[0:1, 3, ds(tile, 1)], min_val=0, max_val=16 ** 3 - 1)
                return [(ready, ready % 2 * (2 * EXPERT)) for ready in (packed % 16, packed // 16 % 16, packed // 256)]

            def first_product(tile, b, expert):
                ready, at = expert
                pe.wait_ge(s["w1_lo"], ready * 2)
                pe.wait_ge(s["xgT"], tile + 1)
                for half in range(2):
                    for k in range(KC):
                        for x_part, w_part in ((0, HIGH), (1, HIGH), (0, LOW)):
                            mm = nc.tensor.matmul(bank[half][:, :], xgT[:, b, x_part, k * P:(k + 1) * P],
                                                  w16[:, ds(at + (w_part + k * EH + half * 512), 512)],
                                                  start=(k == 0 and x_part + w_part == 0), stop=(k == KC - 1 and w_part == LOW))
                    mm.then_inc(s["h_ps"], 1)

            def hidden_T(tile):
                for part, cut, done in ((0, s["h_hi"], s["hT_ps0"]), (1, s["h_lo"], s["hT_ps1"])):
                    pe.wait_ge(cut, tile + 1)
                    transposes(bank[2 + part][:, :].bitcast(F16), [h16[:, part, k * P:(k + 1) * P] for k in range(HC)], done, ident16)

            def second_product(tile, b, expert):
                ready, at = expert
                pe.wait_ge(s["w2_lo"], ready * 2)
                pe.wait_ge(s["hT0"], tile + 1)
                pe.wait_ge(s["hT1"], tile + 1)
                for k in range(HC):
                    for h_part, w_part in ((0, HIGH), (0, LOW), (1, HIGH)):
                        mm = nc.tensor.matmul(bank[5 + b][:, :], hT[b][:, h_part, k * P:(k + 1) * P],
                                              w16[:, ds(at + (w_part + W2_AT + k * D), D)],
                                              start=(k == 0 and h_part + w_part == 0), stop=(k == HC - 1 and h_part == 1))
                mm.then_inc(s["y2_ps"], 1)

            rows_T(0, 16)
            first_product(0, 0, experts_of(0)[0])
            rows_T(1, 16)
            hidden_T(0)
            last = last_of(pe)
            with pe.Fori(0, (SLOT_TILES - 1) // 2) as i:
                with pe.If(i * 2 < last):
                    experts = experts_of(i * 2)
                    for u in (1, 2):
                        first_product(i * 2 + u, u % 2, experts[u])
                        rows_T((u + 1) % 2, i * 16 + 32)
                        second_product(i * 2 + (u - 1), (u - 1) % 2, experts[u - 1])
                        hidden_T(i * 2 + u)
            second_product(last, 0, experts_of(last)[0])

        @block.scalar
        def _(act):
            act.wait_ge(s["cols_in"], 16)

            def ctx_copies(tile):
                for n in range(2 * CC):
                    k, half = n // 2, n % 2
                    use = 2 * CC * tile + n
                    act.wait_ge(s["cxT_ps"], use + 1)
                    nc.scalar.copy(ctxT[:, tile % 2, k, 2 * half:2 * half + 2, 0:KEYS - 1],
                                   bank[use % 2][:, :].rearrange("p (b k) -> p b k", b=2)).then_inc(s["cxT"], 1)

            def biased(dst, first, ps_sem, count, bias, sem):
                for n in range(2):
                    act.wait_ge(ps_sem, count + n + 1)
                    for i in range(2):
                        e = 2 * n + i
                        op = scaled(dst[:, e, :], bank[first + n][:, i * 256:i * 256 + 256], 1.0 / W_SCALE, col(bias, e))
                    op.then_inc(sem, 1)

            def scaled(dst, src_, scale, bias):
                return nc.scalar.activation(dst, src_, ACT.Identity, scale=scale, bias=bias)

            def queries_out(pair):
                for t in range(2):
                    act.wait_ge(s["x1T_ps"], 2 * pair + t + 1)
                    for k in range(KC):
                        op = scaled(x1T[:, k, t * P:(t + 1) * P], bank[t][:, k * P:(k + 1) * P], col("ln1_g", k), col("ln1_b", k))
                    op.then_inc(s["x1T"], 1)
                act.wait_ge(s["x1T"], 2 * pair + 2)
                nc.scalar.copy(x1[:, 0], x1T).then_inc(s["x1_hi"], 1)

            def asked_out(pair):
                for k in range(CC):
                    if k != 1:
                        act.wait_ge((s["qk_ps"], s["qb_ps"])[k // 2], pair + 1)
                    op = scaled(qkT[:, k, :], bank[6 + k // 2][:, k % 2 * 256:k % 2 * 256 + 256], ln2_g_scaled[:, k:k + 1], qk_bias[:, k:k + 1])
                op.then_inc(s["qkT"], 1)
                nc.scalar.activation(q_bias, bank[7][:, 256:258], ACT.Identity, bias=bias_of[:, KC:KC + 1]).then_inc(s["q_bias"], 1)

            def ctx_norm(tile):
                act.wait_ge(s["cx_shift"], tile // 2 + 1)
                for i in range(4, 8):
                    piece = ctx_n[:, tile % 4, i // 2, i % 2, :]
                    op = scaled(piece, piece, cx_rstd[:, tile % 2, i:i + 1], cx_shift[:, i:i + 1])
                op.then_inc(s["cx_n1"], 1)

            def normalised_out(pair):
                for t in range(2):
                    act.wait_ge(s["xnT_ps"], 2 * pair + t + 1)
                    nc.scalar.copy(xnT[:, 0, :, t * P:(t + 1) * P],
                                   bank[t][:, :].rearrange("p (k t) -> p k t", k=KC)).then_inc(s["xnT"], 1)

            def cut_self_high(n):
                act.wait_ge(s["self_weights_in"], 5 * 16)
                act.wait_ge(s["bvo_ps"], 1)
                nc.scalar.activation(self_weights[n][1][0], self_weights[n][0], ACT.Copy, scale=W_SCALE).then_inc(s["sw_hi"], 1)

            for d in range(KC):
                act.wait_ge(s["m1_ps"], d + 1)
                nc.scalar.activation(m1[:, 0, d, :], bank[2 + d][:, 0:DC], ACT.Copy, scale=W_SCALE).then_inc(s["m1_hi"], 1)
            queries_out(0)
            ctx_norm(1)
            act.wait_ge(s["bqk"], 1)
            act.wait_ge(s["scale2"], 1)
            act.wait_ge(s["left_bias"], 1)
            asked_out(0)
            ctx_copies(0)
            ctx_copies(1)
            for pair in range(PAIRS):
                for t in range(2):
                    act.wait_ge(s["sc_nb"], 2 * pair + t + 1)
                    nc.scalar.activation(probs[:, t, 0:KEYS], bank[2 + t][:, 0:KEYS], ACT.Exp, bias=sc_nb[:, t:t + 1],
                                         scale=X_SCALE, accum_out=sc_sum[:, t:t + 1]).then_inc(s["sc_exp"], 1)
                if pair + 1 == PAIRS:
                    cut_self_high(1)
                if pair == 0:
                    for k in range(CC):
                        act.wait_ge(s["m2_ps"], k + 1)
                        nc.scalar.activation(m2[:, 0, k, :], bank[(6, 7, 0)[k]][:, :], ACT.Copy, scale=W_SCALE)\
                            .then_inc(s["m2_hi"], 1)
                for t in range(2):
                    act.wait_ge(s["pT_ps"], 2 * pair + t + 1)
                    nc.scalar.copy(pT[:, t, :], bank[4 + t][:, 0:2 * P]).then_inc(s["pT"], 1)
                    nc.scalar.copy(p_left[0:B, t, :], bank[4 + t][0:B, 2 * P:3 * P]).then_inc(s["pT"], 1)
                if pair + 1 < PAIRS:
                    queries_out(pair + 1)
                    if pair + 2 == PAIRS:
                        cut_self_high(0)
                for t in range(2):
                    act.wait_ge(s["cv_ps"], 2 * pair + t + 1)
                    act.wait_ge(s["sc_rinv"], 2 * pair + t + 1)
                    nc.scalar.activation(cv[:, t, :], bank[2 + t][:, 0:DC], ACT.Copy, scale=sc_rinv[:, t:t + 1]).then_inc(s["cv"], 1)
                if pair + 1 < PAIRS:
                    ctx_copies(2 * pair + 2)
                    ctx_norm(2 * pair + 3)
                    asked_out(pair + 1)
                    ctx_copies(2 * pair + 3)
                else:
                    normalised_out(0)
                act.wait_ge(s["cvT_ps"], 2 * pair + 1)
                for k in range(CC):
                    op = scaled(x2aT[:, k, 0:P], bank[4][:, k * P:(k + 1) * P], col("ln2_g", k), col("ln2_b", k))
                op.then_inc(s["x2aT0"], 1)
                for t in range(2):
                    act.wait_ge((s["x2aT0"], s["x2aT1"])[t], pair + 1)
                    tile_at = slice(t * P, (t + 1) * P)
                    nc.scalar.copy(x2a[:, 0, :, tile_at], x2aT[:, :, tile_at]).then_inc(s["x2a_hi"], 1)

            cut_self_high(2)

            def turned_out(pair):
                if pair:
                    act.wait_ge(s["ss_ps"], 2 * pair)
                biased(q_T, 2, s["sq_ps"], 2 * pair, "sbq", s["sq"])

            def features_out(pair):
                for t in range(2):
                    act.wait_ge(s["xfT_ps"], 2 * pair + t + 1)
                    nc.scalar.copy(xfT[:, :, t * P:(t + 1) * P],
                                   bank[6 + t][:, :].rearrange("p (k t) -> p k t", k=KC)).then_inc(s["xfT"], 1)
                for t in range(2):
                    tile = 2 * pair + t
                    nc.scalar.copy(xf16[:, tile, 0:D], ln4_n[:, t, :]).then_inc(s["xf_hi"], 1)
                    act.wait_ge(s["x_post"], tile + 1)
                    act.dma_start(out[tile * P:(tile + 1) * P, :], x[:, tile * D:(tile + 1) * D]).then_inc(s["out_init"], 16)

            def gate_exp(n):
                lo, hi = ROUTED[n]
                act.wait_ge(s["z"], hi)
                nc.scalar.activation(sig[:, lo:hi], z[:, lo:hi], ACT.Exp, scale=-1.0).then_inc(s["rt_exp"], 1)

            def cut_high(src_, at, pieces, before):
                for n in pieces:
                    act.wait_ge(s["staged"], before + 16 * (n + 1))
                    nc.scalar.activation(w16[:, ds(at + (HIGH + n * PIECE), PIECE)], src_[:, n * PIECE:(n + 1) * PIECE],
                                         ACT.Copy, scale=W_SCALE).then_inc(s["w_hi"], 1)

            def values_out(pair):
                for t in range(2):
                    act.wait_ge(s["sv_ps"], 2 * pair + t + 1)
                    nc.scalar.activation(v[:, pair % 2, t, :], bank[6 + t][:, :], ACT.Copy, scale=1.0 / W_SCALE).then_inc(s["sv"], 1)

            def key_columns(pair):
                act.wait_ge(s["rotated"], 2 * pair + 2)
                for r in range(4):
                    part = slice(r * HD, (r + 1) * HD)
                    op = nc.scalar.copy(k_exp[part, :, :, r, :], kbuf[part].rearrange("p (c b l) -> p c b l", c=KC, l=L))
                op.then_inc(s["k_exp"], 1)

            turned_out(0)
            biased(k_T, 4, s["sk_ps"], 0, "sbk", s["sk"])
            values_out(0)
            normalised_out(1)
            act.wait_ge(s["ptx_zero"], 2)
            key_columns(0)
            for pair in range(PAIRS):
                last = pair + 1 == PAIRS
                if pair and not last:
                    features_out(pair - 1)
                if not last:
                    turned_out(pair + 1)
                for t in range(2):
                    act.wait_ge(s["s_sub"], 2 * pair + t + 1)
                    nc.scalar.activation(soft[:, t, :], soft[:, t, :], ACT.Exp, scale=H_SCALE).then_inc(s["s_exp"], 1)
                if last:
                    features_out(pair - 1)
                    cut_high(expert0, 2 * EXPERT, (0, 1), 0)
                else:
                    biased(k_T, 4, s["sk_ps"], 2 * pair + 2, "sbk", s["sk"])
                    if pair + 2 == PAIRS:
                        gate_exp(0)
                    values_out(pair + 1)
                for t in range(2):
                    act.wait_ge(s["ao_ps"], 2 * pair + t + 1)
                    for k in range(KC):
                        op = nc.scalar.activation(aoT[:, t, k, :], bank[2 + t][:, k * P:(k + 1) * P], ACT.Identity, bias=col("sbv", k))
                    op.then_inc(s["aoT"], 1)
                if pair + 2 < PAIRS:
                    normalised_out(pair + 2)
                if not last:
                    key_columns(pair + 1)

            def load_rows(tile, b):
                first = act.value_load(map_i[0:1, 4, ds(tile, 1)], min_val=0, max_val=E * TOK)
                act.dma_start(xg[:, b, :], xs_dram[ds(first, P), :]).then_inc(xg_in[b], 16)

            def cut_next_high(tile, pieces):
                new = act.value_load(map_i[0:1, 2, ds(tile, 1)], min_val=0, max_val=1)
                with act.If(new == 1):
                    ready = act.value_load(map_i[0:1, 0, ds(tile, 1)], min_val=1, max_val=E)
                    at = act.value_load(map_i[0:1, 1, ds(tile, 1)], min_val=0, max_val=2 * EXPERT)
                    cut_high(stage, at * -1 + 2 * EXPERT, pieces, ready * (16 * W_PIECES))

            def gated(tile, b):
                act.wait_ge(s["gate"], tile + 1)
                act.wait_ge(s["added"], tile + 1)
                act.wait_ge(s["y2_ps"], tile + 1)
                nc.scalar.activation(y_out[:, b, :], bank[5 + b][:, :], ACT.Copy, scale=gates[:, b, 2:3]).then_inc(s["y2"], 1)

            def hidden(tile, b):
                act.wait_ge(s["fields"], tile * 2 + 2)
                load_rows(tile + 2, b)
                for half in range(2):
                    act.wait_ge(s["h_ps"], tile * 2 + (half + 1))
                    nc.scalar.activation(h[:, half * 512:half * 512 + 512], bank[half][:, :], ACT.Silu,
                                         scale=1.0 / W_SCALE).then_inc(s["h"], 1)

            def hidden_copy(tile, b):
                act.wait_ge(s["hT_ps0"], tile + 1)
                nc.scalar.copy(hT[b][:, 0, :], bank[2][:, :].bitcast(F16)).then_inc(s["hT0"], 1)

            gate_exp(1)
            cut_high(expert0, 2 * EXPERT, (2, 3), 0)
            features_out(PAIRS - 1)
            gate_exp(2)
            act.wait_ge(s["rt_map"], 1)
            act.wait_ge(s["scattered"], 16 * 2 * TILES)
            load_rows(0, 0)
            load_rows(1, 1)
            hidden(0, 0)
            hidden_copy(0, 0)
            act.wait_ge(s["w2_lo"], 2)
            cut_high(stage, 0, (0, 1), 16 * W_PIECES)
            last = last_of(act)
            with act.Fori(0, (SLOT_TILES - 1) // 2) as i:
                with act.If(i * 2 < last):
                    for u in (1, 2):
                        hidden(i * 2 + u, u % 2)
                        cut_next_high(i * 2 + (u - 1), (2, 3))
                        cut_next_high(i * 2 + u, (0, 1))
                        hidden_copy(i * 2 + u, u % 2)
                        gated(i * 2 + (u - 1), (u - 1) % 2)
            gated(last, 0)

        @block.vector
        def _(dve):
            steps = {"norm_step": 0, "softmax_step": 0, "max_step": 0, "route": 0}

            def count(op, name, wait=True):
                op.then_inc(s[name], 1)
                steps[name] += 1
                if wait:
                    dve.wait_ge(s[name], steps[name])

            def norm_stats(srcs, stats_, mv_, ve_, ve_sem):
                for i, src in enumerate(srcs):
                    count(nc.vector.bn_stats(stats_[:, i, :], src), "norm_step", wait=(i == len(srcs) - 1))
                norm_mean(stats_, mv_, ve_, ve_sem, len(srcs))

            def norm_mean(stats_, mv_, ve_, ve_sem, n):
                for i in range(n):
                    count(nc.vector.bn_aggr(mv_[:, i, :], stats_[:, i, :]), "norm_step", wait=(i == n - 1))
                nc.vector.tensor_scalar(ve_, mv_[:, :, 1], EPS, None, ALU.add).then_inc(ve_sem, 1)

            def normalise(dst, src, mean, inverse):
                return nc.vector.tensor_scalar(dst, src, mean, inverse, ALU.subtract, ALU.mult)

            def x_at(tile):
                return x[:, tile * D:(tile + 1) * D]

            def norm_pair(srcs, dsts, name, pair):
                norm_stats(srcs, stats, mv, ve, s[f"{name}_ve"])
                dve.wait_ge(s[f"{name}_rstd"], pair + 1)
                out_sem = s[f"{name}_out"]
                for t in range(2):
                    normalise(dsts[t], srcs[t], mv[:, t, 0:1], rstd[:, t:t + 1]).then_inc(out_sem, 1)
                dve.wait_ge(out_sem, 2 * pair + 2)

            count(nc.vector.memset(neg_half, -0.5), "route", wait=False)
            dve.wait_ge(s["const_in"], 16)
            nc.vector.tensor_copy(ident16[:, :], ident).then_inc(s["ident16"], 1)
            dve.wait_ge(s["x_in0"], 16)
            dve.wait_ge(s["cols_in"], 16)

            def left_norm():
                dve.wait_ge(s["left_in"], 16)
                norm_stats([left_n[0:B, :]], l_stats[0:B, None, :], l_mv[0:B, None, :], l_ve[0:B, :],
                           s["left_ve"])
                dve.wait_ge(s["left_rstd"], 1)
                normalise(left_n[0:B, :], left_n[0:B, :], l_mv[0:B, 0:1], l_rstd[0:B, :]).then_inc(s["left_n"], 1)

            def ctx_stats(tile):
                u, part = tile % 2, ctx_n[:, tile % 4]
                if tile % 2 and tile > 1:
                    dve.wait_ge(s["cx_n1"], tile // 2)
                dve.wait_ge(ctx_in[tile % 4], 16 * (tile // 4 + 1))
                pieces = [part[:, b, c2, :] for b in range(BT) for c2 in range(2)]
                norm_stats(pieces, cx_stats[:, u], cx_mv[:, u], cx_ve[:, u], s["cx_ve"])

            def ctx_scale(tile):
                u, part = tile % 2, ctx_n[:, tile % 4]
                pieces = [part[:, b, c2, :] for b in range(BT) for c2 in range(2)]
                dve.wait_ge(s["cx_rstd"], tile + 1)
                if tile % 2:
                    nc.vector.scalar_tensor_tensor(cx_shift, cx_mv[:, u, :, 0], -1.0, cx_rstd[:, u, :], ALU.mult, ALU.mult)\
                        .then_inc(s["cx_shift"], 1)
                for i, piece in enumerate(pieces[0:4] if tile % 2 else pieces):
                    op = normalise(piece, piece, cx_mv[:, u, i, 0:1], cx_rstd[:, u, i:i + 1])
                op.then_inc(s["cx_n0"], 1)

            def query_norms(pair):
                if pair == 1:
                    dve.wait_ge(s["x_in"], 16)
                if pair:
                    dve.wait_ge(s["x1T_ps"], 2 * pair)
                tiles = [x_at(2 * pair), x_at(2 * pair + 1)]
                norm_stats(tiles, stats, mv, ve, s["ln1_ve"])
                dve.wait_ge(s["ln1_rstd"], pair + 1)
                count(nc.vector.tensor_tensor(ve2, mv[:, :, 1], rstd, ALU.mult), "norm_step")
                count(nc.vector.tensor_tensor(ve2, ve2, rstd, ALU.mult), "norm_step")
                nc.vector.tensor_scalar(ve2, ve2, EPS, None, ALU.add).then_inc(s["ln2_ve"], 1)
                dve.wait_ge(s["ln2_rstd"], pair + 1)
                count(nc.vector.tensor_tensor(rstd2, rstd2, rstd, ALU.mult), "norm_step")
                for t in range(2):
                    normalise(xn[:, t, :], tiles[t], mv[:, t, 0:1], rstd2[:, t:t + 1]).then_inc(s["ln2_out"], 1)
                dve.wait_ge(s["ln2_out"], 2 * pair + 2)

            def left_keys(pair):
                for t in range(2):
                    tile = 2 * pair + t
                    nc.vector.tensor_copy(ctxT[:, t, :, :, KEYS - 1], left_T[:, :, tile * BT:(tile + 1) * BT]).then_inc(s["left_cols"], 1)

            def context_max(pair):
                dve.wait_ge(s["q_bias"], pair + 1)
                for t in range(2):
                    tile = 2 * pair + t
                    one = slice(t, t + 1)
                    dve.wait_ge(s["sc_ps"], tile + 1)
                    count(nc.vector.tensor_reduce(sc_max[:, one], bank[2 + t][:, 0:KEYS], AX.X, ALU.max), "max_step")
                    count(nc.vector.tensor_tensor(sc_u[:, one], sc_max[:, one], q_bias[:, one], ALU.add), "max_step")
                    nc.vector.tensor_scalar(sc_nb[:, one], q_bias[:, one], sc_u[:, one], X_SCALE, ALU.subtract, ALU.mult)\
                        .then_inc(s["sc_nb"], 1)

            def context_left_probs(pair):
                for t in range(2):
                    tile = 2 * pair + t
                    dve.wait_ge(s["sc_exp"], tile + 1)
                    at = CONST["left_mask"].start + 28 - BT * tile
                    nc.vector.tensor_scalar(p_mask[:, t, :], consts[:, at:at + B], probs[:, t, KEYS - 1:KEYS], None, ALU.mult)\
                        .then_inc(s["sc_pm"], 1)
                    nc.vector.reciprocal(sc_rinv[:, t:t + 1], sc_sum[:, t:t + 1]).then_inc(s["sc_rinv"], 1)

            def context_residual(pair):
                for t in range(2):
                    tile = 2 * pair + t
                    dve.wait_ge(s["y_ps"], tile + 1)
                    dve.wait_ge(s["x_plus_bo"], tile + 1)
                    nc.vector.scalar_tensor_tensor(x_at(tile), bank[6 + t][:, :], 1.0 / W_SCALE, x_at(tile), ALU.mult, ALU.add)\
                        .then_inc(s["x_new"], 1)

            def sums_low(pair):
                dve.wait_ge(s["cvT_ps"], 2 * pair + 2)
                for k in range(CC):
                    op = nc.vector.tensor_scalar(x2aT[:, k, P:2 * P], bank[5][:, k * P:(k + 1) * P],
                                                 col("ln2_g", k), col("ln2_b", k), ALU.mult, ALU.add)
                op.then_inc(s["x2aT1"], 1)
                for t in range(2):
                    dve.wait_ge(s["x2a_hi"], 2 * pair + t + 1)
                    tile_at = slice(t * P, (t + 1) * P)
                    nc.vector.tensor_tensor(x2a[:, 1, :, tile_at], x2aT[:, :, tile_at], x2a[:, 0, :, tile_at], ALU.subtract)\
                        .then_inc(s["x2a_lo"], 1)

            def first_norm(pair):
                if pair == 0:
                    dve.wait_ge(s["x1T_ps"], TILES)
                dve.wait_ge(s["x_new"], 2 * pair + 2)
                norm_pair([x_at(2 * pair), x_at(2 * pair + 1)], [xn[:, 0, :], xn[:, 1, :]], "ln3", pair)

            def normalised_low(pair):
                for t in range(2):
                    dve.wait_ge(s["xnT"], 2 * pair + t + 1)
                    tile_at = slice(t * P, (t + 1) * P)
                    nc.vector.tensor_tensor(xnT[:, 1, :, tile_at], bank[t][:, :].rearrange("p (k t) -> p k t", k=KC),
                                            xnT[:, 0, :, tile_at], ALU.subtract).then_inc(s["xnT_lo"], 1)

            def cut_self_low(n):
                dve.wait_ge(s["sw_hi"], n + 1)
                w, (high, low_part) = self_weights[n]
                nc.vector.scalar_tensor_tensor(low_part, w, W_SCALE, high, ALU.mult, ALU.subtract).then_inc(s["sw_lo"], 1)

            nc.vector.tensor_scalar(ln2_g_scaled, cols[:, COLS["ln2_g"]], 1.0 / W_SCALE, None, ALU.mult).then_inc(s["scale2"], 1)
            query_norms(0)
            left_norm()
            ctx_stats(0)
            ctx_scale(0)
            dve.wait_ge(s["left_ps"], 1)
            nc.vector.tensor_copy(left_T, bank[0][:, 0:CC * B].rearrange("p (c b) -> p c b", c=CC)).then_inc(s["left_T"], 1)
            dve.wait_ge(s["kb_ps"], 1)
            nc.vector.tensor_tensor(kb, bank[6][:, 0:KC], cols[:, COLS["bk"]], ALU.add).then_inc(s["kb"], 1)
            nc.vector.tensor_tensor(qk_bias, bank[6][:, 8:8 + CC], cols[:, COLS["ln2_g"]], ALU.mult).then_inc(s["bqk"], 1)
            dve.wait_ge(s["left_T"], 1)
            left_keys(0)
            for d in range(KC):
                dve.wait_ge(s["m1_hi"], d + 1)
                nc.vector.scalar_tensor_tensor(m1[:, 1, d, :], bank[2 + d][:, 0:DC], W_SCALE, m1[:, 0, d, :], ALU.mult, ALU.subtract)\
                    .then_inc(s["m1_lo"], 1)
            ctx_stats(1)
            ctx_scale(1)
            dve.wait_ge(s["left_bias_ps"], 1)
            nc.vector.tensor_copy(bias_of, bank[6][:, 16:17 + KC]).then_inc(s["left_bias"], 1)
            dve.wait_ge(s["left_bias"], 1)
            nc.vector.tensor_copy(bias16[:, 0, :], bias_of[:, 0:KC]).then_inc(s["left_bias"], 1)
            dve.wait_ge(s["left_bias"], 2)
            nc.vector.tensor_tensor(bias16[:, 1, :], bias_of[:, 0:KC], bias16[:, 0, :], ALU.subtract).then_inc(s["left_bias"], 1)
            query_norms(1)
            ctx_stats(2)
            for pair in range(PAIRS):
                context_max(pair)
                context_left_probs(pair)
                if pair == 0:
                    for k in range(CC):
                        dve.wait_ge(s["m2_hi"], k + 1)
                        nc.vector.scalar_tensor_tensor(m2[:, 1, k, :], bank[(6, 7, 0)[k]][:, :], W_SCALE, m2[:, 0, k, :],
                                                       ALU.mult, ALU.subtract).then_inc(s["m2_lo"], 1)
                    dve.wait_ge(s["rows_in"], 16)
                    dve.wait_ge(s["bvo_ps"], 1)
                    nc.vector.tensor_tensor(row("bo"), bank[1][:, :], row("bo"), ALU.add).then_inc(s["bvo"], 1)
                if pair + 1 < PAIRS:
                    ctx_scale(2 * pair + 2)
                    ctx_stats(2 * pair + 3)
                if pair:
                    context_residual(pair - 1)
                if pair + 1 < PAIRS:
                    ctx_scale(2 * pair + 3)
                    left_keys(pair + 1)
                if pair + 2 < PAIRS:
                    query_norms(pair + 2)
                    ctx_stats(2 * pair + 4)
                if pair + 1 == PAIRS:
                    first_norm(0)
                    cut_self_low(0)
                    normalised_low(0)
                sums_low(pair)
            cut_self_low(1)
            dve.wait_ge(s["sw_lo"], 1)
            cut_self_low(2)
            context_residual(PAIRS - 1)

            swap = [(i + HD // 2) % HD for i in range(HD)]

            def by_place(a):
                return a.rearrange("p (n l) -> p n l", l=L)

            table = [P, KC * 2 * BT, L]
            sin_t = const("sin")[:, None, :].to_broadcast(table)

            def rotate(pair):
                dve.wait_ge(s["sq"], 2 * pair + 2)
                nc.vector.stream_shuffle(q_sw, qb, swap).then_inc(s["swapped"], 1)
                dve.wait_ge(s["sk"], 2 * pair + 2)
                nc.vector.stream_shuffle(k_sw, kbuf, swap).then_inc(s["swapped"], 1)
                for n, sw in enumerate((q_sw, k_sw)):
                    dve.wait_ge(s["swapped"], 2 * pair + n + 1)
                    nc.vector.tensor_tensor(by_place(sw), by_place(sw), sin_t, ALU.mult).then_inc(s["sined"], 1)

            def rotated(pair):
                dve.wait_ge(s["sined"], 2 * pair + 2)
                dve.wait_ge(s["cosined"], 2 * pair + 1)
                nc.vector.tensor_tensor(qb, qb, q_sw, ALU.add).then_inc(s["rotated"], 1)
                dve.wait_ge(s["cosined"], 2 * pair + 2)
                nc.vector.tensor_tensor(kbuf, kbuf, k_sw, ALU.add).then_inc(s["rotated"], 1)

            by_head = [P, HEADS, L]

            def softmax(pair):
                for t in range(2):
                    tile = 2 * pair + t
                    dve.wait_ge(s["ss_ps"], tile + 1)
                    scores = bank[t][:, :].rearrange("p (h l) -> p h l", l=L)
                    count(nc.vector.tensor_reduce(s_max[:, t, :], scores, AX.X, ALU.max), "softmax_step")
                    nc.vector.tensor_tensor(by_place(soft[:, t, :]), scores, s_max[:, t, :, None].to_broadcast(by_head),
                                            ALU.subtract).then_inc(s["s_sub"], 1)
                for t in range(2):
                    tile = 2 * pair + t
                    dve.wait_ge(s["s_exp"], tile + 1)
                    count(nc.vector.tensor_reduce(s_sum[:, t, :], by_place(soft[:, t, :]), AX.X, ALU.add), "softmax_step")
                    count(nc.vector.reciprocal(s_rinv[:, t, :], s_sum[:, t, :]), "softmax_step")
                    count(nc.vector.tensor_tensor(by_place(soft[:, t, :]), by_place(soft[:, t, :]),
                                                  s_rinv[:, t, :, None].to_broadcast(by_head), ALU.mult), "softmax_step")
                    for b in range(BT):
                        part = slice(b * L, (b + 1) * L)
                        op = nc.vector.transpose(p_T[part, t, :, b * L:(b + 1) * L], by_place(soft[part, t, :]))
                    op.then_inc(s["s_pT"], 1)

            def last_norm(pair):
                for t in range(2):
                    tile = 2 * pair + t
                    dve.wait_ge(s["sy_ps"], tile + 1)
                    dve.wait_ge(s["x_plus_sbo"], tile + 1)
                    nc.vector.tensor_tensor(x_at(tile), bank[4 + t][:, :], x_at(tile), ALU.add).then_inc(s["x_post"], 1)
                    dve.wait_ge(s["x_post"], tile + 1)
                    count(nc.vector.bn_stats(stats[:, t, :], x_at(tile)), "norm_step", wait=(t == 1))
                norm_mean(stats, mv, ve, s["ln4_ve"], 2)
                dve.wait_ge(s["ln4_rstd"], pair + 1)
                if pair:
                    dve.wait_ge(s["xf_lo"], 2 * pair)
                for t in range(2):
                    normalise(ln4_n[:, t, :], x_at(2 * pair + t), mv[:, t, 0:1], rstd[:, t:t + 1]).then_inc(s["xf"], 1)

            def logits_out(pair):
                for t in range(2):
                    tile = 2 * pair + t
                    dve.wait_ge(s["z_ps"], tile + 1)
                    nc.vector.tensor_tensor(z[:, tile, :], bank[2 + t][:, 0:E], row("balance"), ALU.add).then_inc(s["z"], 1)

            tt, ts = nc.vector.tensor_tensor, nc.vector.tensor_scalar

            def then(op):
                count(op, "route")

            def choose(n):
                lo, hi = ROUTED[n]
                tiles, some = hi - lo, slice(lo, hi)
                dve.wait_ge(s["z"], hi)
                full = [P, tiles, E, E]
                more, same = cmp_a[:, 0:tiles], cmp_b[:, 0:tiles]
                then(tt(more, z[:, some, None, :].to_broadcast(full), z[:, some, :, None].to_broadcast(full), ALU.is_gt))
                then(tt(same, z[:, some, None, :].to_broadcast(full), z[:, some, :, None].to_broadcast(full), ALU.is_equal))
                then(tt(same.rearrange("p t a b -> p t (a b)"), same.rearrange("p t a b -> p t (a b)"),
                        low[:, None, :].to_broadcast([P, tiles, E * E]), ALU.mult))
                then(tt(more, more, same, ALU.add))
                then(nc.vector.tensor_reduce(rank[:, some], more, AX.X, ALU.add))
                ts(sel[:, some], rank[:, some], 2.0, None, ALU.is_lt).then_inc(s["rt_sel"], 1)
                for place in range(2):
                    then(ts(chosen[:, place, some], rank[:, some], float(place), None, ALU.is_equal))
                by_choice = [P, 2, tiles, E]
                then(tt(picked[:, :, some], chosen[:, :, some],
                        const("tile_no")[:, None, None, 0:E].to_broadcast(by_choice), ALU.mult))
                then(nc.vector.tensor_reduce(fields_at(some, C_E1), picked[:, :, some], AX.X, ALU.add))
                dve.wait_ge(s["rt_exp"], n + 1)
                then(ts(sig[:, some], sig[:, some], 1.0, None, ALU.add))
                then(nc.vector.reciprocal(sig[:, some], sig[:, some]))
                then(tt(picked[:, :, some], chosen[:, :, some], sig[:, None, some, :].to_broadcast(by_choice), ALU.mult))
                then(nc.vector.tensor_reduce(gate_of_token[:, :, some], picked[:, :, some], AX.X, ALU.add))
                then(tt(gate_sum[:, some], gate_of_token[:, 0, some], gate_of_token[:, 1, some], ALU.add))
                then(ts(gate_sum[:, some], gate_sum[:, some], 1e-6, W_SCALE, ALU.add, ALU.mult))
                then(nc.vector.reciprocal(gate_sum[:, some], gate_sum[:, some]))
                then(tt(fields_at(some, C_G1), gate_of_token[:, :, some], gate_sum[:, None, some].to_broadcast([P, 2, tiles]), ALU.mult))

            def fields_at(some, first):
                return xf[:, some, first:first + 3:2].rearrange("p t n -> p n t")

            def place(n):
                lo, hi = ROUTED[n]
                within, whole = COUNT_BANKS[n]
                some = slice(lo, hi)
                dve.wait_ge(s["rt_cnt_ps"], 2 * n + 2)
                for tile in range(lo, hi):
                    then(tt(base[:, tile + 1, :], bank[whole][:, tile * E:(tile + 1) * E], base[:, tile, :], ALU.add))
                then(tt(slot[:, some], bank[within][:, lo * E:hi * E].rearrange("p (t e) -> p t e", e=E), base[:, some, :], ALU.add))
                then(tt(picked[:, :, some], chosen[:, :, some], slot[:, None, some, :].to_broadcast([P, 2, hi - lo, E]), ALU.mult))
                then(nc.vector.tensor_reduce(slot_f[:, :, some], picked[:, :, some], AX.X, ALU.add))
                nc.vector.tensor_copy(slot_i[:, :, some], slot_f[:, :, some]).then_inc(s["rt_slots"], 1)

            def cut_low(src_, at, pieces, before):
                for n in pieces:
                    dve.wait_ge(s["w_hi"], before + (n + 1))
                    piece = slice(n * PIECE, (n + 1) * PIECE)
                    nc.vector.scalar_tensor_tensor(w16[:, ds(at + (LOW + n * PIECE), PIECE)], src_[:, piece], W_SCALE,
                                                   w16[:, ds(at + (HIGH + n * PIECE), PIECE)], ALU.mult, ALU.subtract)\
                        .then_inc((s["w1_lo"], s["w2_lo"])[n // 2], 1)

            low = const("low")
            then(ts(base[:, 0, :], const("tile_no")[:, 0:E], float(TOK), None, ALU.mult))

            dve.wait_ge(s["xnT_ps"], 2)
            first_norm(1)
            dve.wait_ge(s["ptx_zero"], 2)
            rotate(0)
            rotated(0)
            normalised_low(1)
            for pair in range(PAIRS):
                softmax(pair)
                if pair:
                    logits_out(pair - 1)
                if pair + 2 < PAIRS:
                    first_norm(pair + 2)
                if pair + 1 < PAIRS:
                    rotate(pair + 1)
                if pair + 2 < PAIRS:
                    normalised_low(pair + 2)
                if pair + 1 < PAIRS:
                    rotated(pair + 1)
                else:
                    choose(0)
                    place(0)
                    choose(1)
                last_norm(pair)
            place(1)
            dve.wait_ge(s["sv_ps"], TILES)
            cut_low(expert0, 2 * EXPERT, (0,), 0)
            logits_out(PAIRS - 1)
            choose(2)
            place(2)
            then(tt(total, base[:, TILES, :], base[:, 0, :], ALU.subtract))
            then(tt(over, total[:, :, None].to_broadcast([P, E, 8]), const("steps")[:, None, :].to_broadcast([P, E, 8]), ALU.is_gt))
            then(nc.vector.tensor_reduce(ntile, over, AX.X, ALU.add))
            then(ts(ntile, ntile, 1.0, None, ALU.add))
            then(tt(ends_tmp, ntile[:, None, :].to_broadcast([P, E, E]), low.rearrange("p (a b) -> p a b", a=E), ALU.mult))
            then(nc.vector.tensor_reduce(ends, ends_tmp, AX.X, ALU.add))
            then(tt(ends, ends, ntile, ALU.add))
            by_tile = [P, 32, E]
            then(tt(emap_cmp, ends[:, None, :].to_broadcast(by_tile), const("tile_no")[:, :, None].to_broadcast(by_tile), ALU.is_le))
            then(nc.vector.tensor_reduce(emap, emap_cmp, AX.X, ALU.add))
            then(ts(emap, emap, float(E - 1), None, ALU.min))
            then(ts(skipped, ntile, -float(P), float(TOK), ALU.mult, ALU.add))
            then(tt(emap_cmp, emap_cmp, skipped[:, None, :].to_broadcast(by_tile), ALU.mult))
            then(nc.vector.tensor_reduce(row_at, emap_cmp, AX.X, ALU.add))
            then(nc.vector.scalar_tensor_tensor(row_at, const("tile_no"), float(P), row_at, ALU.mult, ALU.add))
            then(ts(map_i[:, 4, :], row_at, float(E * TOK), None, ALU.min))
            then(nc.vector.tensor_copy(used, ends[:, E - 1:E]))
            then(ts(last_tile, used, 1, 1, ALU.logical_shift_right, ALU.logical_shift_left))
            then(ts(map_i[:, 0, :], emap, 1.0, None, ALU.add))
            then(ts(map_i[:, 1, :], map_i[:, 0, :], 1, int(np.log2(2 * EXPERT)), ALU.bitwise_and, ALU.logical_shift_left))
            then(ts(packed, emap, 1.0, None, ALU.add))
            for ahead, weight in ((1, 16.0), (2, 256.0)):
                n = 32 - ahead
                then(ts(not_last, emap, 1.0, weight, ALU.add, ALU.mult))
                then(tt(packed[:, 0:n], packed[:, 0:n], not_last[:, ahead:32], ALU.add))
            then(nc.vector.tensor_copy(map_i[:, 3, :], packed))
            then(tt(first_of[:, 1:32], emap[:, 1:32], emap[:, 0:31], ALU.is_gt))
            then(nc.vector.memset(first_of[:, 0:1], 1.0))
            then(ts(not_last, emap, E - 1.5, None, ALU.is_lt))
            tt(map_i[:, 2, :], first_of, not_last, ALU.mult).then_inc(s["rt_map"], 1)

            def cut_next_low(tile, pieces):
                new = dve.value_load(map_i[0:1, 2, ds(tile, 1)], min_val=0, max_val=1)
                with dve.If(new == 1):
                    ready = dve.value_load(map_i[0:1, 0, ds(tile, 1)], min_val=1, max_val=E)
                    at = dve.value_load(map_i[0:1, 1, ds(tile, 1)], min_val=0, max_val=2 * EXPERT)
                    cut_low(stage, at * -1 + 2 * EXPERT, pieces, ready * W_PIECES)

            def rows_copy(tile, b, again=True):
                if again:
                    dve.wait_ge(s["idx"], tile - 1)
                dve.wait_ge(s["xgT_ps"], tile + 1)
                nc.vector.tensor_copy(tokens[:, b:b + 1], xg[:, b, C_TOKEN:C_TOKEN + 1].bitcast(I32)).then_inc(s["fields"], 1)
                nc.vector.tensor_copy(fields[:, b, :], xg[:, b, C_G1:C_E2 + 1]).then_inc(s["fields"], 1)
                nc.vector.tensor_copy(xgT[:, b].rearrange("p a d -> p (a d)"), bank[(4, 7)[b]][:, :].bitcast(F16)).then_inc(s["xgT"], 1)

            def cut_hidden(tile):
                dve.wait_ge(s["h"], tile * 2 + 2)
                nc.vector.tensor_copy(h16[:, 0, :], h).then_inc(s["h_hi"], 1)
                dve.wait_ge(s["h_hi"], tile + 1)
                tt(h16[:, 1, :], h, h16[:, 0, :], ALU.subtract).then_inc(s["h_lo"], 1)

            def hidden_copy(tile, b):
                dve.wait_ge(s["hT_ps1"], tile + 1)
                nc.vector.tensor_copy(hT[b][:, 1, :], bank[3][:, :].bitcast(F16)).then_inc(s["hT1"], 1)

            def gate_of(tile, b):
                expert = emap[:, ds(tile, 1)]
                field = {at: fields[:, b, at - C_G1:at - C_G1 + 1] for at in (C_G1, C_E1, C_G2, C_E2)}
                dve.wait_ge(s["fields"], tile * 2 + 2)
                for n, (g_col, e_col) in enumerate(((C_G1, C_E1), (C_G2, C_E2))):
                    op = ts(gates[:, b, n:n + 1], field[e_col], expert, field[g_col], ALU.is_equal, ALU.mult)
                op.then_inc(s["gate_parts"], 1)
                dve.wait_ge(s["gate_parts"], tile + 1)
                tt(gates[:, b, 2:3], gates[:, b, 0:1], gates[:, b, 1:2], ALU.add).then_inc(s["gate"], 1)
                dve.wait_ge(s["added"], tile + 1)
                nc.vector.tensor_copy(idx[:, b:b + 1], tokens[:, b:b + 1]).then_inc(s["idx"], 1)

            cut_low(expert0, 2 * EXPERT, (1,), 0)
            rows_copy(0, 0, again=False)
            cut_low(expert0, 2 * EXPERT, (2, 3), 0)
            rows_copy(1, 1, again=False)
            cut_hidden(0)
            hidden_copy(0, 0)
            cut_low(stage, 0, (0, 1), W_PIECES)
            gate_of(0, 0)
            last = last_of(dve)
            with dve.Fori(0, (SLOT_TILES - 1) // 2) as i:
                with dve.If(i * 2 < last):
                    for u in (1, 2):
                        rows_copy(i * 2 + (u + 1), (u + 1) % 2)
                        cut_hidden(i * 2 + u)
                        cut_next_low(i * 2 + (u - 1), (2, 3))
                        cut_next_low(i * 2 + u, (0, 1))
                        hidden_copy(i * 2 + u, u % 2)
                        gate_of(i * 2 + u, u % 2)

        @block.gpsimd
        def _(pool):
            def inverse_root(name, count, out_, in_, n, parts=P):
                pool.wait_ge(s[f"{name}_ve"], count)
                nc.gpsimd.tensor_tensor(out_, in_, neg_half[0:parts, 0:n], ALU.pow).then_inc(s[f"{name}_rstd"], 1)

            def x_at(tile):
                return x[:, tile * D:(tile + 1) * D]

            def ctx_root(tile):
                inverse_root("cx", tile + 1, cx_rstd[:, tile % 2], cx_ve[:, tile % 2], 8)

            pool.wait_ge(s["route"], 1)
            def query_roots(pair):
                inverse_root("ln1", pair + 1, rstd, ve, 2)
                inverse_root("ln2", pair + 1, rstd2, ve2, 2)

            def plus_bo(pair):
                for tile in (2 * pair, 2 * pair + 1):
                    pool.wait_ge(s["ln2_out"], tile + 1)
                    nc.gpsimd.tensor_tensor(x_at(tile), x_at(tile), row("bo"), ALU.add).then_inc(s["x_plus_bo"], 1)

            def queries_low(pair):
                pool.wait_ge(s["x1_hi"], pair + 1)
                nc.gpsimd.tensor_tensor(x1[:, 1], x1T, x1[:, 0], ALU.subtract).then_inc(s["x1_lo"], 1)

            query_roots(0)
            inverse_root("left", 1, l_rstd[0:B, :], l_ve[0:B, :], 1, B)
            ctx_root(0)
            queries_low(0)
            ctx_root(1)
            query_roots(1)
            ctx_root(2)
            for pair in range(PAIRS):
                if pair + 1 < PAIRS:
                    ctx_root(2 * pair + 3)
                    queries_low(pair + 1)
                if pair + 2 < PAIRS:
                    query_roots(pair + 2)
                    ctx_root(2 * pair + 4)
                if pair == 0:
                    pool.wait_ge(s["bvo"], 1)
                    plus_bo(0)
                if pair + 1 < PAIRS:
                    plus_bo(pair + 1)
            inverse_root("ln3", 1, rstd, ve, 2)
            pool.wait_ge(s["cv_ps"], TILES)
            nc.gpsimd.memset(k_exp, 0.0).then_inc(s["ptx_zero"], 1)
            nc.gpsimd.memset(p_T, 0.0).then_inc(s["ptx_zero"], 1)
            table = [P, KC * 2 * BT, L]
            cos_t = const("cos")[:, None, :].to_broadcast(table)

            def cosines(pair):
                for n, buf in enumerate((qb, kbuf)):
                    pool.wait_ge(s["swapped"], 2 * pair + n + 1)
                    by_place = buf.rearrange("p (n l) -> p n l", l=L)
                    nc.gpsimd.tensor_tensor(by_place, by_place, cos_t, ALU.mult).then_inc(s["cosined"], 1)

            def plus_sbo(pair):
                for t in range(2):
                    tile = 2 * pair + t
                    pool.wait_ge(s["ln3_out"], tile + 1)
                    nc.gpsimd.tensor_tensor(x_at(tile), x_at(tile), row("sbo"), ALU.add).then_inc(s["x_plus_sbo"], 1)

            def features_low(pair):
                for t in range(2):
                    tile = 2 * pair + t
                    pool.wait_ge(s["xf_hi"], tile + 1)
                    nc.gpsimd.tensor_tensor(xf16[:, tile, D:2 * D], ln4_n[:, t, :], xf16[:, tile, 0:D], ALU.subtract)\
                        .then_inc(s["xf_lo"], 1)

            inverse_root("ln3", 2, rstd, ve, 2)
            cosines(0)
            plus_sbo(0)
            plus_sbo(1)
            pool.wait_ge(s["y_ps"], TILES)
            pool.wait_ge(s["ints_in"], 16)
            nc.gpsimd.memset(zrow, 0.0).then_inc(s["zrow_fill"], 1)
            pool.wait_ge(s["zrow_fill"], 1)
            nc.gpsimd.tensor_copy(zrow[:, C_TOKEN:C_TOKEN + 1].bitcast(I32), token_no[:, TILES:TILES + 1]).then_inc(s["zrow"], 1)
            nc.gpsimd.memset(xf[:, :, C_E2 + 1:ROW], 0.0).then_inc(s["rows_set"], 1)
            nc.gpsimd.tensor_copy(xf[:, :, C_TOKEN].bitcast(I32), token_no[:, 0:TILES]).then_inc(s["rows_set"], 1)
            def scatter(n, lo, hi):
                pool.wait_ge(s["xf_lo"], hi)
                pool.wait_ge(s["rt_slots"], n + 1)
                for tile in range(lo, hi):
                    for choice in range(2):
                        nc.gpsimd.indirect_dma_start(
                            xs_dram, bass.IndirectOffsetOnAxis(slot_i[:, choice, tile:tile + 1].bitcast(U32), axis=0), xf[:, tile, :], None,
                        ).then_inc(s["scattered"], 16)

            for pair in range(PAIRS):
                if pair:
                    features_low(pair - 1)
                if pair + 1 == PAIRS:
                    pool.wait_ge(s["xs_zero"], 16)
                    pool.wait_ge(s["rows_set"], 2)
                    scatter(0, 0, 2)
                if pair + 2 < PAIRS:
                    inverse_root("ln3", pair + 3, rstd, ve, 2)
                if pair + 1 < PAIRS:
                    cosines(pair + 1)
                inverse_root("ln4", pair + 1, rstd, ve, 2)
                if pair + 2 < PAIRS:
                    plus_sbo(pair + 2)

            scatter(0, 2, ROUTED[0][1])
            scatter(1, *ROUTED[1])
            features_low(PAIRS - 1)
            scatter(2, *ROUTED[2])

            def add_rows(tile, slot_no, first=False):
                pool.wait_ge(s["y2"], tile + 1)
                pool.wait_ge(s["idx"], tile + 1)
                if not first:
                    pool.wait_ge(s["scat"], tile * 16)
                pool.sem_inc(s["added"], 1)
                nc.gpsimd.indirect_dma_start(
                    out, bass.IndirectOffsetOnAxis(idx[:, slot_no:slot_no + 1].bitcast(U32), axis=0), y_out[:, slot_no, :], None,
                    compute_op=ALU.add).then_inc(s["scat"], 16)

            pool.wait_ge(s["out_init"], 16 * TILES)
            pool.wait_ge(s["out_spare"], 16)
            pool.sem_inc(s["added"], 1)
            pool.wait_ge(s["rt_map"], 1)
            last = last_of(pool)
            add_rows(0, 0, first=True)
            with pool.Fori(0, (SLOT_TILES - 1) // 2) as i:
                with pool.If(i * 2 < last):
                    for u in (1, 2):
                        add_rows(i * 2 + u, u % 2)
            pool.wait_ge(s["scat"], last * 16 + 16)
            pool.wait_ge(xg_in[0], last * 8 + 32)
            pool.wait_ge(xg_in[1], last * 8 + 16)
            pool.sem_inc(s["finished"], 1)


def constants():
    c = np.zeros((P, CONST_W), np.float32)
    p = np.arange(P)
    c[:, CONST["ident"]] = np.eye(P)
    c[:, CONST["before"]] = p[:, None] < p[None, :]
    c[:, CONST["ones"]] = 1.0
    half = HD // 2
    theta = np.float32(10000.0) ** (-np.arange(half, dtype=np.float32) / half)
    angle = theta[p % half][:, None] * np.arange(L, dtype=np.float32)[None, :]
    c[:, CONST["cos"]] = np.cos(angle)
    c[:, CONST["sin"]] = np.sin(angle) * np.where(p % HD < half, -1.0, 1.0)[:, None]
    c[:, CONST["left_mask"]] = np.arange(60)[None, :] - (B - BT) == p[:, None] // L
    e = np.arange(E)
    c[:, CONST["low"]] = (e[None, :] < e[:, None]).reshape(1, -1)
    c[:, CONST["tile_no"]] = np.arange(32)
    c[:, CONST["steps"]] = P * np.arange(1, 9)
    token_no = (p[:, None] + P * np.arange(TILES + 1)[None, :]).astype(np.int32)
    return c, token_no


def kernel(x, ctx_768, L0_xattn_ln1_g, L0_xattn_ln1_b, L0_xattn_ln2_g, L0_xattn_ln2_b, L0_xattn_Wq, L0_xattn_bq,
           L0_xattn_Wk, L0_xattn_bk, L0_xattn_Wv, L0_xattn_bv, L0_xattn_Wo, L0_xattn_bo, L0_attn_Wq, L0_attn_bq,
           L0_attn_Wk, L0_attn_bk, L0_attn_Wv, L0_attn_bv, L0_attn_Wo, L0_attn_bo, L0_ffn_gate_w,
           L0_ffn_balance_bias, L0_ffn_w1, L0_ffn_w2):
    import concourse.bacc as bacc
    from concourse.bass_utils import run_bass_kernel_spmd

    def blocks(a):
        return np.asarray(a).reshape(-1, P).T

    cols = np.concatenate([blocks(a) for a in (L0_xattn_ln1_g, L0_xattn_ln1_b, L0_xattn_bq, L0_xattn_ln2_g, L0_xattn_ln2_b,
                                               L0_xattn_bk, L0_xattn_bv, L0_attn_bq, L0_attn_bk, L0_attn_bv)], 1)
    rows = np.concatenate([np.asarray(a) for a in (L0_xattn_bo, L0_attn_bo, L0_ffn_balance_bias)])
    w1T = np.asarray(L0_ffn_w1).transpose(0, 2, 1).reshape(E, KC, P, EH).transpose(0, 2, 1, 3).reshape(E, P, KC * EH)
    w2T = np.asarray(L0_ffn_w2).transpose(0, 2, 1).reshape(E, HC, P, D).transpose(0, 2, 1, 3).reshape(E, P, HC * D)
    consts, token_no = constants()
    arrays = {
        "x": np.asarray(x).reshape(TOK, D), "ctx_768": ctx_768, "cols": cols, "rows": np.broadcast_to(rows, (P, ROWS_W)),
        "consts": consts, "token_no": token_no,
        "wqT": np.asarray(L0_xattn_Wq).T, "wk": L0_xattn_Wk, "wkT": np.asarray(L0_xattn_Wk).T,
        "wvT": np.asarray(L0_xattn_Wv).T, "wo": L0_xattn_Wo,
        "swqT": np.asarray(L0_attn_Wq).T, "swkT": np.asarray(L0_attn_Wk).T, "swvT": np.asarray(L0_attn_Wv).T,
        "swoT": np.asarray(L0_attn_Wo).T, "gate_wT": np.asarray(L0_ffn_gate_w).T,
        "experts": np.concatenate([w1T, w2T], 2),
    }
    arrays = {name: np.ascontiguousarray(a) for name, a in arrays.items()}
    nc = bacc.Bacc("TRN2", target_bir_lowering=False, num_devices=1)
    t_in = {name: nc.dram_tensor(f"in_{name}", a.shape, mybir.dt.from_np(a.dtype), kind="ExternalInput").ap()
            for name, a in arrays.items()}
    out = nc.dram_tensor("out", (TOK + P, D), F32, kind="ExternalOutput").ap()
    program(nc, t_in, out)
    result = run_bass_kernel_spmd(nc, [{f"in_{name}": a for name, a in arrays.items()}], core_ids=[0])
    return result.results[0]["out"][0:TOK].reshape(B, L, D)
```
